# Optimizing a Trainium2 kernel written in Bass

```python
import numpy as np
import jax
import jax.numpy as jnp

def _softmax(x, axis=-1):
    return jax.nn.softmax(x, axis=axis)

def _gelu(x):
    return jax.nn.gelu(x, approximate=True)

def _silu(x):
    return jax.nn.silu(x)

def _sigmoid(x):
    return jax.nn.sigmoid(x)

def _layernorm(x, axis=-1, eps=1e-05):
    m = jnp.mean(x, axis=axis, keepdims=True)
    v = jnp.var(x, axis=axis, keepdims=True)
    return (x - m) / jnp.sqrt(v + eps)

def _scatter_add(tgt, idx, src, axis=0):
    return tgt.at[idx].add(src)

def _segment_sum(src, seg, n):
    return jax.ops.segment_sum(src, seg, n)
kernel_name = 'mk_gnn_resnorm_d4_gnn_r32_227a7b'

def setup_inputs(seed: int=0):
    np.random.seed(seed)
    _w = jnp.asarray

    def _rec_inputs():
        import jax
        import jax.numpy as jnp
        _gk = jax.random.key(seed)
        x = -0.000202 + 1 * jax.random.normal(jax.random.fold_in(_gk, 1), (3125, 64), jnp.float32)
        _s = jax.random.randint(jax.random.fold_in(_gk, 2), (50000,), 0, 3125, jnp.int32)
        _d = jax.random.randint(jax.random.fold_in(_gk, 3), (50000,), 0, 3125, jnp.int32)
        _loop = jnp.arange(3125, dtype=jnp.int32)
        src = jnp.concatenate([_s, _d, _loop])
        dst = jnp.concatenate([_d, _s, _loop])
        _o = jnp.argsort(dst, stable=True)
        src = src[_o]
        dst = dst[_o]
        edge_attr_64 = -6.74381e-05 + 0.999835 * jax.random.normal(jax.random.fold_in(_gk, 11), (103125, 64), jnp.float32)
        edge_type_4 = jax.random.randint(jax.random.fold_in(_gk, 13), (103125,), 0, 4, jnp.int32)
        edge_weight = jax.random.uniform(jax.random.fold_in(_gk, 14), (103125,), jnp.float32, 0.0, 0.999999)
        return (x, src, dst, edge_attr_64, edge_type_4, edge_weight)
    x, src, dst, edge_attr_64, edge_type_4, edge_weight = _rec_inputs()

    def _L0_gnn_setup():
        import jax, jax.numpy as jnp
        import numpy as np
        N = 3125
        E = 50000
        C = 64
        H = 8
        D = C // H
        R = 4
        L = 2

        def _layer(x, src, dst, edge_type, WQ, WK, WV, Wcat, sw, sb, Ws, g, b):
            inv_sqrt_d = 1.0 / np.sqrt(D)
            rel_msgs = []
            for r in range(R):
                mask = (edge_type == r).astype(x.dtype)
                Q = jnp.einsum('nc,hcd->nhd', x, WQ[r])
                K = jnp.einsum('nc,hcd->nhd', x, WK[r])
                V = jnp.einsum('nc,hcd->nhd', x, WV[r])
                energy = jnp.einsum('ehd,ehd->eh', Q[dst], K[src]) * inv_sqrt_d
                energy = jax.nn.leaky_relu(energy)
                alpha_n = jax.ops.segment_sum(energy * mask[:, None], dst, num_segments=N)
                alpha = jax.nn.softmax(alpha_n, axis=0)
                w = alpha[dst] * mask[:, None]
                m = jax.ops.segment_sum(w[:, :, None] * V[src], dst, num_segments=N)
                rel_msgs.append(m.reshape(N, H * D) @ Wcat[r])
            stacked = jnp.stack(rel_msgs)
            beta = jax.nn.softmax(stacked @ sw + sb, axis=0)
            agg = jnp.einsum('rn,rnc->nc', beta, stacked)
            y = x + jax.nn.gelu(x @ Ws + agg, approximate=False)
            mu = y.mean(-1, keepdims=True)
            var = y.var(-1, keepdims=True)
            return (y - mu) / jnp.sqrt(var + 1e-05) * g + b
        key = jax.random.key(seed)
        ks = jax.random.split(key, 10)
        sc = 1.0 / np.sqrt(C)
        return {'x': jax.random.normal(ks[0], (N, C), jnp.float32), 'edge_index': jax.random.randint(ks[1], (2, E), 0, N), 'edge_type': jax.random.randint(ks[2], (E,), 0, R), 'W_Q': jax.random.normal(ks[3], (L, R, H, C, D), jnp.float32) * sc, 'W_K': jax.random.normal(ks[4], (L, R, H, C, D), jnp.float32) * sc, 'W_V': jax.random.normal(ks[5], (L, R, H, C, D), jnp.float32) * sc, 'W_concat': jax.random.normal(ks[6], (L, R, H * D, C), jnp.float32) * sc, 'sem_w': jax.random.normal(ks[7], (L, C), jnp.float32) * sc, 'sem_b': jnp.zeros((L,), jnp.float32), 'W_self': jax.random.normal(ks[8], (L, C, C), jnp.float32) * sc, 'ln_g': jnp.ones((L, C), jnp.float32), 'ln_b': jnp.zeros((L, C), jnp.float32)}
    _L0_gnn_all = _L0_gnn_setup()
    _L0_gnn_in = {k: v for k, v in _L0_gnn_all.items() if k in ('W_Q', 'W_K', 'W_V', 'W_concat', 'sem_w', 'sem_b', 'W_self', 'ln_g', 'ln_b')}
    del _L0_gnn_all

    def _L1_gnn_setup():
        import jax, jax.numpy as jnp
        import numpy as np
        import math
        N_NODES = 3125
        N_EDGES = 50000
        IN_CH = 64
        OUT_CH = 64
        EPS = 1e-12
        key = jax.random.key(seed)
        k1, k2, k3, k4, k5 = jax.random.split(key, 5)
        x = jax.random.normal(k1, (N_NODES, IN_CH), dtype=jnp.float32)
        edge_index = jax.random.randint(k2, (2, N_EDGES), 0, N_NODES, dtype=jnp.int64)
        edge_attr = jax.random.uniform(k3, (N_EDGES,), dtype=jnp.float32)
        stdv = 1.0 / math.sqrt(IN_CH)
        weight = jax.random.uniform(k4, (IN_CH, OUT_CH), dtype=jnp.float32, minval=-stdv, maxval=stdv)
        bias = jax.random.uniform(k5, (OUT_CH,), dtype=jnp.float32, minval=-stdv, maxval=stdv)
        return {'x': x, 'edge_index': edge_index, 'edge_attr': edge_attr, 'weight': weight, 'bias': bias}
    _L1_gnn_all = _L1_gnn_setup()
    _L1_gnn_in = {k: v for k, v in _L1_gnn_all.items() if k in ('weight', 'bias')}
    del _L1_gnn_all

    def _L2_gnn_setup():
        import jax, jax.numpy as jnp
        import numpy as np
        N_NODES = 50000
        N_EDGES = 1250000
        D_NODE = 64
        D_EDGE = 64
        M_OUT = 64
        U_OUT = 64
        key = jax.random.key(seed)
        k1, k2, k3, k4, k5, k6 = jax.random.split(key, 6)
        H = jax.random.normal(k1, (N_NODES, D_NODE), dtype=jnp.float32)
        Xe = jax.random.normal(k2, (N_EDGES, D_EDGE), dtype=jnp.float32)
        id_Xe = jax.random.randint(k3, (2, N_EDGES), 0, N_NODES, dtype=jnp.int64)
        M_W = jax.random.normal(k4, (M_OUT, D_NODE + D_EDGE), dtype=jnp.float32) * 0.05
        M_b = jnp.zeros((M_OUT,), dtype=jnp.float32)
        U_W = jax.random.normal(k5, (U_OUT, D_NODE + M_OUT), dtype=jnp.float32) * 0.05
        U_b = jnp.zeros((U_OUT,), dtype=jnp.float32)
        return {'H': H, 'Xe': Xe, 'id_Xe': id_Xe, 'M_W': M_W, 'M_b': M_b, 'U_W': U_W, 'U_b': U_b}
    _L2_gnn_all = _L2_gnn_setup()
    _L2_gnn_in = {k: v for k, v in _L2_gnn_all.items() if k in ('M_W', 'M_b', 'U_W', 'U_b')}
    del _L2_gnn_all

    def _L3_gnn_setup():
        import jax, jax.numpy as jnp
        import numpy as np
        NEG_SLOPE = 0.2

        def _gat_layer(x, src, dst, n_nodes, W, a_src, a_dst, b):
            h = x @ W
            alpha_s = h @ a_src
            alpha_d = h @ a_dst
            e = jax.nn.leaky_relu(alpha_s[src] + alpha_d[dst], NEG_SLOPE)
            m = jax.ops.segment_max(e, dst, num_segments=n_nodes)
            w = jnp.exp(e - m[dst])
            z = jax.ops.segment_sum(w, dst, num_segments=n_nodes)
            alpha = w / (z[dst] + 1e-16)
            out = jax.ops.segment_sum(alpha[:, None] * h[src], dst, num_segments=n_nodes)
            return out + b
        key = jax.random.key(seed)
        N, E, D_IN, D_H, D_OUT = (50000, 25000, 64, 64, 64)
        ks = jax.random.split(key, 12)
        x = jax.random.normal(ks[0], (N, D_IN), dtype=jnp.float32)
        edge_index = jax.random.randint(ks[1], (2, E), 0, N, dtype=jnp.int64)
        s = 1.0 / np.sqrt(D_IN)
        W1 = jax.random.normal(ks[2], (D_IN, D_H), dtype=jnp.float32) * s
        a_src1 = jax.random.normal(ks[3], (D_H,), dtype=jnp.float32) * s
        a_dst1 = jax.random.normal(ks[4], (D_H,), dtype=jnp.float32) * s
        b1 = jnp.zeros((D_H,), dtype=jnp.float32)
        s2 = 1.0 / np.sqrt(D_H)
        W2 = jax.random.normal(ks[5], (D_H, D_OUT), dtype=jnp.float32) * s2
        a_src2 = jax.random.normal(ks[6], (D_OUT,), dtype=jnp.float32) * s2
        a_dst2 = jax.random.normal(ks[7], (D_OUT,), dtype=jnp.float32) * s2
        b2 = jnp.zeros((D_OUT,), dtype=jnp.float32)
        return {'x': x, 'edge_index': edge_index, 'W1': W1, 'a_src1': a_src1, 'a_dst1': a_dst1, 'b1': b1, 'W2': W2, 'a_src2': a_src2, 'a_dst2': a_dst2, 'b2': b2}
    _L3_gnn_all = _L3_gnn_setup()
    _L3_gnn_in = {k: v for k, v in _L3_gnn_all.items() if k in ('W1', 'a_src1', 'a_dst1', 'b1', 'W2', 'a_src2', 'a_dst2', 'b2')}
    del _L3_gnn_all
    return {'x': x, 'src': src, 'dst': dst, 'edge_attr_64': edge_attr_64, 'edge_type_4': edge_type_4, 'edge_weight': edge_weight, 'L0_gnn_W_Q': _L0_gnn_in['W_Q'], 'L0_gnn_W_K': _L0_gnn_in['W_K'], 'L0_gnn_W_V': _L0_gnn_in['W_V'], 'L0_gnn_W_concat': _L0_gnn_in['W_concat'], 'L0_gnn_sem_w': _L0_gnn_in['sem_w'], 'L0_gnn_sem_b': _L0_gnn_in['sem_b'], 'L0_gnn_W_self': _L0_gnn_in['W_self'], 'L0_gnn_ln_g': _L0_gnn_in['ln_g'], 'L0_gnn_ln_b': _L0_gnn_in['ln_b'], 'L1_gnn_weight': _L1_gnn_in['weight'], 'L1_gnn_bias': _L1_gnn_in['bias'], 'L2_gnn_M_W': _L2_gnn_in['M_W'], 'L2_gnn_M_b': _L2_gnn_in['M_b'], 'L2_gnn_U_W': _L2_gnn_in['U_W'], 'L2_gnn_U_b': _L2_gnn_in['U_b'], 'L3_gnn_W1': _L3_gnn_in['W1'], 'L3_gnn_a_src1': _L3_gnn_in['a_src1'], 'L3_gnn_a_dst1': _L3_gnn_in['a_dst1'], 'L3_gnn_b1': _L3_gnn_in['b1'], 'L3_gnn_W2': _L3_gnn_in['W2'], 'L3_gnn_a_src2': _L3_gnn_in['a_src2'], 'L3_gnn_a_dst2': _L3_gnn_in['a_dst2'], 'L3_gnn_b2': _L3_gnn_in['b2']}

def reference(x, src, dst, edge_attr_64, edge_type_4, edge_weight, L0_gnn_W_Q, L0_gnn_W_K, L0_gnn_W_V, L0_gnn_W_concat, L0_gnn_sem_w, L0_gnn_sem_b, L0_gnn_W_self, L0_gnn_ln_g, L0_gnn_ln_b, L1_gnn_weight, L1_gnn_bias, L2_gnn_M_W, L2_gnn_M_b, L2_gnn_U_W, L2_gnn_U_b, L3_gnn_W1, L3_gnn_a_src1, L3_gnn_a_dst1, L3_gnn_b1, L3_gnn_W2, L3_gnn_a_src2, L3_gnn_a_dst2, L3_gnn_b2):
    import jax
    import jax.numpy as jnp

    def _L0_gnn_ref(x, edge_index, edge_type, W_Q, W_K, W_V, W_concat, sem_w, sem_b, W_self, ln_g, ln_b):
        import jax, jax.numpy as jnp
        import numpy as np
        N = 3125
        E = 50000
        C = 64
        H = 8
        D = C // H
        R = 4
        L = 2

        def _layer(x, src, dst, edge_type, WQ, WK, WV, Wcat, sw, sb, Ws, g, b):
            inv_sqrt_d = 1.0 / np.sqrt(D)
            rel_msgs = []
            for r in range(R):
                mask = (edge_type == r).astype(x.dtype)
                Q = jnp.einsum('nc,hcd->nhd', x, WQ[r])
                K = jnp.einsum('nc,hcd->nhd', x, WK[r])
                V = jnp.einsum('nc,hcd->nhd', x, WV[r])
                energy = jnp.einsum('ehd,ehd->eh', Q[dst], K[src]) * inv_sqrt_d
                energy = jax.nn.leaky_relu(energy)
                alpha_n = jax.ops.segment_sum(energy * mask[:, None], dst, num_segments=N)
                alpha = jax.nn.softmax(alpha_n, axis=0)
                w = alpha[dst] * mask[:, None]
                m = jax.ops.segment_sum(w[:, :, None] * V[src], dst, num_segments=N)
                rel_msgs.append(m.reshape(N, H * D) @ Wcat[r])
            stacked = jnp.stack(rel_msgs)
            beta = jax.nn.softmax(stacked @ sw + sb, axis=0)
            agg = jnp.einsum('rn,rnc->nc', beta, stacked)
            y = x + jax.nn.gelu(x @ Ws + agg, approximate=False)
            mu = y.mean(-1, keepdims=True)
            var = y.var(-1, keepdims=True)
            return (y - mu) / jnp.sqrt(var + 1e-05) * g + b
        src, dst = (edge_index[0], edge_index[1])
        for l in range(L):
            x = _layer(x, src, dst, edge_type, W_Q[l], W_K[l], W_V[l], W_concat[l], sem_w[l], sem_b[l], W_self[l], ln_g[l], ln_b[l])
        return x

    def _L1_gnn_ref(x, edge_index, edge_attr, weight, bias):
        import jax, jax.numpy as jnp
        import numpy as np
        import math
        N_NODES = 3125
        N_EDGES = 50000
        IN_CH = 64
        OUT_CH = 64
        EPS = 1e-12
        row, col = (edge_index[0], edge_index[1])
        msgs = edge_attr[:, None] * x[col]
        agg = jax.ops.segment_sum(msgs, row, num_segments=x.shape[0])
        out = agg @ weight + bias
        norm = jnp.linalg.norm(out, axis=-1, keepdims=True)
        out = out / jnp.maximum(norm, EPS)
        return out

    def _L2_gnn_ref(H, Xe, id_Xe, M_W, M_b, U_W, U_b):
        import jax, jax.numpy as jnp
        import numpy as np
        N_NODES = 50000
        N_EDGES = 1250000
        D_NODE = 64
        D_EDGE = 64
        M_OUT = 64
        U_OUT = 64
        features = H[id_Xe[0]]
        M_in = jnp.concatenate([features, Xe], axis=1)
        Y = jax.nn.relu(M_in @ M_W.T + M_b)
        Z = jax.ops.segment_sum(Y, id_Xe[1], num_segments=H.shape[0])
        U_in = jnp.concatenate([H, Z], axis=1)
        H_next = jax.nn.relu(U_in @ U_W.T + U_b)
        return H_next

    def _L3_gnn_ref(x, edge_index, W1, a_src1, a_dst1, b1, W2, a_src2, a_dst2, b2):
        import jax, jax.numpy as jnp
        import numpy as np
        NEG_SLOPE = 0.2

        def _gat_layer(x, src, dst, n_nodes, W, a_src, a_dst, b):
            h = x @ W
            alpha_s = h @ a_src
            alpha_d = h @ a_dst
            e = jax.nn.leaky_relu(alpha_s[src] + alpha_d[dst], NEG_SLOPE)
            m = jax.ops.segment_max(e, dst, num_segments=n_nodes)
            w = jnp.exp(e - m[dst])
            z = jax.ops.segment_sum(w, dst, num_segments=n_nodes)
            alpha = w / (z[dst] + 1e-16)
            out = jax.ops.segment_sum(alpha[:, None] * h[src], dst, num_segments=n_nodes)
            return out + b
        n_nodes = x.shape[0]
        loops = jnp.arange(n_nodes, dtype=edge_index.dtype)
        src = jnp.concatenate([edge_index[0], loops])
        dst = jnp.concatenate([edge_index[1], loops])
        h = _gat_layer(x, src, dst, n_nodes, W1, a_src1, a_dst1, b1)
        h = jax.nn.relu(h)
        out = _gat_layer(h, src, dst, n_nodes, W2, a_src2, a_dst2, b2)
        return out
    edge_index = jnp.stack([src, dst])
    x = _layernorm(x + _L0_gnn_ref(x, edge_index, edge_type_4, L0_gnn_W_Q, L0_gnn_W_K, L0_gnn_W_V, L0_gnn_W_concat, L0_gnn_sem_w, L0_gnn_sem_b, L0_gnn_W_self, L0_gnn_ln_g, L0_gnn_ln_b), axis=-1)
    x = _layernorm(x + _L1_gnn_ref(x, edge_index, edge_weight, L1_gnn_weight, L1_gnn_bias), axis=-1)
    x = _layernorm(x + _L2_gnn_ref(x, edge_attr_64, edge_index, L2_gnn_M_W, L2_gnn_M_b, L2_gnn_U_W, L2_gnn_U_b), axis=-1)
    x = _layernorm(x + _L3_gnn_ref(x, edge_index, L3_gnn_W1, L3_gnn_a_src1, L3_gnn_a_dst1, L3_gnn_b1, L3_gnn_W2, L3_gnn_a_src2, L3_gnn_a_dst2, L3_gnn_b2), axis=-1)
    return x

_drawn_inputs = setup_inputs


def setup_inputs(seed=0):
    import zlib

    import numpy as np

    out = dict(_drawn_inputs(seed))
    spreads = {'L0_gnn_sem_b': (0.0, 0.8),
     'L0_gnn_ln_g': (1.0, 0.2),
     'L0_gnn_ln_b': (0.0, 0.1),
     'L2_gnn_M_b': (0.0, 0.1),
     'L2_gnn_U_b': (0.0, 0.1),
     'L3_gnn_b1': (0.0, 0.1),
     'L3_gnn_b2': (0.0, 0.1)}
    factors = {'L0_gnn_W_Q': 8.0,
     'L0_gnn_W_K': 8.0,
     'L0_gnn_W_V': 8.0,
     'L0_gnn_W_concat': 8.0,
     'L0_gnn_sem_w': 8.0,
     'L1_gnn_bias': 8.0,
     'L3_gnn_a_dst1': 2.796,
     'L3_gnn_a_src2': 26.999,
     'L3_gnn_a_dst2': 64.0}
    for name, (base, spread) in spreads.items():
        noise = np.random.default_rng([zlib.crc32(name.encode()), seed]).standard_normal(out[name].shape)
        drawn = base * np.exp(spread * noise) if base else spread * noise
        out[name] = jnp.asarray(drawn.astype(out[name].dtype))
    for name, factor in factors.items():
        out[name] = (out[name] * factor).astype(out[name].dtype)
    return out
```

```python
from contextlib import ExitStack

import concourse.bass as bass
from concourse import mybir

P = 128
N = 3125
NB = -(-N // P)
NPAD = NB * P
LAST = N - (NB - 1) * P
E = 103125
C = 64
R = 4
H = 8
D = C // H
EC = 808
HALF = 4
TURN = 2 * HALF
PAIR = 2
PAIRS = (E - NB) // (PAIR * P) + NB
NC = -(-PAIRS * PAIR // TURN) * TURN
TURNS = NC // TURN
CP = NC + TURN
NPK = CP // HALF
ROWS = P * CP
META = 8
ROWW = C + META
(M_REL, M_SRC, M_DLO, M_TYPE, M_WEIGHT, M_SROW, M_SLO, M_SPARE) = range(META)
NOWHERE = 1 << 20
NOBODY = 200.0
SROWW = C + 1
TW = 2 * C
GW = C + 1
UC = C * 0 + 73
BANK = 512
BIG = 1.0e30
assert P * EC >= E and EC % TURN == 0 and NPAD >= N

F32 = mybir.dt.float32
BF16 = mybir.dt.bfloat16
I32 = mybir.dt.int32
ALU = mybir.AluOpType
ACT = mybir.ActivationFunctionType
AX = mybir.AxisListType.X
IN_RANGE = "worked out on the chip from 25 blocks, so it is below that"


def psum_column(b):
    return b // 7 * BANK + b % 7 * UC


class Stage:

    def __init__(self, nc, name):
        self.nc, self.name, self.ctx, self.sems = nc, name, ExitStack(), []

    def __enter__(self):
        self.ctx.__enter__()
        return self

    def __exit__(self, *a):
        said = self.ctx.__exit__(*a)
        if self.sems and a[0] is None:
            self.nc.clear_and_free_semaphores(self.sems)
            self.nc.all_engine_barrier()
        return said

    def sb(self, name, shape, dt=F32):
        return self.ctx.enter_context(self.nc.sbuf_tensor(f"{self.name}_{name}", shape, dt))

    def ps(self, name, shape, dt=F32):
        return self.ctx.enter_context(self.nc.psum_tensor(f"{self.name}_ps_{name}", shape, dt))

    def sem(self, name):
        self.sems.append(self.nc.alloc_semaphore(f"{self.name}_sem_{name}"))
        return self.sems[-1]

    def block(self):
        return self.ctx.enter_context(self.nc.Block())


def chain(engine, sem):
    count = [0]

    def link(instruction):
        count[0] += 1
        instruction.then_inc(sem, 1)
        engine.wait_ge(sem, count[0])
    return link


def wide(ap, n):
    return ap.unsqueeze(len(ap.shape)).to_broadcast([*ap.shape, n])


def load_constants(nc, g, src):
    with Stage(nc, "load") as s:
        loaded = s.sem("loaded")
        block = s.block()

        @block.sync
        def _(sp):
            n = 0
            for to, of in src:
                sp.dma_start(to, of).then_inc(loaded, 16)
                n += 16
            sp.wait_ge(loaded, n)

        @block.vector
        def _(dve):
            nc.vector.memset(g.ones[:, :], 1.0)
            nc.vector.memset(g.zeros[:, :], 0.0)
            nc.vector.memset(g.fill[:, :, :], 0.0)


def fill_tables(nc, g):
    with Stage(nc, "fill") as s:
        block = s.block()

        @block.vector
        def _(dve):
            nc.vector.memset(g.fill[:, :, C + M_DLO:C + M_DLO + 1], NOBODY)
            nc.vector.memset(g.fill[:, :, C + M_SLO:C + M_SLO + 1], NOBODY)
            nc.vector.memset(g.fill[:, :, C + M_SROW:C + M_SROW + 1].bitcast(I32), NOWHERE)
            nc.vector.memset(g.sfill[:, :, 0:C], 0.0)
            nc.vector.memset(g.sfill[:, :, C:C + 1], NOBODY)
            nc.vector.tensor_copy(g.ident_b[:, :], g.ident[:, :])


def route(nc, g):
    with Stage(nc, "route") as s:
        hi_i = s.sb("hi_i", [P, EC], I32)
        hi = s.sb("hi", [P, EC])
        lo_i = s.sb("lo_i", [P, EC], I32)
        eq = s.sb("eq", [P, EC])
        cum = s.sb("cum", [P, EC])
        hit = s.sb("hit", [P, EC])
        rank = s.sb("rank", [P, EC])
        ones = s.sb("ones", [P, EC])
        cnt = s.sb("cnt", [P, 32])
        base = s.sb("base", [P, 32])
        padded = s.sb("padded", [NB, 1])
        padded_i = s.sb("padded_i", [NB, 1], I32)
        start = s.sb("start", [NB, 1])
        diag = s.sb("diag", [NB, NB])
        begun = s.sb("begun", [NB, CP // PAIR])
        blk = s.sb("blk", [1, CP // PAIR])
        bank_no = s.sb("bank_no", [1, CP // PAIR])
        col = s.sb("col", [1, CP // PAIR])
        ps_tot = s.ps("tot", [NB, 1])
        ps_start = s.ps("start", [NB, 1])
        ps_base = s.ps("base", [P, NB])
        ps_blk = s.ps("blk", [1, CP // PAIR])
        filled = s.sem("filled")
        step = s.sem("step")
        loop = [s.sem(f"loop{j}") for j in range(4)]
        counted = s.sem("counted")
        totals = s.sem("totals")
        rounded = s.sem("rounded")
        started = s.sem("started")
        diagonal = s.sem("diagonal")
        based = s.sem("based")
        begun_ready = s.sem("begun_ready")
        blocks = s.sem("blocks")
        block = s.block()

        @block.sync
        def _(sp):
            n = CP // TURN
            sp.dma_start(g.slots.rearrange("(p n u) w -> p n (u w)", p=P, n=n),
                         g.fill[:, :, :].rearrange("p u w -> p (u w)").unsqueeze(1)
                         .to_broadcast([P, n, TURN * ROWW])).then_inc(filled, 16)
            sp.dma_start(g.sslots.rearrange("(p n u) w -> p n (u w)", p=P, n=n),
                         g.sfill[:, :, :].rearrange("p u w -> p (u w)").unsqueeze(1)
                         .to_broadcast([P, n, TURN * SROWW])).then_inc(filled, 16)
            sp.wait_ge(filled, 32)

        @block.tensor
        def _(pe):
            for k in range(2):
                pe.wait_ge(counted, k + 1)
                nc.tensor.matmul(ps_tot[:, :], cnt[:, 0:NB], g.ones[:, 0:1],
                                 start=True, stop=True).then_inc(totals, 1)
                pe.wait_ge(rounded, k + 1)
                nc.tensor.matmul(ps_start[:, :], g.before[0:NB, 0:NB], padded[:, :],
                                 start=True, stop=True).then_inc(started, 1)
                pe.wait_ge(diagonal, k + 1)
                nc.tensor.matmul(ps_base[:, :], g.before[:, :], cnt[:, 0:NB], start=True, stop=False)
                nc.tensor.matmul(ps_base[:, :], g.ones[0:NB, :], diag[:, :],
                                 start=False, stop=True).then_inc(based, 1)
                pe.wait_ge(begun_ready, k + 1)
                nc.tensor.matmul(ps_blk[:, :], g.ones[0:NB, 0:1], begun[:, :],
                                 start=True, stop=True).then_inc(blocks, 1)

        @block.vector
        def _(dve):
            link = chain(dve, step)
            link(nc.vector.memset(ones[:, :], 1.0))
            plan = [(g.dst_i, g.blk_dst, g.col_dst, M_DLO, None), (g.src_i, g.blk_src, g.col_src, M_SLO, M_SROW)]
            for k, (key, blk_out, col_out, m_lo, m_row) in enumerate(plan):
                link(nc.vector.tensor_scalar(hi_i[:, :], key[:, :], 7, None, ALU.logical_shift_right))
                link(nc.vector.tensor_copy(hi[:, :], hi_i[:, :]))
                link(nc.vector.scalar_tensor_tensor(hi[:, :], g.absent[:, :], 100.0, hi[:, :], ALU.mult, ALU.add))
                link(nc.vector.tensor_scalar(lo_i[:, :], key[:, :], P - 1, None, ALU.bitwise_and))
                link(nc.vector.tensor_copy(g.meta0[:, :, m_lo], lo_i[:, :]))
                link(nc.vector.memset(rank[:, :], 0.0))
                with dve.Fori(0, NB) as b:
                    at = b + k * NB
                    nc.vector.tensor_scalar(eq[:, :], hi[:, :], g.iota[:, bass.ds(b, 1)], None,
                                            ALU.is_equal).then_inc(loop[0], 1)
                    dve.wait_ge(loop[0], at + 1)
                    nc.vector.tensor_tensor_scan(cum[:, :], ones[:, :], eq[:, :], 0.0,
                                                 ALU.mult, ALU.add).then_inc(loop[1], 1)
                    dve.wait_ge(loop[1], at + 1)
                    nc.vector.scalar_tensor_tensor(hit[:, :], cum[:, :], -1.0, eq[:, :],
                                                   ALU.add, ALU.mult).then_inc(loop[2], 1)
                    nc.vector.tensor_copy(cnt[:, bass.ds(b, 1)], cum[:, EC - 1:EC])
                    dve.wait_ge(loop[2], b + 2 * k * NB + 1)
                    nc.vector.tensor_tensor(rank[:, :], rank[:, :], hit[:, :], ALU.add).then_inc(loop[3], 1)
                    dve.wait_ge(loop[3], b + 2 * k * NB + 1)
                dve.engine_nop().then_inc(counted, 1)
                dve.wait_ge(totals, k + 1)
                link(nc.vector.tensor_scalar(padded_i[:, :], ps_tot[:, :], float(PAIR * P - 1), None, ALU.add))
                link(nc.vector.tensor_scalar(padded_i[:, :], padded_i[:, :], 8, 8,
                                             ALU.logical_shift_right, ALU.logical_shift_left))
                nc.vector.tensor_copy(padded[:, :], padded_i[:, :]).then_inc(rounded, 1)
                dve.wait_ge(started, k + 1)
                link(nc.vector.tensor_copy(start[:, :], ps_start[:, :]))
                nc.vector.tensor_scalar(diag[:, :], g.ident[0:NB, 0:NB], start[:, 0:1], None,
                                        ALU.mult).then_inc(diagonal, 1)
                nc.vector.tensor_scalar(begun[:, :], g.pair_slot[:, :], start[:, 0:1], None,
                                        ALU.is_ge).then_inc(begun_ready, 1)
                dve.wait_ge(based, k + 1)
                link(nc.vector.tensor_copy(base[:, 0:NB], ps_base[:, :]))
                with dve.Fori(0, NB) as b:
                    nc.vector.tensor_scalar(hit[:, :], hi[:, :], g.iota[:, bass.ds(b, 1)], base[:, bass.ds(b, 1)],
                                            ALU.is_equal, ALU.mult).then_inc(loop[2], 1)
                    dve.wait_ge(loop[2], b + (2 * k + 1) * NB + 1)
                    nc.vector.tensor_tensor(rank[:, :], rank[:, :], hit[:, :], ALU.add).then_inc(loop[3], 1)
                    dve.wait_ge(loop[3], b + (2 * k + 1) * NB + 1)
                link(nc.vector.tensor_copy(hi_i[:, :], rank[:, :]))
                link(nc.vector.tensor_scalar(lo_i[:, :], hi_i[:, :], P - 1, None, ALU.bitwise_and))
                link(nc.vector.tensor_scalar(hi_i[:, :], hi_i[:, :], 7, None, ALU.logical_shift_right))
                link(nc.vector.tensor_copy(eq[:, :], lo_i[:, :]))
                link(nc.vector.tensor_copy(cum[:, :], hi_i[:, :]))
                link(nc.vector.scalar_tensor_tensor(hit[:, :], eq[:, :], float(CP), cum[:, :], ALU.mult, ALU.add))
                to = g.row0[:, :] if m_row is None else g.meta0[:, :, m_row].bitcast(I32)
                link(nc.vector.scalar_tensor_tensor(to, g.absent[:, :], float(NOWHERE), hit[:, :], ALU.mult, ALU.add))
                dve.wait_ge(blocks, k + 1)
                link(nc.vector.tensor_scalar(blk[:, :], ps_blk[:, :], -1.0, None, ALU.add))
                link(nc.vector.tensor_scalar(bank_no[:, :], blk[:, :], 7.0, None, ALU.is_ge))
                for edge in (14.0, 21.0):
                    link(nc.vector.scalar_tensor_tensor(bank_no[:, :], blk[:, :], edge, bank_no[:, :], ALU.is_ge, ALU.add))
                link(nc.vector.tensor_scalar(bank_no[:, :], bank_no[:, :], float(BANK - 7 * UC), None, ALU.mult))
                link(nc.vector.scalar_tensor_tensor(col[:, :], blk[:, :], float(UC), bank_no[:, :], ALU.mult, ALU.add))
                for of, to, shift in ((blk, blk_out, 5), (col, col_out, 12)):
                    two = of[:, :].rearrange("a (h j) -> a h j", j=PAIR)
                    link(nc.vector.memset(to[:, 0:1], 0))
                    link(nc.vector.scalar_tensor_tensor(to[:, 1:1 + NPK], two[:, :, 1], float(1 << shift), two[:, :, 0],
                                                        ALU.mult, ALU.add))
            link(nc.vector.tensor_copy(eq[:, :], g.typ_i[:, :]))
            link(nc.vector.tensor_copy(g.meta0[:, :, M_TYPE], eq[:, :]))
            link(nc.vector.tensor_copy(cum[:, :], g.src_i[:, :]))
            link(nc.vector.scalar_tensor_tensor(g.meta0[:, :, M_REL].bitcast(I32), eq[:, :], float(NPAD), cum[:, :],
                                                ALU.mult, ALU.add))
            link(nc.vector.tensor_copy(g.meta0[:, :, M_SRC].bitcast(I32), cum[:, :]))
            link(nc.vector.tensor_copy(g.meta0[:, :, M_WEIGHT], g.weight0[:, :]))
            link(nc.vector.memset(g.meta0[:, :, M_SPARE:M_SPARE + 1], 0.0))


def scatter_edges(nc, g):
    with Stage(nc, "scatter") as s:
        chan = [s.sb(f"chan{h}", [C, HALF * P]) for h in range(2)]
        row = [s.sb(f"row{h}", [P, HALF, ROWW]) for h in range(2)]
        to = [s.sb(f"to{h}", [P, HALF], I32) for h in range(2)]
        ps = [s.ps(f"msg{h}", [P, HALF, C]) for h in range(2)]
        chan_ready = [s.sem(f"chan_ready{h}") for h in range(2)]
        msg_ready = s.sem("msg_ready")
        row_ready = s.sem("row_ready")
        scattered = [s.sem(f"scattered{h}") for h in range(2)]
        row_free = s.sem("row_free")
        opened = s.sem("opened")
        block = s.block()

        @block.sync
        def _(sp):
            sp.sem_inc(row_free, 2)
            with sp.Fori(0, EC // TURN) as i:
                for h in range(2):
                    sp.wait_ge(msg_ready, 2 * i + h + 1)
                    sp.dma_start(chan[h][:, :], g.attr[:, bass.ds(i * (TURN * P) + h * HALF * P, HALF * P)]
                                 ).then_inc(chan_ready[h], 16)

        @block.scalar
        def _(act):
            with act.Fori(0, EC // TURN) as i:
                for h in range(2):
                    act.wait_ge(scattered[h], 16 * HALF * i + 16 * HALF)
                    act.sem_inc(row_free, 1)

        @block.tensor
        def _(pe):
            pe.sem_inc(msg_ready, 2)
            with pe.Fori(0, EC // TURN) as i:
                for h in range(2):
                    pe.wait_ge(chan_ready[h], 16 * i + 16)
                    pe.wait_ge(row_ready, 2 * i + h + 1)
                    for c in range(HALF):
                        last = nc.tensor.matmul(ps[h][:, c, :], chan[h][:, c * P:(c + 1) * P], g.w_msg_edge[:, :],
                                                start=True, stop=True)
                    last.then_inc(msg_ready, 1)

        @block.vector
        def _(dve):
            dve.sem_inc(row_ready, 2)
            with dve.Fori(0, EC // TURN) as i:
                for h in range(2):
                    k = 2 * i + h
                    at = i * TURN + h * HALF
                    dve.wait_ge(msg_ready, k + 3)
                    dve.wait_ge(row_free, k + 1)
                    nc.vector.tensor_tensor(row[h][:, :, 0:C], ps[h][:, :, :],
                                            g.b_msg[:, :].unsqueeze(1).to_broadcast([P, HALF, C]), ALU.add)
                    nc.vector.tensor_copy(row[h][:, :, C:ROWW], g.meta0[:, bass.ds(at, HALF), :])
                    nc.vector.tensor_copy(to[h][:, :], g.row0[:, bass.ds(at, HALF)]).then_inc(row_ready, 1)

        @block.gpsimd
        def _(pool):
            with pool.Fori(0, EC // TURN) as i:
                for h in range(2):
                    pool.wait_ge(row_ready, 2 * i + h + 3)
                    pool.sem_inc(opened, 1)
                    for c in range(HALF):
                        pool.indirect_dma_start(g.slots, bass.IndirectOffsetOnAxis(ap=to[h][:, c:c + 1], axis=0),
                                                row[h][:, c, :], None, bounds_check=ROWS - 1, oob_is_err=False
                                                ).then_inc(scattered[h], 16)
            for h in range(2):
                pool.wait_ge(scattered[h], 16 * HALF * (EC // TURN))


def load_meta(nc, g):
    with Stage(nc, "meta") as s:
        loaded = s.sem("loaded")
        block = s.block()

        @block.sync
        def _(sp):
            rows = g.slots.rearrange("(p n) w -> p n w", p=P)
            sp.dma_start(g.meta[:, :, :], rows[:, :, C:ROWW]).then_inc(loaded, 16)
            sp.wait_ge(loaded, 16)

    with Stage(nc, "mask") as s:
        block = s.block()

        @block.vector
        def _(dve):
            for r in range(R):
                nc.vector.tensor_scalar(g.mask[:, :, r], g.meta[:, :, M_TYPE], float(r), None, ALU.is_equal)


def node_product(nc, g, name, src, width, weight, outs):
    GROUP = 5
    units = [(b, o) for b in range(GROUP) for o in outs]
    U = len(units)
    with Stage(nc, name) as s:
        rows = s.sb("rows", [P, GROUP, width])
        cols = s.sb("cols", [width, GROUP, P])
        ps_t = s.ps("t", [width, GROUP, P])
        ps = [s.ps(f"p{j}", [P, BANK]) for j in range(4)]
        rows_ready = s.sem("rows_ready")
        opened = s.sem("opened")
        turned = s.sem("turned")
        cols_ready = s.sem("cols_ready")
        product = s.sem("product")
        taken = s.sem("taken")
        block = s.block()

        @block.vector
        def _(dve):
            with dve.Fori(0, NB // GROUP) as i:
                dve.wait_ge(turned, i + 1)
                nc.vector.tensor_copy(rows[:, :, :], src[:, bass.ds(i * GROUP, GROUP), :]).then_inc(rows_ready, 1)

        @block.tensor
        def _(pe):
            pe.sem_inc(turned, 1)
            with pe.Fori(0, NB // GROUP) as i:
                pe.wait_ge(rows_ready, i + 1)
                pe.wait_ge(cols_ready, i + 1)
                pe.sem_inc(opened, 1)
                for b in range(GROUP):
                    last = nc.tensor.transpose(ps_t[:, b, :], rows[:, b, :], g.ident[:, :])
                last.then_inc(turned, 1)
                pe.wait_ge(cols_ready, i + 2)
                for u, (b, (c0, c1, to)) in enumerate(units):
                    before = u - 4 if u >= 4 else max(v for v in range(U) if v % 4 == u % 4) - U if U > u else 0
                    pe.wait_ge(taken, i * U + before + 1 + U)
                    nc.tensor.matmul(ps[u % 4][:, 0:c1 - c0], cols[:, b, :], weight[:, c0:c1],
                                     start=True, stop=True).then_inc(product, 1)

        @block.scalar
        def _(act):
            act.sem_inc(cols_ready, 1)
            act.sem_inc(taken, U)
            with act.Fori(0, NB // GROUP) as i:
                act.wait_ge(turned, i + 2)
                nc.scalar.copy(cols[:, :, :], ps_t[:, :, :]).then_inc(cols_ready, 1)
                for u, (b, (c0, c1, to)) in enumerate(units):
                    act.wait_ge(product, i * U + u + 1)
                    nc.scalar.copy(to[:, bass.ds(i * GROUP + b, 1), :], ps[u % 4][:, 0:c1 - c0].unsqueeze(1)
                                   ).then_inc(taken, 1)


def split_bf16(nc, link, parts, whole, rest):
    link(nc.vector.tensor_copy(parts[0], whole))
    link(nc.vector.tensor_tensor(rest, whole, parts[0], ALU.subtract))
    link(nc.vector.tensor_copy(parts[1], rest))
    link(nc.vector.tensor_tensor(parts[2], rest, parts[1], ALU.subtract))


def two_blocks(nc, engine, packed, k, shift, top):
    word = engine.value_load(packed[0:1, bass.ds(k, 1)])
    return [nc.s_assert_within((word >> (shift * j)) & ((1 << shift) - 1), 0, top,
                               skip_runtime_bounds_check_because=IN_RANGE) for j in range(2)]


def relation_products(nc, g, l):
    with Stage(nc, f"rel{l}") as s:
        kv = s.sb("kv", [P, NB, R * TW])
        q = s.sb("q", [P, NB, R * C])
        node_product(nc, g, f"relp{l}", g.h, C, g.w_rel[l],
                     [(0, R * TW, kv), (R * TW, R * (TW + C), q), (R * (TW + C), R * (TW + C) + C, g.own)])
        written = s.sem("written")
        step = s.sem("step")
        block = s.block()

        @block.sync
        def _(sp):
            rows = g.rel_table.rearrange("(r b p) w -> r p b w", r=R, p=P)
            for r in range(R):
                sp.dma_start(rows[r], kv[:, :, r * TW:(r + 1) * TW]).then_inc(written, 16)
            sp.wait_ge(written, 16 * R)

        @block.vector
        def _(dve):
            link = chain(dve, step)
            link(nc.vector.tensor_scalar(q[:, :, :], q[:, :, :], float(D) ** -0.5, None, ALU.mult))
            split_bf16(nc, link, [g.q_split[:, j, :, :] for j in range(3)], q[:, :, :], q[:, :, :])


def relation_pass(nc, g, l):
    W = R * C + R * H
    with Stage(nc, f"relpass{l}") as s:
        idx = [s.sb(f"idx{h}", [P, HALF], I32) for h in range(2)]
        row = [s.sb(f"row{h}", [P, HALF, TW]) for h in range(2)]
        hot_b = [s.sb(f"hot_b{h}", [P, HALF, P], BF16) for h in range(2)]
        hot_t = [s.sb(f"hot_t{h}", [P, HALF, P], BF16) for h in range(2)]
        hot = [s.sb(f"hot{h}", [P, HALF, P]) for h in range(2)]
        prod = s.sb("prod", [P, HALF, R * C])
        en = s.sb("en", [P, HALF, R * H])
        en_m = s.sb("en_m", [P, HALF, R * H])
        val = [s.sb(f"val{h}", [P, HALF, W]) for h in range(2)]
        ps_t = [s.ps(f"t{h}", [P, HALF, 2 * P], BF16) for h in range(2)]
        ps_q = [s.ps(f"q{h}", [P, HALF, R * C]) for h in range(2)]
        ps_s = [s.ps(f"s{j}", [P, BANK]) for j in range(2)]
        idx_ready = s.sem("idx_ready")
        opened = s.sem("opened")
        gathered = [s.sem(f"gathered{h}") for h in range(2)]
        hot_b_ready = s.sem("hot_b_ready")
        turned = s.sem("turned")
        hot_t_ready = s.sem("hot_t_ready")
        query_ready = s.sem("query_ready")
        query_used = s.sem("query_used")
        reduced = s.sem("reduced")
        energy_ready = s.sem("energy_ready")
        value_ready = s.sem("value_ready")
        summed = s.sem("summed")
        added = s.sem("added")
        step = s.sem("step")
        block = s.block()

        @block.gpsimd
        def _(pool):
            with pool.Fori(0, TURNS) as i:
                for h in range(2):
                    k = 2 * i + h
                    pool.wait_ge(idx_ready, k + 1)
                    pool.wait_ge(value_ready, k + 1)
                    pool.sem_inc(opened, 1)
                    for c in range(HALF):
                        pool.indirect_dma_start(row[h][:, c, :], None, g.rel_table,
                                                bass.IndirectOffsetOnAxis(ap=idx[h][:, c:c + 1], axis=0)
                                                ).then_inc(gathered[h], 16)

        @block.scalar
        def _(act):
            def take(h, wait):
                act.wait_ge(turned, wait)
                nc.scalar.copy(hot_t[h][:, :, :], ps_t[h][:, :, 0:P]).then_inc(hot_t_ready, 1)

            act.sem_inc(hot_t_ready, 2)
            act.sem_inc(value_ready, 2)
            take(0, 3)
            with act.Fori(0, TURNS) as i:
                for h in range(2):
                    k = 2 * i + h
                    act.wait_ge(query_ready, k + 2)
                    take(1 - h, k + 4)
                    act.wait_ge(gathered[h], 16 * HALF * i + 16 * HALF)
                    act.wait_ge(summed, k + 1)
                    for c in range(HALF):
                        for r in range(R):
                            last = nc.scalar.mul(val[h][:, c, r * C:(r + 1) * C], row[h][:, c, C:TW],
                                                 g.mask[:, bass.ds(i * TURN + h * HALF + c, 1), r])
                    last.then_inc(value_ready, 1)

        @block.tensor
        def _(pe):
            def turn(h, wait):
                pe.wait_ge(hot_b_ready, wait)
                pe.wait_ge(hot_t_ready, wait - 2)
                for c in range(HALF):
                    last = nc.tensor.transpose(ps_t[h][:, c, 0:P], hot_b[h][:, c, :], g.ident_b[:, :])
                last.then_inc(turned, 1)

            def query(h, k, wait):
                b = two_blocks(nc, pe, g.blk_dst, k + 1, 5, NB - 1)
                pe.wait_ge(hot_t_ready, wait)
                pe.wait_ge(query_used, wait - 2)
                for c in range(HALF):
                    for j in range(3):
                        last = nc.tensor.matmul(ps_q[h][:, c, :], hot_t[h][:, c, :],
                                                g.q_split[:, j, bass.ds(b[c // PAIR], 1), :].squeeze(1),
                                                start=(j == 0), stop=(j == 2))
                last.then_inc(query_ready, 1)

            pe.sem_inc(turned, 2)
            pe.sem_inc(query_ready, 2)
            pe.sem_inc(summed, 1)
            for j in range(2):
                last = nc.tensor.matmul(ps_s[j][:, :], g.zeros[:, 0:P], g.zeros[:, :], start=True, stop=True)
            last.then_inc(summed, 1)
            turn(0, 3)
            query(0, 0, 3)
            with pe.Fori(0, TURNS) as i:
                for h in range(2):
                    k = 2 * i + h
                    turn(1 - h, k + 4)
                    query(1 - h, k + 1, k + 4)
                    pe.wait_ge(energy_ready, k + 1)
                    pe.wait_ge(value_ready, k + 3)
                    pe.wait_ge(added, k + 1)
                    for c in range(HALF):
                        last = nc.tensor.matmul(ps_s[c // PAIR][:, 0:W], hot[h][:, c, :], val[h][:, c, :],
                                                start=(c % PAIR == 0), stop=(c % PAIR == PAIR - 1))
                    last.then_inc(summed, 1)

        @block.vector
        def _(dve):
            def hots(h, at, free):
                dve.wait_ge(turned, free)
                nc.vector.tensor_tensor(hot_b[h][:, :, :], g.iota[:, :].unsqueeze(1).to_broadcast([P, HALF, P]),
                                        wide(g.meta[:, bass.ds(at, HALF), M_DLO], P), ALU.is_equal
                                        ).then_inc(hot_b_ready, 1)

            def stage(h, at):
                nc.vector.tensor_copy(idx[h][:, :], g.meta[:, bass.ds(at, HALF), M_REL].bitcast(I32)
                                      ).then_inc(idx_ready, 1)

            def add(k, wait):
                b = two_blocks(nc, dve, g.blk_dst, k, 5, NB - 1)
                dve.wait_ge(summed, wait)
                for j in range(2):
                    dve.wait_ge(step, k * 2 + j + 1)
                    to = g.acc[:, bass.ds(b[j], 1), :].squeeze(1)
                    ins = nc.vector.tensor_tensor(to, ps_s[j][:, 0:W], to, ALU.add)
                    ins.then_inc(step, 1)
                dve.wait_ge(step, k * 2 + 3)
                dve.sem_inc(added, 1)

            dve.sem_inc(hot_b_ready, 2)
            dve.sem_inc(query_used, 2)
            nc.vector.memset(g.acc[:, :, :], 0.0).then_inc(step, 1)
            hots(0, 0, 1)
            for h in range(2):
                stage(h, h * HALF)
            with dve.Fori(0, TURNS) as i:
                for h in range(2):
                    k = 2 * i + h
                    at = i * TURN + h * HALF
                    hots(1 - h, at + HALF, k + 2)
                    dve.wait_ge(query_ready, k + 3)
                    dve.wait_ge(gathered[h], 16 * HALF * i + 16 * HALF)
                    for c in range(HALF):
                        last = nc.vector.tensor_tensor(
                            prod[:, c, :].rearrange("p (r w) -> p r w", r=R),
                            ps_q[h][:, c, :].rearrange("p (r w) -> p r w", r=R),
                            row[h][:, c, 0:C].unsqueeze(1).to_broadcast([P, R, C]), ALU.mult)
                    last.then_inc(query_used, 1)
                    dve.wait_ge(query_used, k + 3)
                    nc.vector.tensor_reduce(en[:, :, :], prod[:, :, :].rearrange("p c (g d) -> p c g d", d=D),
                                            AX, ALU.add).then_inc(reduced, 1)
                    stage(h, at + TURN)
                    nc.vector.tensor_tensor(hot[h][:, :, :], g.iota[:, :].unsqueeze(1).to_broadcast([P, HALF, P]),
                                            wide(g.meta[:, bass.ds(at, HALF), M_DLO], P), ALU.is_equal)
                    add(k, k + 2)
                    dve.wait_ge(reduced, 2 * k + 1)
                    nc.vector.tensor_tensor(en_m[:, :, :].rearrange("p c (r h) -> p (c r) h", r=R),
                                            en[:, :, :].rearrange("p c (r h) -> p (c r) h", r=R),
                                            wide(g.mask[:, bass.ds(at, HALF), :].rearrange("p c r -> p (c r)"), H),
                                            ALU.mult).then_inc(reduced, 1)
                    dve.wait_ge(reduced, 2 * k + 2)
                    nc.vector.scalar_tensor_tensor(val[h][:, :, R * C:W], en_m[:, :, :], 0.01, en_m[:, :, :],
                                                   ALU.mult, ALU.max).then_inc(energy_ready, 1)
            add(2 * TURNS, 2 * TURNS + 2)


def layer_norm(nc, g, name, y, affine=None):
    with Stage(nc, name) as s:
        mean = s.sb("mean", [P, NB])
        sq = s.sb("sq", [P, NB, C])
        step = s.sem("step")
        var_ready = s.sem("var_ready")
        sd_ready = s.sem("sd_ready")
        block = s.block()

        @block.scalar
        def _(act):
            act.wait_ge(var_ready, 1)
            nc.scalar.activation(mean[:, :], mean[:, :], ACT.Sqrt).then_inc(sd_ready, 1)

        @block.vector
        def _(dve):
            link = chain(dve, step)
            link(nc.vector.tensor_reduce(mean[:, :], y[:, :, :], AX, ALU.add))
            link(nc.vector.tensor_scalar(mean[:, :], mean[:, :], 1.0 / C, None, ALU.mult))
            link(nc.vector.tensor_tensor(y[:, :, :], y[:, :, :], wide(mean[:, :], C), ALU.subtract))
            link(nc.vector.tensor_tensor(sq[:, :, :], y[:, :, :], y[:, :, :], ALU.mult))
            link(nc.vector.tensor_reduce(mean[:, :], sq[:, :, :], AX, ALU.add))
            nc.vector.tensor_scalar(mean[:, :], mean[:, :], 1.0 / C, 1e-5, ALU.mult, ALU.add).then_inc(var_ready, 1)
            dve.wait_ge(sd_ready, 1)
            link(nc.vector.reciprocal(mean[:, :], mean[:, :]))
            link(nc.vector.tensor_tensor(y[:, :, :], y[:, :, :], wide(mean[:, :], C), ALU.mult))
            if affine is not None:
                for v, op in zip(affine, (ALU.mult, ALU.add)):
                    link(nc.vector.tensor_tensor(y[:, :, :], y[:, :, :],
                                                 v.unsqueeze(1).to_broadcast([P, NB, C]), op))


def relation_nodes(nc, g, l):
    RH = R * H
    with Stage(nc, f"relnode{l}") as s:
        en = s.sb("en", [P, NB, RH])
        part = s.sb("part", [P, RH])
        top = s.sb("top", [RH, 1])
        diag = s.sb("diag", [RH, RH])
        msg = s.sb("msg", [P, NB, R * C])
        mix = s.sb("mix", [P, NB * R, C])
        score = s.sb("score", [P, NB, R])
        best = s.sb("best", [P, NB])
        val = g.acc[:, :, 0:R * C]

        with Stage(nc, f"alpha{l}") as a:
            ps_a = a.ps("a", [P, BANK])
            ps_b = a.ps("b", [P, BANK])
            ps_c = a.ps("c", [P, BANK])
            step = a.sem("step")
            part_ready = a.sem("part_ready")
            turned = a.sem("turned")
            diag_ready = a.sem("diag_ready")
            shift_ready = a.sem("shift_ready")
            shifted = a.sem("shifted")
            exps = a.sem("exps")
            sums_ready = a.sem("sums_ready")
            total = a.sem("total")
            block = a.block()

            @block.tensor
            def _(pe):
                pe.wait_ge(part_ready, 1)
                nc.tensor.transpose(ps_a[0:RH, 0:P], part[:, :], g.ident[:, :]).then_inc(turned, 1)
                pe.wait_ge(diag_ready, 1)
                nc.tensor.matmul(ps_b[:, 0:RH], g.ones[0:RH, :], diag[:, :], start=True, stop=True).then_inc(shift_ready, 1)
                pe.wait_ge(sums_ready, 1)
                nc.tensor.matmul(ps_c[:, 0:RH], g.ones[:, :], part[:, :], start=True, stop=True).then_inc(total, 1)

            @block.scalar
            def _(act):
                act.wait_ge(shifted, 1)
                nc.scalar.activation(en[:, :, :], en[:, :, :], ACT.Exp).then_inc(exps, 1)

            @block.vector
            def _(dve):
                link = chain(dve, step)
                link(nc.vector.tensor_copy(en[:, :, :], g.acc[:, :, R * C:]))
                link(nc.vector.tensor_scalar(en[:, NB - 1, :], en[:, NB - 1, :], g.no_node[:, 0:1], None, ALU.add))
                nc.vector.tensor_reduce(part[:, :], en[:, :, :].rearrange("p b g -> p g b"), AX, ALU.max
                                        ).then_inc(part_ready, 1)
                dve.wait_ge(turned, 1)
                link(nc.vector.tensor_reduce(top[:, :], ps_a[0:RH, 0:P], AX, ALU.max))
                nc.vector.tensor_scalar(diag[:, :], g.ident[0:RH, 0:RH], top[:, 0:1], None, ALU.mult
                                        ).then_inc(diag_ready, 1)
                dve.wait_ge(shift_ready, 1)
                nc.vector.tensor_tensor(en[:, :, :], en[:, :, :], ps_b[:, 0:RH].unsqueeze(1).to_broadcast([P, NB, RH]),
                                        ALU.subtract).then_inc(shifted, 1)
                dve.wait_ge(exps, 1)
                nc.vector.tensor_reduce(part[:, :], en[:, :, :].rearrange("p b g -> p g b"), AX, ALU.add
                                        ).then_inc(sums_ready, 1)
                dve.wait_ge(total, 1)
                link(nc.vector.reciprocal(part[:, :], ps_c[:, 0:RH]))
                link(nc.vector.tensor_tensor(en[:, :, :], en[:, :, :], part[:, :].unsqueeze(1).to_broadcast([P, NB, RH]),
                                             ALU.mult))
                v = val.rearrange("p b (g d) -> p b g d", d=D)
                link(nc.vector.tensor_tensor(v, v, wide(en[:, :, :], D), ALU.mult))

        for j in range(2):
            node_product(nc, g, f"cat{l}{j}", g.acc[:, :, j * P:(j + 1) * P], P, g.w_cat[l][j],
                         [(0, P, msg[:, :, j * P:(j + 1) * P])])

        with Stage(nc, f"mix{l}") as a:
            step = a.sem("step")
            shifted = a.sem("shifted")
            exps = a.sem("exps")
            sum_ready = a.sem("sum_ready")
            gelu = a.sem("gelu")
            block = a.block()
            m = msg[:, :, :].rearrange("p b (r c) -> p (b r) c", c=C)

            @block.scalar
            def _(act):
                act.wait_ge(shifted, 1)
                nc.scalar.activation(score[:, :, :], score[:, :, :], ACT.Exp).then_inc(exps, 1)
                act.wait_ge(sum_ready, 1)
                nc.scalar.activation(g.own[:, :, :], g.own[:, :, :], ACT.Gelu).then_inc(gelu, 1)

            @block.vector
            def _(dve):
                link = chain(dve, step)
                flat = score[:, :, :].rearrange("p b r -> p (b r)")
                link(nc.vector.tensor_tensor(mix[:, :, :], m, g.sem_w[l].unsqueeze(1).to_broadcast([P, NB * R, C]),
                                             ALU.mult))
                link(nc.vector.tensor_reduce(flat, mix[:, :, :], AX, ALU.add))
                link(nc.vector.tensor_scalar(flat, flat, g.sem_b[:, l:l + 1], None, ALU.add))
                link(nc.vector.tensor_reduce(best[:, :], score[:, :, :], AX, ALU.max))
                nc.vector.tensor_tensor(score[:, :, :], score[:, :, :], wide(best[:, :], R), ALU.subtract
                                        ).then_inc(shifted, 1)
                dve.wait_ge(exps, 1)
                link(nc.vector.tensor_reduce(best[:, :], score[:, :, :], AX, ALU.add))
                link(nc.vector.reciprocal(best[:, :], best[:, :]))
                link(nc.vector.tensor_tensor(score[:, :, :], score[:, :, :], wide(best[:, :], R), ALU.mult))
                link(nc.vector.tensor_tensor(mix[:, :, :], m, wide(flat, C), ALU.mult))
                link(nc.vector.tensor_reduce(msg[:, :, 0:C], mix[:, :, :].rearrange("p (b r) c -> p b c r", r=R),
                                             AX, ALU.add))
                nc.vector.tensor_tensor(g.own[:, :, :], g.own[:, :, :], msg[:, :, 0:C], ALU.add).then_inc(sum_ready, 1)
                dve.wait_ge(gelu, 1)
                link(nc.vector.tensor_tensor(g.h[:, :, :], g.h[:, :, :], g.own[:, :, :], ALU.add))
    layer_norm(nc, g, f"relln{l}", g.h, (g.ln_g[l], g.ln_b[l]))


def residual_norm(nc, g, name):
    with Stage(nc, name + "_add") as s:
        block = s.block()

        @block.vector
        def _(dve):
            nc.vector.tensor_tensor(g.x[:, :, :], g.x[:, :, :], g.h[:, :, :], ALU.add)
    layer_norm(nc, g, name + "_ln", g.x)
    with Stage(nc, name + "_next") as s:
        block = s.block()

        @block.vector
        def _(dve):
            nc.vector.tensor_copy(g.h[:, :, :], g.x[:, :, :])


def gather_idx(nc, g, idx, h, at, word):
    return nc.vector.tensor_copy(idx[h][:, :], g.meta[:, bass.ds(at, HALF), word].bitcast(I32))


def one_hot(nc, g, to, at, word):
    return nc.vector.tensor_tensor(to, g.iota[:, :].unsqueeze(1).to_broadcast([P, HALF, P]),
                                   wide(g.meta[:, bass.ds(at, HALF), word], P), ALU.is_equal)


def weigh_pass(nc, g):
    with Stage(nc, "weigh") as s:
        split = s.sb("split", [P, 3, NB, C], BF16)
        to = [s.sb(f"to{h}", [P, HALF], I32) for h in range(2)]
        row = [s.sb(f"row{h}", [P, HALF, SROWW]) for h in range(2)]
        hot_b = [s.sb(f"hot_b{h}", [P, HALF, P], BF16) for h in range(2)]
        hot_t = [s.sb(f"hot_t{h}", [P, HALF, P], BF16) for h in range(2)]
        ps_t = [s.ps(f"t{h}", [P, HALF, 2 * P], BF16) for h in range(2)]
        ps_x = [s.ps(f"x{h}", [P, HALF, 2 * C]) for h in range(2)]
        opened = s.sem("opened")
        hot_b_ready = s.sem("hot_b_ready")
        turned = s.sem("turned")
        hot_t_ready = s.sem("hot_t_ready")
        found = s.sem("found")
        row_ready = s.sem("row_ready")
        row_free = s.sem("row_free")
        scattered = [s.sem(f"scattered{h}") for h in range(2)]
        split_rows(nc, g, "weigh_split", g.h, split)
        block = s.block()

        @block.sync
        def _(sp):
            sp.sem_inc(row_free, 2)
            with sp.Fori(0, TURNS) as i:
                for h in range(2):
                    sp.wait_ge(scattered[h], 16 * HALF * i + 16 * HALF)
                    sp.sem_inc(row_free, 1)

        @block.gpsimd
        def _(pool):
            with pool.Fori(0, TURNS) as i:
                for h in range(2):
                    pool.wait_ge(row_ready, 2 * i + h + 3)
                    pool.sem_inc(opened, 1)
                    for c in range(HALF):
                        pool.indirect_dma_start(g.sslots, bass.IndirectOffsetOnAxis(ap=to[h][:, c:c + 1], axis=0),
                                                row[h][:, c, :], None, bounds_check=ROWS - 1, oob_is_err=False
                                                ).then_inc(scattered[h], 16)
            for h in range(2):
                pool.wait_ge(scattered[h], 16 * HALF * TURNS)

        @block.scalar
        def _(act):
            act.sem_inc(hot_t_ready, 2)
            with act.Fori(0, TURNS) as i:
                for h in range(2):
                    k = 2 * i + h
                    act.wait_ge(turned, k + 3)
                    act.wait_ge(found, k + 1)
                    nc.scalar.copy(hot_t[h][:, :, :], ps_t[h][:, :, 0:P]).then_inc(hot_t_ready, 1)

        @block.tensor
        def _(pe):
            pe.sem_inc(turned, 2)
            pe.sem_inc(found, 2)
            with pe.Fori(0, TURNS) as i:
                for h in range(2):
                    k = 2 * i + h
                    b = two_blocks(nc, pe, g.blk_dst, k + 1, 5, NB - 1)
                    pe.wait_ge(hot_b_ready, k + 1)
                    pe.wait_ge(hot_t_ready, k + 1)
                    for c in range(HALF):
                        last = nc.tensor.transpose(ps_t[h][:, c, 0:P], hot_b[h][:, c, :], g.ident_b[:, :])
                    last.then_inc(turned, 1)
                    pe.wait_ge(hot_t_ready, k + 3)
                    pe.wait_ge(row_ready, k + 1)
                    for c in range(HALF):
                        for j in range(3):
                            last = nc.tensor.matmul(ps_x[h][:, c, 0:C], hot_t[h][:, c, :],
                                                    split[:, j, bass.ds(b[c // PAIR], 1), :].squeeze(1),
                                                    start=(j == 0), stop=(j == 2))
                    last.then_inc(found, 1)

        @block.vector
        def _(dve):
            dve.sem_inc(row_ready, 2)
            with dve.Fori(0, TURNS) as i:
                for h in range(2):
                    k = 2 * i + h
                    at = i * TURN + h * HALF
                    dve.wait_ge(turned, k + 1)
                    one_hot(nc, g, hot_b[h][:, :, :], at, M_DLO).then_inc(hot_b_ready, 1)
                    dve.wait_ge(found, k + 3)
                    dve.wait_ge(row_free, k + 1)
                    nc.vector.tensor_tensor(row[h][:, :, 0:C], ps_x[h][:, :, 0:C],
                                            wide(g.meta[:, bass.ds(at, HALF), M_WEIGHT], C), ALU.mult)
                    nc.vector.tensor_copy(row[h][:, :, C], g.meta[:, bass.ds(at, HALF), M_SLO])
                    gather_idx(nc, g, to, h, at, M_SROW).then_inc(row_ready, 1)


def split_rows(nc, g, name, of, split):
    with Stage(nc, name) as s:
        rest = s.sb("rest", [P, *of.shape[1:]])
        step = s.sem("step")
        block = s.block()

        @block.vector
        def _(dve):
            link = chain(dve, step)
            link(nc.vector.tensor_copy(rest[:], of[:]))
            split_bf16(nc, link, [split[:, j] for j in range(3)], rest[:], rest[:])


def open_sums(nc, pe, g, ps_sum):
    for j in range(4):
        last = nc.tensor.matmul(ps_sum[:, j * BANK:(j + 1) * BANK], g.zeros[:, 0:P], g.zeros[:, :],
                                start=True, stop=True, skip_group_check=True)
    return last


def add_sums(nc, pe, ps_sum, col, hot, val, width):
    for c in range(HALF):
        last = nc.tensor.matmul(ps_sum[:, bass.ds(col[c // PAIR], width)], hot[:, c, :], val[:, c, :],
                                start=False, stop=True, skip_group_check=True)
    return last


def take_sums(nc, name, ps_sum, out, width):
    with Stage(nc, name) as s:
        block = s.block()

        @block.vector
        def _(dve):
            for j in range(-(-NB // 7)):
                n = min(7, NB - 7 * j)
                nc.vector.tensor_copy(out[:, 7 * j:7 * j + n, 0:width],
                                      ps_sum[:, j * BANK:j * BANK + n * UC].rearrange("p (b w) -> p b w", w=UC)
                                      [:, :, 0:width])


def source_sum_pass(nc, g, out):
    with Stage(nc, "srcsum") as s:
        rows = [s.sb(f"rows{h}", [P, TURN, SROWW]) for h in range(2)]
        hot = [s.sb(f"hot{h}", [P, HALF, P]) for h in range(2)]
        ps_sum = s.ps("sum", [P, 4 * BANK])
        rows_ready = [s.sem(f"rows_ready{h}") for h in range(2)]
        hot_ready = s.sem("hot_ready")
        summed = s.sem("summed")
        src = g.sslots.rearrange("(p n) w -> p n w", p=P)

        with Stage(nc, "srcsum_block") as t:
            block = t.block()

            @block.sync
            def _(sp):
                with sp.Fori(0, (TURNS + 1) // 2) as i:
                    for h in range(2):
                        sp.wait_ge(summed, 4 * i + 2 * h + 2)
                        sp.dma_start(rows[h][:, :, :], src[:, bass.ds((2 * i + h) * TURN, TURN), :]
                                     ).then_inc(rows_ready[h], 16)

            @block.vector
            def _(dve):
                with dve.Fori(0, (TURNS + 1) // 2) as i:
                    for h in range(2):
                        dve.wait_ge(rows_ready[h], 16 * i + 16)
                        for q in range(2):
                            k = 4 * i + 2 * h + q
                            dve.wait_ge(summed, k + 3)
                            nc.vector.tensor_tensor(
                                hot[q][:, :, :], g.iota[:, :].unsqueeze(1).to_broadcast([P, HALF, P]),
                                wide(rows[h][:, q * HALF:(q + 1) * HALF, C], P), ALU.is_equal).then_inc(hot_ready, 1)

            @block.tensor
            def _(pe):
                pe.sem_inc(summed, 3)
                open_sums(nc, pe, g, ps_sum).then_inc(summed, 1)
                with pe.Fori(0, (TURNS + 1) // 2) as i:
                    for h in range(2):
                        for q in range(2):
                            k = 4 * i + 2 * h + q
                            col = two_blocks(nc, pe, g.col_src, k + 1, 12, psum_column(NB - 1))
                            pe.wait_ge(hot_ready, k + 1)
                            pe.wait_ge(rows_ready[h], 16 * i + 16)
                            add_sums(nc, pe, ps_sum, col, hot[q], rows[h][:, q * HALF:(q + 1) * HALF, 0:C], C
                                     ).then_inc(summed, 1)

        take_sums(nc, "srcsum_take", ps_sum, out, C)


def message_pass(nc, g, out):
    with Stage(nc, "message") as s:
        idx = [s.sb(f"idx{h}", [P, HALF], I32) for h in range(2)]
        row = [s.sb(f"row{h}", [P, HALF, C]) for h in range(2)]
        own = [s.sb(f"own{h}", [P, HALF, C]) for h in range(2)]
        both = [s.sb(f"both{h}", [P, HALF, C]) for h in range(2)]
        val = [s.sb(f"val{h}", [P, HALF, C]) for h in range(2)]
        hot = [s.sb(f"hot{h}", [P, HALF, P]) for h in range(2)]
        ps_sum = s.ps("sum", [P, 4 * BANK])
        opened = s.sem("opened")
        idx_ready = s.sem("idx_ready")
        gathered = [s.sem(f"gathered{h}") for h in range(2)]
        own_ready = [s.sem(f"own_ready{h}") for h in range(2)]
        both_ready = s.sem("both_ready")
        val_ready = s.sem("val_ready")
        hot_ready = s.sem("hot_ready")
        summed = s.sem("summed")

        with Stage(nc, "message_block") as t:
            block = t.block()

            @block.sync
            def _(sp):
                src = g.slots.rearrange("(p n) w -> p n w", p=P)
                with sp.Fori(0, TURNS) as i:
                    for h in range(2):
                        sp.wait_ge(both_ready, 2 * i + h + 1)
                        sp.dma_start(own[h][:, :, :], src[:, bass.ds(i * TURN + h * HALF, HALF), 0:C]
                                     ).then_inc(own_ready[h], 16)

            @block.gpsimd
            def _(pool):
                with pool.Fori(0, TURNS) as i:
                    for h in range(2):
                        pool.wait_ge(idx_ready, 2 * i + h + 1)
                        pool.sem_inc(opened, 1)
                        for c in range(HALF):
                            pool.indirect_dma_start(row[h][:, c, :], None, g.msg_table,
                                                    bass.IndirectOffsetOnAxis(ap=idx[h][:, c:c + 1], axis=0)
                                                    ).then_inc(gathered[h], 16)

            @block.vector
            def _(dve):
                dve.sem_inc(both_ready, 2)
                for h in range(2):
                    gather_idx(nc, g, idx, h, h * HALF, M_SRC).then_inc(idx_ready, 1)
                with dve.Fori(0, TURNS) as i:
                    for h in range(2):
                        k = 2 * i + h
                        at = i * TURN + h * HALF
                        dve.wait_ge(summed, k + 1)
                        one_hot(nc, g, hot[h][:, :, :], at, M_DLO).then_inc(hot_ready, 1)
                        dve.wait_ge(gathered[h], 16 * HALF * i + 16 * HALF)
                        dve.wait_ge(own_ready[h], 16 * i + 16)
                        dve.wait_ge(val_ready, k + 1)
                        nc.vector.tensor_tensor(both[h][:, :, :], row[h][:, :, :], own[h][:, :, :], ALU.add
                                                ).then_inc(both_ready, 1)
                        gather_idx(nc, g, idx, h, at + TURN, M_SRC).then_inc(idx_ready, 1)

            @block.scalar
            def _(act):
                act.sem_inc(val_ready, 2)
                with act.Fori(0, TURNS) as i:
                    for h in range(2):
                        k = 2 * i + h
                        act.wait_ge(both_ready, k + 3)
                        act.wait_ge(summed, k + 1)
                        nc.scalar.activation(val[h][:, :, :], both[h][:, :, :], ACT.Relu).then_inc(val_ready, 1)

            @block.tensor
            def _(pe):
                pe.sem_inc(summed, 1)
                open_sums(nc, pe, g, ps_sum).then_inc(summed, 1)
                with pe.Fori(0, TURNS) as i:
                    for h in range(2):
                        k = 2 * i + h
                        col = two_blocks(nc, pe, g.col_dst, k + 1, 12, psum_column(NB - 1))
                        pe.wait_ge(hot_ready, k + 1)
                        pe.wait_ge(val_ready, k + 3)
                        add_sums(nc, pe, ps_sum, col, hot[h], val[h], C).then_inc(summed, 1)

        take_sums(nc, "message_take", ps_sum, out, C)


def gat_max_pass(nc, g, l):
    with Stage(nc, f"gatmax{l}") as s:
        idx = [s.sb(f"idx{h}", [P, HALF], I32) for h in range(2)]
        row = [s.sb(f"row{h}", [P, HALF, GW]) for h in range(2)]
        score = [s.sb(f"score{h}", [P, HALF, P]) for h in range(2)]
        none = s.sb("none", [P, HALF, P])
        red = [s.sb(f"red{h}", [P, PAIR]) for h in range(2)]
        ps = [s.ps(f"t{h}", [P, HALF, P]) for h in range(2)]
        opened = s.sem("opened")
        idx_ready = s.sem("idx_ready")
        gathered = [s.sem(f"gathered{h}") for h in range(2)]
        stored = [s.sem(f"stored{h}") for h in range(2)]
        row_free = s.sem("row_free")
        drafted = s.sem("drafted")
        score_ready = s.sem("score_ready")
        turned = s.sem("turned")
        step = s.sem("step")
        block = s.block()
        to = g.gat_rows.rearrange("(p n) w -> p n w", p=P)

        @block.sync
        def _(sp):
            with sp.Fori(0, TURNS) as i:
                for h in range(2):
                    sp.wait_ge(gathered[h], 16 * HALF * i + 16 * HALF)
                    sp.dma_start(to[:, bass.ds(i * TURN + h * HALF, HALF), :], row[h][:, :, :]).then_inc(stored[h], 16)

        @block.scalar
        def _(act):
            act.sem_inc(row_free, 2)
            with act.Fori(0, TURNS) as i:
                for h in range(2):
                    act.wait_ge(stored[h], 16 * i + 16)
                    act.sem_inc(row_free, 1)

        @block.gpsimd
        def _(pool):
            with pool.Fori(0, TURNS) as i:
                for h in range(2):
                    pool.wait_ge(row_free, 2 * i + h + 1)
                    pool.wait_ge(idx_ready, 2 * i + h + 1)
                    pool.sem_inc(opened, 1)
                    for c in range(HALF):
                        pool.indirect_dma_start(row[h][:, c, :], None, g.gat_table,
                                                bass.IndirectOffsetOnAxis(ap=idx[h][:, c:c + 1], axis=0)
                                                ).then_inc(gathered[h], 16)

        @block.tensor
        def _(pe):
            pe.sem_inc(turned, 2)
            with pe.Fori(0, TURNS) as i:
                for h in range(2):
                    k = 2 * i + h
                    pe.wait_ge(score_ready, k + 1)
                    for c in range(HALF):
                        last = nc.tensor.transpose(ps[h][:, c, :], score[h][:, c, :], g.ident[:, :])
                    last.then_inc(turned, 1)

        @block.vector
        def _(dve):
            def lift(j, h, b, at):
                dve.wait_ge(step, at)
                to = g.top[:, bass.ds(b, 1)]
                nc.vector.tensor_tensor(to, to, red[h][:, j:j + 1], ALU.max).then_inc(step, 1)

            for h in range(2):
                gather_idx(nc, g, idx, h, h * HALF, M_SRC).then_inc(idx_ready, 1)
            with dve.Fori(0, TURNS) as i:
                for h in range(2):
                    k = 2 * i + h
                    at = i * TURN + h * HALF
                    b = two_blocks(nc, dve, g.blk_dst, k + 1, 5, NB - 1)
                    dve.wait_ge(gathered[h], 16 * HALF * i + 16 * HALF)
                    dve.wait_ge(turned, k + 1)
                    for c in range(HALF):
                        node = g.meta[:, bass.ds(at + c, 1), M_DLO]
                        nc.vector.tensor_scalar(score[h][:, c, :], g.iota[:, :], node, row[h][:, c, C:GW],
                                                ALU.is_equal, ALU.mult)
                        last = nc.vector.tensor_scalar(none[:, c, :], g.iota[:, :], node, -BIG,
                                                       ALU.not_equal, ALU.mult)
                    last.then_inc(drafted, 1)
                    gather_idx(nc, g, idx, h, at + TURN, M_SRC).then_inc(idx_ready, 1)
                    dve.wait_ge(drafted, k + 1)
                    nc.vector.tensor_tensor(score[h][:, :, :], score[h][:, :, :], none[:, :, :], ALU.add
                                            ).then_inc(score_ready, 1)
                    dve.wait_ge(turned, k + 3)
                    nc.vector.tensor_reduce(red[h][:, :], ps[h][:, :, :].rearrange("p (j c) e -> p j (c e)", j=PAIR),
                                            AX, ALU.max).then_inc(step, 1)
                    for j in range(PAIR):
                        lift(j, h, b[j], 3 * k + j + 1)
                    dve.wait_ge(step, 3 * k + 3)


def gat_sum_pass(nc, g, l, out):
    with Stage(nc, f"gatsum{l}") as s:
        row = [s.sb(f"row{h}", [P, HALF, GW]) for h in range(2)]
        hot_b = [s.sb(f"hot_b{h}", [P, HALF, P], BF16) for h in range(2)]
        hot_t = [s.sb(f"hot_t{h}", [P, HALF, P], BF16) for h in range(2)]
        hot = [s.sb(f"hot{h}", [P, HALF, P]) for h in range(2)]
        at_dst = s.sb("at_dst", [P, HALF, 2])
        e = s.sb("e", [P, HALF])
        e2 = s.sb("e2", [P, HALF])
        e3 = [s.sb(f"e3{h}", [P, HALF]) for h in range(2)]
        w = [s.sb(f"w{h}", [P, HALF]) for h in range(2)]
        val = [s.sb(f"val{h}", [P, HALF, GW]) for h in range(2)]
        ps_t = [s.ps(f"t{h}", [P, HALF, 2 * P], BF16) for h in range(2)]
        ps_f = [s.ps(f"f{h}", [P, HALF, P]) for h in range(2)]
        ps_sum = s.ps("sum", [P, 4 * BANK])
        row_ready = [s.sem(f"row_ready{h}") for h in range(2)]
        hot_b_ready = s.sem("hot_b_ready")
        turned = s.sem("turned")
        hot_t_ready = s.sem("hot_t_ready")
        found = s.sem("found")
        step = s.sem("step")
        e_ready = s.sem("e_ready")
        w_ready = s.sem("w_ready")
        val_ready = s.sem("val_ready")
        summed = s.sem("summed")

        with Stage(nc, f"gatsum{l}_block") as t:
            block = t.block()

            @block.sync
            def _(sp):
                src = g.gat_rows.rearrange("(p n) w -> p n w", p=P)
                with sp.Fori(0, TURNS) as i:
                    for h in range(2):
                        sp.wait_ge(val_ready, 2 * i + h + 1)
                        sp.dma_start(row[h][:, :, :], src[:, bass.ds(i * TURN + h * HALF, HALF), :]
                                     ).then_inc(row_ready[h], 16)

            @block.scalar
            def _(act):
                def take(h, k):
                    act.wait_ge(turned, k + 3)
                    act.wait_ge(found, k + 1)
                    nc.scalar.copy(hot_t[h][:, :, :], ps_t[h][:, :, 0:P]).then_inc(hot_t_ready, 1)

                act.sem_inc(hot_t_ready, 2)
                take(0, 0)
                with act.Fori(0, TURNS) as i:
                    for h in range(2):
                        k = 2 * i + h
                        take(1 - h, k + 1)
                        act.wait_ge(e_ready, k + 3)
                        act.wait_ge(val_ready, k + 1)
                        nc.scalar.activation(w[h][:, :], e3[h][:, :], ACT.Exp).then_inc(w_ready, 1)

            @block.tensor
            def _(pe):
                def find(h, k):
                    b = two_blocks(nc, pe, g.blk_dst, k + 1, 5, NB - 1)
                    pe.wait_ge(hot_b_ready, k + 1)
                    pe.wait_ge(hot_t_ready, k + 1)
                    for c in range(HALF):
                        last = nc.tensor.transpose(ps_t[h][:, c, 0:P], hot_b[h][:, c, :], g.ident_b[:, :])
                    last.then_inc(turned, 1)
                    pe.wait_ge(hot_t_ready, k + 3)
                    pe.wait_ge(e_ready, k + 1)
                    for c in range(HALF):
                        last = nc.tensor.matmul(ps_f[h][:, c, 0:6], hot_t[h][:, c, :],
                                                g.at_node[:, bass.ds(b[c // PAIR], 1), :].squeeze(1),
                                                start=True, stop=True)
                    last.then_inc(found, 1)

                pe.sem_inc(turned, 2)
                pe.sem_inc(found, 2)
                pe.sem_inc(summed, 1)
                open_sums(nc, pe, g, ps_sum).then_inc(summed, 1)
                find(0, 0)
                with pe.Fori(0, TURNS) as i:
                    for h in range(2):
                        k = 2 * i + h
                        find(1 - h, k + 1)
                        col = two_blocks(nc, pe, g.col_dst, k + 1, 12, psum_column(NB - 1))
                        pe.wait_ge(val_ready, k + 3)
                        add_sums(nc, pe, ps_sum, col, hot[h], val[h], GW).then_inc(summed, 1)

            @block.vector
            def _(dve):
                def hots(h, at, k):
                    dve.wait_ge(turned, k + 1)
                    one_hot(nc, g, hot_b[h][:, :, :], at, M_DLO).then_inc(hot_b_ready, 1)

                dve.sem_inc(val_ready, 2)
                dve.sem_inc(e_ready, 2)
                hots(0, 0, 0)
                with dve.Fori(0, TURNS) as i:
                    for h in range(2):
                        k = 2 * i + h
                        at = i * TURN + h * HALF
                        hots(1 - h, at + HALF, k + 1)
                        dve.wait_ge(found, k + 3)
                        dve.wait_ge(row_ready[h], 16 * i + 16)
                        nc.vector.tensor_reduce(at_dst[:, :, :], ps_f[h][:, :, 0:6].rearrange("p c (q s) -> p c q s", s=3),
                                                AX, ALU.add).then_inc(step, 1)
                        dve.wait_ge(step, 4 * k + 1)
                        nc.vector.tensor_tensor(e[:, :], row[h][:, :, C], at_dst[:, :, 0], ALU.add).then_inc(step, 1)
                        dve.wait_ge(step, 4 * k + 2)
                        nc.vector.scalar_tensor_tensor(e2[:, :], e[:, :], 0.2, e[:, :], ALU.mult, ALU.max).then_inc(step, 1)
                        dve.wait_ge(step, 4 * k + 3)
                        nc.vector.tensor_tensor(e[:, :], e2[:, :], at_dst[:, :, 1], ALU.subtract).then_inc(step, 1)
                        dve.wait_ge(step, 4 * k + 4)
                        nc.vector.tensor_scalar(e3[h][:, :], e[:, :], 0.0, None, ALU.min).then_inc(e_ready, 1)
                        dve.wait_ge(summed, k + 1)
                        one_hot(nc, g, hot[h][:, :, :], at, M_DLO)
                        dve.wait_ge(w_ready, k + 1)
                        nc.vector.tensor_tensor(val[h][:, :, 0:C], row[h][:, :, 0:C], wide(w[h][:, :], C), ALU.mult)
                        nc.vector.tensor_copy(val[h][:, :, C], w[h][:, :]).then_inc(val_ready, 1)

        take_sums(nc, f"gatsum{l}_take", ps_sum, out, GW)


def weighted_layer(nc, g):
    weigh_pass(nc, g)
    with Stage(nc, "wsum") as s:
        agg = s.sb("agg", [P, NB, C])
        source_sum_pass(nc, g, agg)
        node_product(nc, g, "wproj", agg, C, g.w_agg, [(0, C, g.h)])
        norm = s.sb("norm", [P, NB])
        step = s.sem("step")
        square = s.sem("square")
        root = s.sem("root")
        block = s.block()

        @block.scalar
        def _(act):
            act.wait_ge(square, 1)
            nc.scalar.activation(norm[:, :], norm[:, :], ACT.Sqrt).then_inc(root, 1)

        @block.vector
        def _(dve):
            link = chain(dve, step)
            link(nc.vector.tensor_tensor(g.h[:, :, :], g.h[:, :, :], g.b_agg.unsqueeze(1).to_broadcast([P, NB, C]),
                                         ALU.add))
            link(nc.vector.tensor_tensor(agg[:, :, :], g.h[:, :, :], g.h[:, :, :], ALU.mult))
            nc.vector.tensor_reduce(norm[:, :], agg[:, :, :], AX, ALU.add).then_inc(square, 1)
            dve.wait_ge(root, 1)
            link(nc.vector.tensor_scalar(norm[:, :], norm[:, :], 1e-12, None, ALU.max))
            link(nc.vector.reciprocal(norm[:, :], norm[:, :]))
            link(nc.vector.tensor_tensor(g.h[:, :, :], g.h[:, :, :], wide(norm[:, :], C), ALU.mult))


def store_table(nc, name, table, rows):
    with Stage(nc, name) as s:
        stored = s.sem("stored")
        block = s.block()

        @block.sync
        def _(sp):
            sp.dma_start(table.rearrange("(b p) w -> p b w", p=P), rows[:, :, :]).then_inc(stored, 16)
            sp.wait_ge(stored, 16)


def message_layer(nc, g):
    with Stage(nc, "msg") as s:
        pair = s.sb("pair", [P, NB, 2 * C])
        node_product(nc, g, "msgp", g.h, C, g.w_msg_node, [(0, C, pair[:, :, 0:C])])
        store_table(nc, "msgt", g.msg_table, pair[:, :, 0:C])
        message_pass(nc, g, pair[:, :, C:2 * C])
        with Stage(nc, "msgpair") as t:
            block = t.block()

            @block.vector
            def _(dve):
                nc.vector.tensor_copy(pair[:, :, 0:C], g.h[:, :, :])
        node_product(nc, g, "msgu", pair, 2 * C, g.w_upd, [(0, C, g.h)])
        step = s.sem("step")
        block = s.block()

        @block.vector
        def _(dve):
            link = chain(dve, step)
            link(nc.vector.tensor_tensor(g.h[:, :, :], g.h[:, :, :], g.b_upd.unsqueeze(1).to_broadcast([P, NB, C]),
                                         ALU.add))
            link(nc.vector.tensor_scalar(g.h[:, :, :], g.h[:, :, :], 0.0, None, ALU.max))


def gat_layer(nc, g, l):
    with Stage(nc, f"gat{l}") as s:
        table = s.sb("table", [P, NB, GW])
        tmp = s.sb("tmp", [P, NB, C])
        both = s.sb("both", [P, 2, NB])
        self_e = s.sb("self_e", [P, NB])
        g.top = s.sb("top", [P, NB])
        g.at_node = s.sb("at_node", [P, NB, 6], BF16)
        split = s.sb("split", [P, 3, 2, NB], BF16)
        agg = s.sb("agg", [P, NB, GW])
        node_product(nc, g, f"gatp{l}", g.h, C, g.w_gat[l], [(0, C, table[:, :, 0:C])])
        with Stage(nc, f"gatscore{l}") as t:
            step = t.sem("step")
            block = t.block()

            @block.vector
            def _(dve):
                link = chain(dve, step)
                for a, to in ((g.a_src[l], table[:, :, C]), (g.a_dst[l], both[:, 0, :])):
                    link(nc.vector.tensor_tensor(tmp[:, :, :], table[:, :, 0:C], a.unsqueeze(1).to_broadcast([P, NB, C]),
                                                 ALU.mult))
                    link(nc.vector.tensor_reduce(to, tmp[:, :, :], AX, ALU.add))
                link(nc.vector.tensor_copy(g.top[:, :], table[:, :, C]))
        store_table(nc, f"gatt{l}", g.gat_table, table)
        gat_max_pass(nc, g, l)
        with Stage(nc, f"gattop{l}") as t:
            step = t.sem("step")
            block = t.block()

            @block.vector
            def _(dve):
                link = chain(dve, step)

                def leaky(to, a, b):
                    link(nc.vector.tensor_tensor(tmp[:, :, 0], a, b, ALU.add))
                    link(nc.vector.scalar_tensor_tensor(to, tmp[:, :, 0], 0.2, tmp[:, :, 0], ALU.mult, ALU.max))
                leaky(both[:, 1, :], g.top[:, :], both[:, 0, :])
                leaky(self_e[:, :], table[:, :, C], both[:, 0, :])
        split_rows(nc, g, f"gatsplit{l}", both, split)
        with Stage(nc, f"gatorder{l}") as t:
            exp_in = t.sem("exp_in")
            block = t.block()

            @block.vector
            def _(dve):
                nc.vector.tensor_copy(g.at_node[:, :, :].rearrange("p b (q s) -> p b q s", s=3),
                                      split[:, :, :, :].rearrange("p s q b -> p b q s"))
                nc.vector.tensor_tensor(self_e[:, :], self_e[:, :], both[:, 1, :], ALU.subtract).then_inc(exp_in, 1)

            @block.scalar
            def _(act):
                act.wait_ge(exp_in, 1)
                nc.scalar.activation(self_e[:, :], self_e[:, :], ACT.Exp)
        gat_sum_pass(nc, g, l, agg)
        step = s.sem("step")
        block = s.block()

        @block.vector
        def _(dve):
            link = chain(dve, step)
            link(nc.vector.tensor_tensor(tmp[:, :, :], table[:, :, 0:C], wide(self_e[:, :], C), ALU.mult))
            link(nc.vector.tensor_tensor(agg[:, :, 0:C], agg[:, :, 0:C], tmp[:, :, :], ALU.add))
            link(nc.vector.tensor_tensor(self_e[:, :], self_e[:, :], agg[:, :, C], ALU.add))
            link(nc.vector.tensor_scalar(self_e[:, :], self_e[:, :], 1e-16, None, ALU.add))
            link(nc.vector.reciprocal(self_e[:, :], self_e[:, :]))
            link(nc.vector.tensor_tensor(g.h[:, :, :], agg[:, :, 0:C], wide(self_e[:, :], C), ALU.mult))
            link(nc.vector.tensor_tensor(g.h[:, :, :], g.h[:, :, :], g.b_gat[l].unsqueeze(1).to_broadcast([P, NB, C]),
                                         ALU.add))
            if l == 0:
                link(nc.vector.tensor_scalar(g.h[:, :, :], g.h[:, :, :], 0.0, None, ALU.max))



class Held:
    pass


NVEC = 2 * 3 + 8 + 1
(V_SEMW, V_LNG, V_LNB, V_AGGB, V_MSGB, V_UPDB, V_GATB, V_ASRC, V_ADST) = (0, 2, 4, 6, 7, 8, 9, 11, 13)


def build(nc, d, out, stop=None):
    g = Held()
    ctx = ExitStack()
    with ctx:
        def sb(name, shape, dt=F32):
            return ctx.enter_context(nc.sbuf_tensor(name, shape, dt))

        g.x = sb("x", [P, NB, C])
        g.h = sb("h", [P, NB, C])
        g.own = sb("own", [P, NB, C])
        g.meta = sb("meta", [P, CP, META])
        g.blk_dst = sb("blk_dst", [1, 1 + NPK], I32)
        g.col_dst = sb("col_dst", [1, 1 + NPK], I32)
        g.blk_src = sb("blk_src", [1, 1 + NPK], I32)
        g.col_src = sb("col_src", [1, 1 + NPK], I32)
        g.ident = sb("ident", [P, P])
        g.iota = sb("iota", [P, P])
        g.before = sb("before", [P, P])
        g.no_node = sb("no_node", [P, 1])
        g.ident_b = sb("ident_b", [P, P], BF16)
        g.zeros = sb("zeros", [P, BANK])
        g.ones = sb("ones", [P, P])
        g.pair_slot = sb("pair_slot", [NB, CP // PAIR])
        g.w_rel_t = sb("w_rel_t", [C, 2, R * (TW + C) + C])
        g.w_cat_t = sb("w_cat_t", [P, 4, P])
        g.vec = sb("vec", [P, NVEC, C])
        g.sem_b = sb("sem_b", [P, 2])
        g.w_agg = sb("w_agg", [C, C])
        g.w_msg_edge = sb("w_msg_edge", [C, C])
        g.w_msg_node = sb("w_msg_node", [C, C])
        g.w_upd = sb("w_upd", [2 * C, C])
        g.w_gat_t = sb("w_gat_t", [C, 2, C])
        g.w_rel = [g.w_rel_t[:, l, :] for l in range(2)]
        g.w_cat = [[g.w_cat_t[:, 2 * l + j, :] for j in range(2)] for l in range(2)]
        g.w_gat = [g.w_gat_t[:, l, :] for l in range(2)]
        vec = lambda i: g.vec[:, i, :]
        g.sem_w = [vec(V_SEMW + l) for l in range(2)]
        g.ln_g = [vec(V_LNG + l) for l in range(2)]
        g.ln_b = [vec(V_LNB + l) for l in range(2)]
        g.b_agg, g.b_msg, g.b_upd = vec(V_AGGB), vec(V_MSGB), vec(V_UPDB)
        g.b_gat = [vec(V_GATB + l) for l in range(2)]
        g.a_src = [vec(V_ASRC + l) for l in range(2)]
        g.a_dst = [vec(V_ADST + l) for l in range(2)]
        dram = lambda name, shape: nc.dram_tensor(name, shape, F32).ap()
        g.slots = dram("slots", [ROWS, ROWW])
        g.sslots = dram("sslots", [ROWS, SROWW])
        g.rel_table = dram("rel_table", [R * NPAD, TW])
        g.msg_table = dram("msg_table", [NPAD, C])
        g.gat_table = dram("gat_table", [NPAD, GW])
        g.gat_rows = dram("gat_rows", [ROWS, GW])
        g.attr = d["attr"]

        with ExitStack() as routing:
            def tmp(name, shape, dt=F32):
                return routing.enter_context(nc.sbuf_tensor(name, shape, dt))
            g.src_i = tmp("src_i", [P, EC], I32)
            g.dst_i = tmp("dst_i", [P, EC], I32)
            g.typ_i = tmp("typ_i", [P, EC], I32)
            g.weight0 = tmp("weight0", [P, EC])
            g.absent = tmp("absent", [P, EC])
            g.meta0 = tmp("meta0", [P, EC, META])
            g.row0 = tmp("row0", [P, EC], I32)
            g.fill = tmp("fill", [P, TURN, ROWW])
            g.sfill = tmp("sfill", [P, TURN, SROWW])
            load_constants(nc, g, [
                (g.src_i[:, :], d["src"]), (g.dst_i[:, :], d["dst"]), (g.typ_i[:, :], d["typ"]),
                (g.absent[:, :], d["absent"]), (g.weight0[:, :], d["weight"]), (g.iota[:, :], d["iota"]),
                (g.before[:, :], d["before"]), (g.ident[:, :], d["ident"]), (g.pair_slot[:, :], d["pair_slot"]),
                (g.x[:, :, :], d["x"].rearrange("(b p) c -> p b c", p=P)),
                (g.h[:, :, :], d["x"].rearrange("(b p) c -> p b c", p=P)),
                (g.no_node[:, :], d["no_node"]), (g.w_rel_t[:, :, :], d["w_rel"]), (g.w_cat_t[:, :, :], d["w_cat"]),
                (g.vec[:, :, :], d["vectors"]), (g.sem_b[:, :], d["sem_b"]), (g.w_agg[:, :], d["w_agg"]),
                (g.w_msg_edge[:, :], d["w_msg_edge"]), (g.w_msg_node[:, :], d["w_msg_node"]),
                (g.w_upd[:, :], d["w_upd"]), (g.w_gat_t[:, :, :], d["w_gat"])])
            fill_tables(nc, g)
            route(nc, g)
            scatter_edges(nc, g)
        if stop == "scatter":
            return finish(nc, g, out, g.x)
        with ExitStack() as relations:
            def tmp(name, shape, dt=F32):
                return relations.enter_context(nc.sbuf_tensor(name, shape, dt))
            g.mask = tmp("mask", [P, CP, R])
            g.q_split = tmp("q_split", [P, 3, NB, R * C], BF16)
            load_meta(nc, g)
            for l in range(2):
                relation_products(nc, g, l)
                with nc.sbuf_tensor(f"acc{l}", [P, NB, R * C + R * H], F32) as acc:
                    g.acc = acc
                    relation_pass(nc, g, l)
                    relation_nodes(nc, g, l)
                if stop == f"rel{l}":
                    return finish(nc, g, out, g.h)
            residual_norm(nc, g, "res0")
        if stop == "res0":
            return finish(nc, g, out, g.x)
        weighted_layer(nc, g)
        residual_norm(nc, g, "res1")
        if stop == "res1":
            return finish(nc, g, out, g.x)
        message_layer(nc, g)
        residual_norm(nc, g, "res2")
        if stop == "res2":
            return finish(nc, g, out, g.x)
        for l in range(2):
            gat_layer(nc, g, l)
        residual_norm(nc, g, "res3")
        finish(nc, g, out, g.x)


def finish(nc, g, out, what):
    with Stage(nc, "store") as s:
        stored = s.sem("stored")
        block = s.block()

        @block.sync
        def _(sp):
            full = (NB - 1) * P
            sp.dma_start(out[0:full, :].rearrange("(b p) c -> p b c", p=P), what[:, 0:NB - 1, :]).then_inc(stored, 16)
            sp.dma_start(out[full:N, :], what[0:LAST, NB - 1, :]).then_inc(stored, 16)
            sp.wait_ge(stored, 32)


STOP = None


def kernel(**inputs):
    import numpy as np
    from concourse import bacc
    from concourse.bass_utils import run_bass_kernel_spmd

    a = {k: np.asarray(v) for k, v in inputs.items()}
    f = np.float32

    def lanes(v):
        o = np.zeros(P * EC, v.dtype)
        o[:E] = v
        return o.reshape(P, EC)

    attr = np.zeros((P * EC, C), f)
    attr[:E] = a["edge_attr_64"]
    x = np.zeros((NPAD, C), f)
    x[:N] = a["x"]
    w_rel = np.zeros((C, 2, R * (TW + C) + C), f)
    w_cat = np.zeros((P, 4, P), f)
    for l in range(2):
        cols = lambda w, r: a[w][l, r].transpose(1, 0, 2).reshape(C, C)
        for r in range(R):
            w_rel[:, l, r * TW:r * TW + C] = cols("L0_gnn_W_K", r)
            w_rel[:, l, r * TW + C:(r + 1) * TW] = cols("L0_gnn_W_V", r)
            w_rel[:, l, R * TW + r * C:R * TW + (r + 1) * C] = cols("L0_gnn_W_Q", r)
            j, k = divmod(r, 2)
            w_cat[k * C:(k + 1) * C, 2 * l + j, k * C:(k + 1) * C] = a["L0_gnn_W_concat"][l, r]
        w_rel[:, l, R * (TW + C):] = a["L0_gnn_W_self"][l]
    vectors = [a["L0_gnn_sem_w"][0], a["L0_gnn_sem_w"][1], a["L0_gnn_ln_g"][0], a["L0_gnn_ln_g"][1],
               a["L0_gnn_ln_b"][0], a["L0_gnn_ln_b"][1], a["L1_gnn_bias"], a["L2_gnn_M_b"], a["L2_gnn_U_b"],
               a["L3_gnn_b1"], a["L3_gnn_b2"], a["L3_gnn_a_src1"], a["L3_gnn_a_src2"], a["L3_gnn_a_dst1"],
               a["L3_gnn_a_dst2"]]
    order = np.arange(P)
    arrays = {
        "x": x, "src": lanes(a["src"]), "dst": lanes(a["dst"]), "typ": lanes(a["edge_type_4"]),
        "weight": lanes(a["edge_weight"]),
        "attr": np.ascontiguousarray(attr.reshape(P, EC, C).transpose(2, 1, 0)).reshape(C, EC * P),
        "absent": (np.arange(P * EC) >= E).astype(f).reshape(P, EC),
        "no_node": np.where(order >= LAST, -BIG, 0.0).astype(f)[:, None],
        "ident": np.eye(P, dtype=f), "iota": np.broadcast_to(order.astype(f), (P, P)).copy(),
        "before": (order[:, None] < order[None, :]).astype(f),
        "pair_slot": np.broadcast_to(np.arange(CP // PAIR, dtype=f) * (PAIR * P), (NB, CP // PAIR)).copy(),
        "w_rel": w_rel, "w_cat": w_cat,
        "vectors": np.ascontiguousarray(np.broadcast_to(np.stack(vectors), (P, NVEC, C))),
        "sem_b": np.ascontiguousarray(np.broadcast_to(a["L0_gnn_sem_b"], (P, 2))),
        "w_agg": a["L1_gnn_weight"],
        "w_msg_node": np.ascontiguousarray(a["L2_gnn_M_W"][:, :C].T),
        "w_msg_edge": np.ascontiguousarray(a["L2_gnn_M_W"][:, C:].T),
        "w_upd": np.ascontiguousarray(a["L2_gnn_U_W"].T),
        "w_gat": np.ascontiguousarray(np.stack([a["L3_gnn_W1"], a["L3_gnn_W2"]], axis=1)),
    }
    nc = bacc.Bacc("TRN2", target_bir_lowering=False, num_devices=1)
    d = {k: nc.dram_tensor(f"in_{k}", v.shape, mybir.dt.from_np(v.dtype), kind="ExternalInput").ap()
         for k, v in arrays.items()}
    out = nc.dram_tensor("out_x", (N, C), F32, kind="ExternalOutput").ap()
    build(nc, d, out, STOP)
    r = run_bass_kernel_spmd(nc, [{f"in_{k}": v for k, v in arrays.items()}], core_ids=[0])
    return r.results[0]["out_x"]
```

```python
from contextlib import ExitStack

import concourse.bass as bass
from concourse import mybir

P = 128
N = 3125
NB = -(-N // P)
NPAD = NB * P
LAST = N - (NB - 1) * P
E = 103125
C = 64
R = 4
H = 8
D = C // H
EC = 808
HALF = 4
DEPTH = 4
TURN = DEPTH * HALF
ETURN = 2 * HALF
PAIR = 2
PAIRS = (E - NB) // (PAIR * P) + NB
NC = -(-PAIRS * PAIR // TURN) * TURN
TURNS = NC // TURN
CP = NC + TURN
NPK = CP // HALF
ROWS = P * CP
META = 8
ROWW = C + META
(M_REL, M_SRC, M_DLO, M_TYPE, M_WEIGHT, M_SROW, M_SLO, M_SPARE) = range(META)
NOWHERE = 1 << 20
NOBODY = 200.0
SROWW = C + 1
TW = 2 * C
GW = C + 2
UC = C * 0 + 73
BANK = 512
BIG = 1.0e30
assert P * EC >= E and EC % ETURN == 0 and NPAD >= N

F32 = mybir.dt.float32
BF16 = mybir.dt.bfloat16
I32 = mybir.dt.int32
ALU = mybir.AluOpType
ACT = mybir.ActivationFunctionType
AX = mybir.AxisListType.X
IN_RANGE = "worked out on the chip from 25 blocks, so it is below that"


def psum_column(b):
    return b // 7 * BANK + b % 7 * UC


class Stage:

    def __init__(self, nc, name):
        self.nc, self.name, self.ctx, self.sems = nc, name, ExitStack(), []

    def __enter__(self):
        self.ctx.__enter__()
        return self

    def __exit__(self, *a):
        said = self.ctx.__exit__(*a)
        if self.sems and a[0] is None:
            self.nc.clear_and_free_semaphores(self.sems)
            self.nc.all_engine_barrier()
        return said

    def sb(self, name, shape, dt=F32):
        return self.ctx.enter_context(self.nc.sbuf_tensor(f"{self.name}_{name}", shape, dt))

    def ps(self, name, shape, dt=F32):
        return self.ctx.enter_context(self.nc.psum_tensor(f"{self.name}_ps_{name}", shape, dt))

    def sem(self, name):
        self.sems.append(self.nc.alloc_semaphore(f"{self.name}_sem_{name}"))
        return self.sems[-1]

    def block(self):
        return self.ctx.enter_context(self.nc.Block())


def chain(engine, sem):
    count = [0]

    def link(instruction):
        count[0] += 1
        instruction.then_inc(sem, 1)
        engine.wait_ge(sem, count[0])
    return link


def wide(ap, n):
    return ap.unsqueeze(len(ap.shape)).to_broadcast([*ap.shape, n])


def load_constants(nc, g, src):
    with Stage(nc, "load") as s:
        loaded = s.sem("loaded")
        block = s.block()

        @block.sync
        def _(sp):
            n = 0
            for to, of in src:
                sp.dma_start(to, of).then_inc(loaded, 16)
                n += 16
            sp.wait_ge(loaded, n)

        @block.vector
        def _(dve):
            nc.vector.memset(g.ones[:, :], 1.0)
            nc.vector.memset(g.zeros[:, :], 0.0)
            nc.vector.memset(g.fill[:, :, :], 0.0)


def fill_tables(nc, g):
    with Stage(nc, "fill") as s:
        block = s.block()

        @block.vector
        def _(dve):
            nc.vector.memset(g.fill[:, :, C + M_DLO:C + M_DLO + 1], NOBODY)
            nc.vector.memset(g.fill[:, :, C + M_SLO:C + M_SLO + 1], NOBODY)
            nc.vector.memset(g.fill[:, :, C + M_SROW:C + M_SROW + 1].bitcast(I32), NOWHERE)
            nc.vector.memset(g.sfill[:, :, 0:C], 0.0)
            nc.vector.memset(g.sfill[:, :, C:C + 1], NOBODY)
            nc.vector.tensor_copy(g.ident_b[:, :], g.ident[:, :])
            nc.vector.tensor_copy(g.iota_b[:, :], g.iota[:, :])


def route(nc, g):
    with Stage(nc, "route") as s:
        hi_i = s.sb("hi_i", [P, EC], I32)
        hi = s.sb("hi", [P, EC])
        lo_i = s.sb("lo_i", [P, EC], I32)
        eq = s.sb("eq", [P, EC])
        cum = s.sb("cum", [P, EC])
        hit = s.sb("hit", [P, EC])
        rank = s.sb("rank", [P, EC])
        ones = s.sb("ones", [P, EC])
        cnt = s.sb("cnt", [P, 32])
        base = s.sb("base", [P, 32])
        padded = s.sb("padded", [NB, 1])
        padded_i = s.sb("padded_i", [NB, 1], I32)
        start = s.sb("start", [NB, 1])
        diag = s.sb("diag", [NB, NB])
        begun = s.sb("begun", [NB, CP // PAIR])
        blk = s.sb("blk", [1, CP // PAIR])
        bank_no = s.sb("bank_no", [1, CP // PAIR])
        col = s.sb("col", [1, CP // PAIR])
        ps_tot = s.ps("tot", [NB, 1])
        ps_start = s.ps("start", [NB, 1])
        ps_base = s.ps("base", [P, NB])
        ps_blk = s.ps("blk", [1, CP // PAIR])
        filled = s.sem("filled")
        step = s.sem("step")
        loop = [s.sem(f"loop{j}") for j in range(4)]
        counted = s.sem("counted")
        totals = s.sem("totals")
        rounded = s.sem("rounded")
        started = s.sem("started")
        diagonal = s.sem("diagonal")
        based = s.sem("based")
        begun_ready = s.sem("begun_ready")
        blocks = s.sem("blocks")
        block = s.block()

        @block.sync
        def _(sp):
            n = CP // TURN
            sp.dma_start(g.slots.rearrange("(p n u) w -> p n (u w)", p=P, n=n),
                         g.fill[:, :, :].rearrange("p u w -> p (u w)").unsqueeze(1)
                         .to_broadcast([P, n, TURN * ROWW])).then_inc(filled, 16)
            sp.dma_start(g.sslots.rearrange("(p n u) w -> p n (u w)", p=P, n=n),
                         g.sfill[:, :, :].rearrange("p u w -> p (u w)").unsqueeze(1)
                         .to_broadcast([P, n, TURN * SROWW])).then_inc(filled, 16)
            sp.wait_ge(filled, 32)

        @block.tensor
        def _(pe):
            for k in range(2):
                pe.wait_ge(counted, k + 1)
                nc.tensor.matmul(ps_tot[:, :], cnt[:, 0:NB], g.ones[:, 0:1],
                                 start=True, stop=True).then_inc(totals, 1)
                pe.wait_ge(rounded, k + 1)
                nc.tensor.matmul(ps_start[:, :], g.before[0:NB, 0:NB], padded[:, :],
                                 start=True, stop=True).then_inc(started, 1)
                pe.wait_ge(diagonal, k + 1)
                nc.tensor.matmul(ps_base[:, :], g.before[:, :], cnt[:, 0:NB], start=True, stop=False)
                nc.tensor.matmul(ps_base[:, :], g.ones[0:NB, :], diag[:, :],
                                 start=False, stop=True).then_inc(based, 1)
                pe.wait_ge(begun_ready, k + 1)
                nc.tensor.matmul(ps_blk[:, :], g.ones[0:NB, 0:1], begun[:, :],
                                 start=True, stop=True).then_inc(blocks, 1)

        @block.vector
        def _(dve):
            link = chain(dve, step)
            link(nc.vector.memset(ones[:, :], 1.0))
            plan = [(g.dst_i, g.blk_dst, g.col_dst, M_DLO, None), (g.src_i, g.blk_src, g.col_src, M_SLO, M_SROW)]
            for k, (key, blk_out, col_out, m_lo, m_row) in enumerate(plan):
                link(nc.vector.tensor_scalar(hi_i[:, :], key[:, :], 7, None, ALU.logical_shift_right))
                link(nc.vector.tensor_copy(hi[:, :], hi_i[:, :]))
                link(nc.vector.scalar_tensor_tensor(hi[:, :], g.absent[:, :], 100.0, hi[:, :], ALU.mult, ALU.add))
                link(nc.vector.tensor_scalar(lo_i[:, :], key[:, :], P - 1, None, ALU.bitwise_and))
                link(nc.vector.tensor_copy(g.meta0[:, :, m_lo], lo_i[:, :]))
                link(nc.vector.memset(rank[:, :], 0.0))
                with dve.Fori(0, NB) as b:
                    at = b + k * NB
                    nc.vector.tensor_scalar(eq[:, :], hi[:, :], g.iota[:, bass.ds(b, 1)], None,
                                            ALU.is_equal).then_inc(loop[0], 1)
                    dve.wait_ge(loop[0], at + 1)
                    nc.vector.tensor_tensor_scan(cum[:, :], ones[:, :], eq[:, :], 0.0,
                                                 ALU.mult, ALU.add).then_inc(loop[1], 1)
                    dve.wait_ge(loop[1], at + 1)
                    nc.vector.scalar_tensor_tensor(hit[:, :], cum[:, :], -1.0, eq[:, :],
                                                   ALU.add, ALU.mult).then_inc(loop[2], 1)
                    nc.vector.tensor_copy(cnt[:, bass.ds(b, 1)], cum[:, EC - 1:EC])
                    dve.wait_ge(loop[2], b + 2 * k * NB + 1)
                    nc.vector.tensor_tensor(rank[:, :], rank[:, :], hit[:, :], ALU.add).then_inc(loop[3], 1)
                    dve.wait_ge(loop[3], b + 2 * k * NB + 1)
                dve.engine_nop().then_inc(counted, 1)
                dve.wait_ge(totals, k + 1)
                link(nc.vector.tensor_scalar(padded_i[:, :], ps_tot[:, :], float(PAIR * P - 1), None, ALU.add))
                link(nc.vector.tensor_scalar(padded_i[:, :], padded_i[:, :], 8, 8,
                                             ALU.logical_shift_right, ALU.logical_shift_left))
                nc.vector.tensor_copy(padded[:, :], padded_i[:, :]).then_inc(rounded, 1)
                dve.wait_ge(started, k + 1)
                link(nc.vector.tensor_copy(start[:, :], ps_start[:, :]))
                nc.vector.tensor_scalar(diag[:, :], g.ident[0:NB, 0:NB], start[:, 0:1], None,
                                        ALU.mult).then_inc(diagonal, 1)
                nc.vector.tensor_scalar(begun[:, :], g.pair_slot[:, :], start[:, 0:1], None,
                                        ALU.is_ge).then_inc(begun_ready, 1)
                dve.wait_ge(based, k + 1)
                link(nc.vector.tensor_copy(base[:, 0:NB], ps_base[:, :]))
                with dve.Fori(0, NB) as b:
                    nc.vector.tensor_scalar(hit[:, :], hi[:, :], g.iota[:, bass.ds(b, 1)], base[:, bass.ds(b, 1)],
                                            ALU.is_equal, ALU.mult).then_inc(loop[2], 1)
                    dve.wait_ge(loop[2], b + (2 * k + 1) * NB + 1)
                    nc.vector.tensor_tensor(rank[:, :], rank[:, :], hit[:, :], ALU.add).then_inc(loop[3], 1)
                    dve.wait_ge(loop[3], b + (2 * k + 1) * NB + 1)
                link(nc.vector.tensor_copy(hi_i[:, :], rank[:, :]))
                link(nc.vector.tensor_scalar(lo_i[:, :], hi_i[:, :], P - 1, None, ALU.bitwise_and))
                link(nc.vector.tensor_scalar(hi_i[:, :], hi_i[:, :], 7, None, ALU.logical_shift_right))
                link(nc.vector.tensor_copy(eq[:, :], lo_i[:, :]))
                link(nc.vector.tensor_copy(cum[:, :], hi_i[:, :]))
                link(nc.vector.scalar_tensor_tensor(hit[:, :], eq[:, :], float(CP), cum[:, :], ALU.mult, ALU.add))
                to = g.row0[:, :] if m_row is None else g.meta0[:, :, m_row].bitcast(I32)
                link(nc.vector.scalar_tensor_tensor(to, g.absent[:, :], float(NOWHERE), hit[:, :], ALU.mult, ALU.add))
                dve.wait_ge(blocks, k + 1)
                link(nc.vector.tensor_scalar(blk[:, :], ps_blk[:, :], -1.0, None, ALU.add))
                link(nc.vector.tensor_scalar(bank_no[:, :], blk[:, :], 7.0, None, ALU.is_ge))
                for edge in (14.0, 21.0):
                    link(nc.vector.scalar_tensor_tensor(bank_no[:, :], blk[:, :], edge, bank_no[:, :], ALU.is_ge, ALU.add))
                link(nc.vector.tensor_scalar(bank_no[:, :], bank_no[:, :], float(BANK - 7 * UC), None, ALU.mult))
                link(nc.vector.scalar_tensor_tensor(col[:, :], blk[:, :], float(UC), bank_no[:, :], ALU.mult, ALU.add))
                for of, to, shift in ((blk, blk_out, 5), (col, col_out, 12)):
                    two = of[:, :].rearrange("a (h j) -> a h j", j=PAIR)
                    link(nc.vector.memset(to[:, 0:1], 0))
                    link(nc.vector.scalar_tensor_tensor(to[:, 1:1 + NPK], two[:, :, 1], float(1 << shift), two[:, :, 0],
                                                        ALU.mult, ALU.add))
            link(nc.vector.tensor_copy(eq[:, :], g.typ_i[:, :]))
            link(nc.vector.tensor_copy(g.meta0[:, :, M_TYPE], eq[:, :]))
            link(nc.vector.tensor_copy(cum[:, :], g.src_i[:, :]))
            link(nc.vector.scalar_tensor_tensor(g.meta0[:, :, M_REL].bitcast(I32), eq[:, :], float(NPAD), cum[:, :],
                                                ALU.mult, ALU.add))
            link(nc.vector.tensor_copy(g.meta0[:, :, M_SRC].bitcast(I32), cum[:, :]))
            link(nc.vector.tensor_copy(g.meta0[:, :, M_WEIGHT], g.weight0[:, :]))
            link(nc.vector.memset(g.meta0[:, :, M_SPARE:M_SPARE + 1], 0.0))


def scatter_edges(nc, g):
    with Stage(nc, "scatter") as s:
        chan = [s.sb(f"chan{h}", [C, HALF * P]) for h in range(2)]
        row = [s.sb(f"row{h}", [P, HALF, ROWW]) for h in range(2)]
        to = [s.sb(f"to{h}", [P, HALF], I32) for h in range(2)]
        ps = [s.ps(f"msg{h}", [P, HALF, C]) for h in range(2)]
        chan_ready = [s.sem(f"chan_ready{h}") for h in range(2)]
        msg_ready = s.sem("msg_ready")
        row_ready = s.sem("row_ready")
        scattered = [s.sem(f"scattered{h}") for h in range(2)]
        row_free = s.sem("row_free")
        opened = s.sem("opened")
        block = s.block()

        @block.sync
        def _(sp):
            sp.sem_inc(row_free, 2)
            with sp.Fori(0, EC // ETURN) as i:
                for h in range(2):
                    sp.wait_ge(msg_ready, 2 * i + h + 1)
                    sp.dma_start(chan[h][:, :], g.attr[:, bass.ds(i * (ETURN * P) + h * HALF * P, HALF * P)]
                                 ).then_inc(chan_ready[h], 16)

        @block.scalar
        def _(act):
            with act.Fori(0, EC // ETURN) as i:
                for h in range(2):
                    act.wait_ge(scattered[h], 16 * HALF * i + 16 * HALF)
                    act.sem_inc(row_free, 1)

        @block.tensor
        def _(pe):
            pe.sem_inc(msg_ready, 2)
            with pe.Fori(0, EC // ETURN) as i:
                for h in range(2):
                    pe.wait_ge(chan_ready[h], 16 * i + 16)
                    pe.wait_ge(row_ready, 2 * i + h + 1)
                    for c in range(HALF):
                        last = nc.tensor.matmul(ps[h][:, c, :], chan[h][:, c * P:(c + 1) * P], g.w_msg_edge[:, :],
                                                start=True, stop=True)
                    last.then_inc(msg_ready, 1)

        @block.vector
        def _(dve):
            dve.sem_inc(row_ready, 2)
            with dve.Fori(0, EC // ETURN) as i:
                for h in range(2):
                    k = 2 * i + h
                    at = i * ETURN + h * HALF
                    dve.wait_ge(msg_ready, k + 3)
                    dve.wait_ge(row_free, k + 1)
                    nc.vector.tensor_tensor(row[h][:, :, 0:C], ps[h][:, :, :],
                                            g.b_msg[:, :].unsqueeze(1).to_broadcast([P, HALF, C]), ALU.add)
                    nc.vector.tensor_copy(row[h][:, :, C:ROWW], g.meta0[:, bass.ds(at, HALF), :])
                    nc.vector.tensor_copy(to[h][:, :], g.row0[:, bass.ds(at, HALF)]).then_inc(row_ready, 1)

        @block.gpsimd
        def _(pool):
            with pool.Fori(0, EC // ETURN) as i:
                for h in range(2):
                    pool.wait_ge(row_ready, 2 * i + h + 3)
                    pool.sem_inc(opened, 1)
                    for c in range(HALF):
                        pool.indirect_dma_start(g.slots, bass.IndirectOffsetOnAxis(ap=to[h][:, c:c + 1], axis=0),
                                                row[h][:, c, :], None, bounds_check=ROWS - 1, oob_is_err=False
                                                ).then_inc(scattered[h], 16)
            for h in range(2):
                pool.wait_ge(scattered[h], 16 * HALF * (EC // ETURN))


def load_meta(nc, g):
    with Stage(nc, "meta") as s:
        loaded = s.sem("loaded")
        block = s.block()

        @block.sync
        def _(sp):
            rows = g.slots.rearrange("(p n) w -> p n w", p=P)
            sp.dma_start(g.meta[:, :, :], rows[:, :, C:ROWW]).then_inc(loaded, 16)
            sp.wait_ge(loaded, 16)

    with Stage(nc, "mask") as s:
        block = s.block()

        @block.vector
        def _(dve):
            for r in range(R):
                nc.vector.tensor_scalar(g.mask[:, :, r], g.meta[:, :, M_TYPE], float(r), None, ALU.is_equal)


def node_product(nc, g, name, src, width, weight, outs):
    GROUP = 5
    units = [(b, o) for b in range(GROUP) for o in outs]
    U = len(units)
    with Stage(nc, name) as s:
        rows = s.sb("rows", [P, GROUP, width])
        cols = s.sb("cols", [width, GROUP, P])
        ps_t = s.ps("t", [width, GROUP, P])
        ps = [s.ps(f"p{j}", [P, BANK]) for j in range(4)]
        rows_ready = s.sem("rows_ready")
        opened = s.sem("opened")
        turned = s.sem("turned")
        cols_ready = s.sem("cols_ready")
        product = s.sem("product")
        taken = s.sem("taken")
        block = s.block()

        @block.vector
        def _(dve):
            with dve.Fori(0, NB // GROUP) as i:
                dve.wait_ge(turned, i + 1)
                nc.vector.tensor_copy(rows[:, :, :], src[:, bass.ds(i * GROUP, GROUP), :]).then_inc(rows_ready, 1)

        @block.tensor
        def _(pe):
            pe.sem_inc(turned, 1)
            with pe.Fori(0, NB // GROUP) as i:
                pe.wait_ge(rows_ready, i + 1)
                pe.wait_ge(cols_ready, i + 1)
                pe.sem_inc(opened, 1)
                for b in range(GROUP):
                    last = nc.tensor.transpose(ps_t[:, b, :], rows[:, b, :], g.ident[:, :])
                last.then_inc(turned, 1)
                pe.wait_ge(cols_ready, i + 2)
                for u, (b, (c0, c1, to)) in enumerate(units):
                    before = u - 4 if u >= 4 else max(v for v in range(U) if v % 4 == u % 4) - U if U > u else 0
                    pe.wait_ge(taken, i * U + before + 1 + U)
                    nc.tensor.matmul(ps[u % 4][:, 0:c1 - c0], cols[:, b, :], weight[:, c0:c1],
                                     start=True, stop=True).then_inc(product, 1)

        @block.scalar
        def _(act):
            act.sem_inc(cols_ready, 1)
            act.sem_inc(taken, U)
            with act.Fori(0, NB // GROUP) as i:
                act.wait_ge(turned, i + 2)
                nc.scalar.copy(cols[:, :, :], ps_t[:, :, :]).then_inc(cols_ready, 1)
                for u, (b, (c0, c1, to)) in enumerate(units):
                    act.wait_ge(product, i * U + u + 1)
                    nc.scalar.copy(to[:, bass.ds(i * GROUP + b, 1), :], ps[u % 4][:, 0:c1 - c0].unsqueeze(1)
                                   ).then_inc(taken, 1)


def split_bf16(nc, link, parts, whole, rest):
    link(nc.vector.tensor_copy(parts[0], whole))
    link(nc.vector.tensor_tensor(rest, whole, parts[0], ALU.subtract))
    link(nc.vector.tensor_copy(parts[1], rest))
    link(nc.vector.tensor_tensor(parts[2], rest, parts[1], ALU.subtract))


def two_blocks(nc, engine, packed, k, shift, top):
    word = engine.value_load(packed[0:1, bass.ds(k, 1)])
    return [nc.s_assert_within((word >> (shift * j)) & ((1 << shift) - 1), 0, top,
                               skip_runtime_bounds_check_because=IN_RANGE) for j in range(2)]


def relation_products(nc, g, l):
    with Stage(nc, f"rel{l}") as s:
        kv = s.sb("kv", [P, NB, R * TW])
        q = g.acc[:, :, 0:R * C]
        node_product(nc, g, f"relp{l}", g.h, C, g.w_rel[l],
                     [(0, R * TW, kv), (R * TW, R * (TW + C), q), (R * (TW + C), R * (TW + C) + C, g.own)])
        written = s.sem("written")
        step = s.sem("step")
        block = s.block()

        @block.sync
        def _(sp):
            rows = g.rel_table.rearrange("(r b p) w -> r p b w", r=R, p=P)
            for r in range(R):
                sp.dma_start(rows[r], kv[:, :, r * TW:(r + 1) * TW]).then_inc(written, 16)
            sp.wait_ge(written, 16 * R)

        @block.vector
        def _(dve):
            link = chain(dve, step)
            link(nc.vector.tensor_scalar(q[:, :, :], q[:, :, :], float(D) ** -0.5, None, ALU.mult))
            split_bf16(nc, link, [g.q_split[:, j, :, :] for j in range(3)], q[:, :, :], q[:, :, :])


def relation_pass(nc, g, l):
    W = R * C + R * H
    BY_DVE = 1
    AHEAD = DEPTH - 1
    with Stage(nc, f"relpass{l}") as s:
        idx = [s.sb(f"idx{h}", [P, HALF], I32) for h in range(DEPTH)]
        row = [s.sb(f"row{h}", [P, HALF, TW]) for h in range(DEPTH)]
        hot_b = [s.sb(f"hot_b{h}", [P, HALF, P], BF16) for h in range(DEPTH)]
        hot_t = [s.sb(f"hot_t{h}", [P, HALF, P], BF16) for h in range(2)]
        hot = [s.sb(f"hot{h}", [P, HALF, P]) for h in range(2)]
        prod = s.sb("prod", [P, HALF, R * C])
        en = s.sb("en", [P, HALF, R * H])
        en_m = s.sb("en_m", [P, HALF, R * H])
        val = [s.sb(f"val{h}", [P, HALF, W]) for h in range(2)]
        ps_t = [s.ps(f"t{h}", [P, HALF, 2 * P], BF16) for h in range(2)]
        ps_q = [s.ps(f"q{h}", [P, HALF, R * C]) for h in range(2)]
        ps_s = [s.ps(f"s{j}", [P, BANK]) for j in range(2)]
        idx_ready = s.sem("idx_ready")
        opened = s.sem("opened")
        gathered = [s.sem(f"gathered{h}") for h in range(DEPTH)]
        hot_b_ready = s.sem("hot_b_ready")
        hot_ready = s.sem("hot_ready")
        turned = s.sem("turned")
        hot_t_ready = s.sem("hot_t_ready")
        query_ready = s.sem("query_ready")
        query_used = s.sem("query_used")
        reduced = s.sem("reduced")
        masked = s.sem("masked")
        energy_ready = s.sem("energy_ready")
        value_ready = s.sem("value_ready")
        summed = s.sem("summed")
        added_first = s.sem("added_first")
        added = s.sem("added")
        block = s.block()


        @block.gpsimd
        def _(pool):
            with pool.Fori(0, TURNS) as i:
                for h in range(DEPTH):
                    k = DEPTH * i + h
                    pool.wait_ge(idx_ready, k + 1)
                    pool.wait_ge(value_ready, k + 1)
                    pool.sem_inc(opened, 1)
                    for c in range(HALF):
                        pool.indirect_dma_start(row[h][:, c, :], None, g.rel_table,
                                                bass.IndirectOffsetOnAxis(ap=idx[h][:, c:c + 1], axis=0)
                                                ).then_inc(gathered[h], 16)

        @block.scalar
        def _(act):
            def take(p, k):
                act.wait_ge(turned, k + 3)
                nc.scalar.copy(hot_t[p][:, :, :], ps_t[p][:, :, 0:P]).then_inc(hot_t_ready, 1)

            act.sem_inc(hot_t_ready, 2)
            act.sem_inc(hot_ready, 2)
            act.sem_inc(value_ready, DEPTH)
            take(0, 0)
            take(1, 1)
            with act.Fori(0, TURNS) as i:
                for h in range(DEPTH):
                    k, p = DEPTH * i + h, h % 2
                    act.wait_ge(gathered[h], 16 * HALF * i + 16 * HALF)
                    act.wait_ge(summed, k + 1)
                    act.wait_ge(hot_b_ready, k + 3)
                    nc.scalar.copy(hot[p][:, :, :], hot_b[h][:, :, :]).then_inc(hot_ready, 1)
                    for c in range(HALF):
                        for r in range(0 if c < HALF - BY_DVE else 1, R):
                            last = nc.scalar.mul(val[p][:, c, r * C:(r + 1) * C], row[h][:, c, C:TW],
                                                 g.mask[:, bass.ds(i * TURN + h * HALF + c, 1), r])
                    last.then_inc(value_ready, 1)
                    act.wait_ge(query_ready, k + 3)
                    take(p, k + 2)

        @block.tensor
        def _(pe):
            def turn(h, k):
                pe.wait_ge(hot_b_ready, k + 3)
                pe.wait_ge(hot_t_ready, k + 1)
                for c in range(HALF):
                    last = nc.tensor.transpose(ps_t[h % 2][:, c, 0:P], hot_b[h][:, c, :], g.ident_b[:, :])
                last.then_inc(turned, 1)

            def query(p, k, b):
                pe.wait_ge(hot_t_ready, k + 3)
                pe.wait_ge(query_used, k + 1)
                for c in range(HALF):
                    for j in range(3):
                        last = nc.tensor.matmul(ps_q[p][:, c, :], hot_t[p][:, c, :],
                                                g.q_split[:, j, bass.ds(b[c // PAIR], 1), :].squeeze(1),
                                                start=(j == 0), stop=(j == 2))
                last.then_inc(query_ready, 1)

            pe.sem_inc(turned, 2)
            pe.sem_inc(query_ready, 2)
            pe.sem_inc(summed, 1)
            for j in range(2):
                last = nc.tensor.matmul(ps_s[j][:, :], g.zeros[:, 0:P], g.zeros[:, :], start=True, stop=True)
            last.then_inc(summed, 1)
            turn(0, 0)
            turn(1, 1)
            query(0, 0, two_blocks(nc, pe, g.blk_dst, 1, 5, NB - 1))
            with pe.Fori(0, TURNS) as i:
                for h in range(DEPTH):
                    k, p = DEPTH * i + h, h % 2
                    b = two_blocks(nc, pe, g.blk_dst, k + 2, 5, NB - 1)
                    turn((h + 2) % DEPTH, k + 2)
                    query(1 - p, k + 1, b)
                    pe.wait_ge(energy_ready, k + 1)
                    pe.wait_ge(hot_ready, k + 3)
                    pe.wait_ge(value_ready, k + 1 + DEPTH)
                    pe.wait_ge(added, k + 2)
                    for c in range(HALF):
                        last = nc.tensor.matmul(ps_s[c // PAIR][:, 0:W], hot[p][:, c, :], val[p][:, c, :],
                                                start=(c % PAIR == 0), stop=(c % PAIR == PAIR - 1))
                    last.then_inc(summed, 1)

        @block.vector
        def _(dve):
            def hots(h, at, chunks):
                for c in chunks:
                    last = nc.vector.tensor_scalar(hot_b[h][:, c, :], g.iota_b[:, :],
                                                   g.meta[:, bass.ds(at + c, 1), M_DLO], None, ALU.is_equal)
                return last

            def stage(h, at):
                gather_idx(nc, g, idx, h, at, M_REL).then_inc(idx_ready, 1)

            def add(j, b):
                to = g.acc[:, bass.ds(b, 1), :].squeeze(1)
                return nc.vector.tensor_tensor(to, ps_s[j][:, 0:W], to, ALU.add)

            dve.sem_inc(hot_b_ready, 2)
            dve.sem_inc(query_used, 2)
            nc.vector.memset(g.acc[:, :, :], 0.0).then_inc(added, 1)
            for h in range(AHEAD):
                hots(h, h * HALF, range(HALF)).then_inc(hot_b_ready, 1)
            for h in range(DEPTH):
                stage(h, h * HALF)
            with dve.Fori(0, TURNS) as i:
                for h in range(DEPTH):
                    k, p = DEPTH * i + h, h % 2
                    at = i * TURN + h * HALF
                    ahead, at_ahead = (h + AHEAD) % DEPTH, at + AHEAD * HALF
                    dve.wait_ge(query_ready, k + 3)
                    dve.wait_ge(gathered[h], 16 * HALF * i + 16 * HALF)
                    nc.vector.tensor_tensor(
                        prod[:, :, :].rearrange("p c (r w) -> p c r w", r=R),
                        ps_q[p][:, :, :].rearrange("p c (r w) -> p c r w", r=R),
                        row[h][:, :, 0:C].unsqueeze(2).to_broadcast([P, HALF, R, C]), ALU.mult
                    ).then_inc(query_used, 1)
                    for c in range(HALF - BY_DVE, HALF):
                        nc.vector.tensor_scalar(val[p][:, c, 0:C], row[h][:, c, C:TW],
                                                g.mask[:, bass.ds(at + c, 1), 0], None, ALU.mult)
                    stage(h, at + TURN)
                    b = two_blocks(nc, dve, g.blk_dst, k, 5, NB - 1)
                    dve.wait_ge(query_used, k + 3)
                    nc.vector.tensor_reduce(en[:, :, :], prod[:, :, :].rearrange("p c (g d) -> p c g d", d=D),
                                            AX, ALU.add).then_inc(reduced, 1)
                    dve.wait_ge(turned, k + 2)
                    dve.wait_ge(hot_ready, k + 2)
                    hots(ahead, at_ahead, range(HALF - 2))
                    dve.wait_ge(reduced, k + 1)
                    nc.vector.tensor_tensor(en_m[:, :, :].rearrange("p c (r h) -> p (c r) h", r=R),
                                            en[:, :, :].rearrange("p c (r h) -> p (c r) h", r=R),
                                            wide(g.mask[:, bass.ds(at, HALF), :].rearrange("p c r -> p (c r)"), H),
                                            ALU.mult).then_inc(masked, 1)
                    hots(ahead, at_ahead, [HALF - 2])
                    dve.wait_ge(masked, k + 1)
                    nc.vector.scalar_tensor_tensor(val[p][:, :, R * C:W], en_m[:, :, :], 0.01, en_m[:, :, :],
                                                   ALU.mult, ALU.max).then_inc(energy_ready, 1)
                    dve.wait_ge(summed, k + 2)
                    dve.wait_ge(added, k + 1)
                    add(0, b[0]).then_inc(added_first, 1)
                    hots(ahead, at_ahead, [HALF - 1]).then_inc(hot_b_ready, 1)
                    dve.wait_ge(added_first, k + 1)
                    add(1, b[1]).then_inc(added, 1)
            last_step = DEPTH * TURNS
            b = two_blocks(nc, dve, g.blk_dst, last_step, 5, NB - 1)
            dve.wait_ge(summed, last_step + 2)
            dve.wait_ge(added, last_step + 1)
            add(0, b[0]).then_inc(added_first, 1)
            dve.wait_ge(added_first, last_step + 1)
            add(1, b[1]).then_inc(added, 1)


def layer_norm(nc, g, name, y, affine=None):
    with Stage(nc, name) as s:
        mean = s.sb("mean", [P, NB])
        sq = s.sb("sq", [P, NB, C])
        step = s.sem("step")
        var_ready = s.sem("var_ready")
        sd_ready = s.sem("sd_ready")
        block = s.block()

        @block.scalar
        def _(act):
            act.wait_ge(var_ready, 1)
            nc.scalar.activation(mean[:, :], mean[:, :], ACT.Sqrt).then_inc(sd_ready, 1)

        @block.vector
        def _(dve):
            link = chain(dve, step)
            link(nc.vector.tensor_reduce(mean[:, :], y[:, :, :], AX, ALU.add))
            link(nc.vector.tensor_scalar(mean[:, :], mean[:, :], 1.0 / C, None, ALU.mult))
            link(nc.vector.tensor_tensor(y[:, :, :], y[:, :, :], wide(mean[:, :], C), ALU.subtract))
            link(nc.vector.tensor_tensor(sq[:, :, :], y[:, :, :], y[:, :, :], ALU.mult))
            link(nc.vector.tensor_reduce(mean[:, :], sq[:, :, :], AX, ALU.add))
            nc.vector.tensor_scalar(mean[:, :], mean[:, :], 1.0 / C, 1e-5, ALU.mult, ALU.add).then_inc(var_ready, 1)
            dve.wait_ge(sd_ready, 1)
            link(nc.vector.reciprocal(mean[:, :], mean[:, :]))
            link(nc.vector.tensor_tensor(y[:, :, :], y[:, :, :], wide(mean[:, :], C), ALU.mult))
            if affine is not None:
                for v, op in zip(affine, (ALU.mult, ALU.add)):
                    link(nc.vector.tensor_tensor(y[:, :, :], y[:, :, :],
                                                 v.unsqueeze(1).to_broadcast([P, NB, C]), op))


def relation_nodes(nc, g, l):
    RH = R * H
    with Stage(nc, f"relnode{l}") as s:
        en = s.sb("en", [P, NB, RH])
        part = s.sb("part", [P, RH])
        top = s.sb("top", [RH, 1])
        diag = s.sb("diag", [RH, RH])
        msg = s.sb("msg", [P, NB, R * C])
        mix = s.sb("mix", [P, NB * R, C])
        score = s.sb("score", [P, NB, R])
        best = s.sb("best", [P, NB])
        val = g.acc[:, :, 0:R * C]

        with Stage(nc, f"alpha{l}") as a:
            ps_a = a.ps("a", [P, BANK])
            ps_b = a.ps("b", [P, BANK])
            ps_c = a.ps("c", [P, BANK])
            step = a.sem("step")
            part_ready = a.sem("part_ready")
            turned = a.sem("turned")
            diag_ready = a.sem("diag_ready")
            shift_ready = a.sem("shift_ready")
            shifted = a.sem("shifted")
            exps = a.sem("exps")
            sums_ready = a.sem("sums_ready")
            total = a.sem("total")
            block = a.block()

            @block.tensor
            def _(pe):
                pe.wait_ge(part_ready, 1)
                nc.tensor.transpose(ps_a[0:RH, 0:P], part[:, :], g.ident[:, :]).then_inc(turned, 1)
                pe.wait_ge(diag_ready, 1)
                nc.tensor.matmul(ps_b[:, 0:RH], g.ones[0:RH, :], diag[:, :], start=True, stop=True).then_inc(shift_ready, 1)
                pe.wait_ge(sums_ready, 1)
                nc.tensor.matmul(ps_c[:, 0:RH], g.ones[:, :], part[:, :], start=True, stop=True).then_inc(total, 1)

            @block.scalar
            def _(act):
                act.wait_ge(shifted, 1)
                nc.scalar.activation(en[:, :, :], en[:, :, :], ACT.Exp).then_inc(exps, 1)

            @block.vector
            def _(dve):
                link = chain(dve, step)
                link(nc.vector.tensor_copy(en[:, :, :], g.acc[:, :, R * C:]))
                link(nc.vector.tensor_scalar(en[:, NB - 1, :], en[:, NB - 1, :], g.no_node[:, 0:1], None, ALU.add))
                nc.vector.tensor_reduce(part[:, :], en[:, :, :].rearrange("p b g -> p g b"), AX, ALU.max
                                        ).then_inc(part_ready, 1)
                dve.wait_ge(turned, 1)
                link(nc.vector.tensor_reduce(top[:, :], ps_a[0:RH, 0:P], AX, ALU.max))
                nc.vector.tensor_scalar(diag[:, :], g.ident[0:RH, 0:RH], top[:, 0:1], None, ALU.mult
                                        ).then_inc(diag_ready, 1)
                dve.wait_ge(shift_ready, 1)
                nc.vector.tensor_tensor(en[:, :, :], en[:, :, :], ps_b[:, 0:RH].unsqueeze(1).to_broadcast([P, NB, RH]),
                                        ALU.subtract).then_inc(shifted, 1)
                dve.wait_ge(exps, 1)
                nc.vector.tensor_reduce(part[:, :], en[:, :, :].rearrange("p b g -> p g b"), AX, ALU.add
                                        ).then_inc(sums_ready, 1)
                dve.wait_ge(total, 1)
                link(nc.vector.reciprocal(part[:, :], ps_c[:, 0:RH]))
                link(nc.vector.tensor_tensor(en[:, :, :], en[:, :, :], part[:, :].unsqueeze(1).to_broadcast([P, NB, RH]),
                                             ALU.mult))
                v = val.rearrange("p b (g d) -> p b g d", d=D)
                link(nc.vector.tensor_tensor(v, v, wide(en[:, :, :], D), ALU.mult))

        for j in range(2):
            node_product(nc, g, f"cat{l}{j}", g.acc[:, :, j * P:(j + 1) * P], P, g.w_cat[l][j],
                         [(0, P, msg[:, :, j * P:(j + 1) * P])])

        with Stage(nc, f"mix{l}") as a:
            step = a.sem("step")
            shifted = a.sem("shifted")
            exps = a.sem("exps")
            sum_ready = a.sem("sum_ready")
            gelu = a.sem("gelu")
            block = a.block()
            m = msg[:, :, :].rearrange("p b (r c) -> p (b r) c", c=C)

            @block.scalar
            def _(act):
                act.wait_ge(shifted, 1)
                nc.scalar.activation(score[:, :, :], score[:, :, :], ACT.Exp).then_inc(exps, 1)
                act.wait_ge(sum_ready, 1)
                nc.scalar.activation(g.own[:, :, :], g.own[:, :, :], ACT.Gelu).then_inc(gelu, 1)

            @block.vector
            def _(dve):
                link = chain(dve, step)
                flat = score[:, :, :].rearrange("p b r -> p (b r)")
                link(nc.vector.tensor_tensor(mix[:, :, :], m, g.sem_w[l].unsqueeze(1).to_broadcast([P, NB * R, C]),
                                             ALU.mult))
                link(nc.vector.tensor_reduce(flat, mix[:, :, :], AX, ALU.add))
                link(nc.vector.tensor_scalar(flat, flat, g.sem_b[:, l:l + 1], None, ALU.add))
                link(nc.vector.tensor_reduce(best[:, :], score[:, :, :], AX, ALU.max))
                nc.vector.tensor_tensor(score[:, :, :], score[:, :, :], wide(best[:, :], R), ALU.subtract
                                        ).then_inc(shifted, 1)
                dve.wait_ge(exps, 1)
                link(nc.vector.tensor_reduce(best[:, :], score[:, :, :], AX, ALU.add))
                link(nc.vector.reciprocal(best[:, :], best[:, :]))
                link(nc.vector.tensor_tensor(score[:, :, :], score[:, :, :], wide(best[:, :], R), ALU.mult))
                link(nc.vector.tensor_tensor(mix[:, :, :], m, wide(flat, C), ALU.mult))
                link(nc.vector.tensor_reduce(msg[:, :, 0:C], mix[:, :, :].rearrange("p (b r) c -> p b c r", r=R),
                                             AX, ALU.add))
                nc.vector.tensor_tensor(g.own[:, :, :], g.own[:, :, :], msg[:, :, 0:C], ALU.add).then_inc(sum_ready, 1)
                dve.wait_ge(gelu, 1)
                link(nc.vector.tensor_tensor(g.h[:, :, :], g.h[:, :, :], g.own[:, :, :], ALU.add))
    layer_norm(nc, g, f"relln{l}", g.h, (g.ln_g[l], g.ln_b[l]))


def residual_norm(nc, g, name):
    with Stage(nc, name + "_add") as s:
        block = s.block()

        @block.vector
        def _(dve):
            nc.vector.tensor_tensor(g.x[:, :, :], g.x[:, :, :], g.h[:, :, :], ALU.add)
    layer_norm(nc, g, name + "_ln", g.x)
    with Stage(nc, name + "_next") as s:
        block = s.block()

        @block.vector
        def _(dve):
            nc.vector.tensor_copy(g.h[:, :, :], g.x[:, :, :])


def gather_idx(nc, g, idx, h, at, word):
    return nc.vector.tensor_copy(idx[h][:, :], g.meta[:, bass.ds(at, HALF), word].bitcast(I32))


def one_hot(nc, g, to, at, word):
    return nc.vector.tensor_tensor(to, g.iota[:, :].unsqueeze(1).to_broadcast([P, HALF, P]),
                                   wide(g.meta[:, bass.ds(at, HALF), word], P), ALU.is_equal)


def weigh_pass(nc, g):
    with Stage(nc, "weigh") as s:
        split = s.sb("split", [P, 3, NB, C], BF16)
        to = [s.sb(f"to{h}", [P, HALF], I32) for h in range(DEPTH)]
        row = [s.sb(f"row{h}", [P, HALF, SROWW]) for h in range(DEPTH)]
        hot_b = [s.sb(f"hot_b{h}", [P, HALF, P], BF16) for h in range(2)]
        hot_t = [s.sb(f"hot_t{h}", [P, HALF, P], BF16) for h in range(2)]
        ps_t = [s.ps(f"t{h}", [P, HALF, 2 * P], BF16) for h in range(2)]
        ps_x = [s.ps(f"x{h}", [P, HALF, 2 * C]) for h in range(2)]
        opened = s.sem("opened")
        hot_b_ready = s.sem("hot_b_ready")
        turned = s.sem("turned")
        hot_t_ready = s.sem("hot_t_ready")
        found = s.sem("found")
        row_ready = s.sem("row_ready")
        row_free = s.sem("row_free")
        scattered = [s.sem(f"scattered{h}") for h in range(DEPTH)]
        split_rows(nc, g, "weigh_split", g.h, split)
        block = s.block()

        @block.sync
        def _(sp):
            sp.sem_inc(row_free, DEPTH)
            with sp.Fori(0, TURNS) as i:
                for h in range(DEPTH):
                    sp.wait_ge(scattered[h], 16 * HALF * i + 16 * HALF)
                    sp.sem_inc(row_free, 1)

        @block.gpsimd
        def _(pool):
            with pool.Fori(0, TURNS) as i:
                for h in range(DEPTH):
                    pool.wait_ge(row_ready, DEPTH * i + h + 3)
                    pool.sem_inc(opened, 1)
                    for c in range(HALF):
                        pool.indirect_dma_start(g.sslots, bass.IndirectOffsetOnAxis(ap=to[h][:, c:c + 1], axis=0),
                                                row[h][:, c, :], None, bounds_check=ROWS - 1, oob_is_err=False
                                                ).then_inc(scattered[h], 16)
            for h in range(DEPTH):
                pool.wait_ge(scattered[h], 16 * HALF * TURNS)

        @block.scalar
        def _(act):
            act.sem_inc(hot_t_ready, 2)
            with act.Fori(0, TURNS) as i:
                for h in range(DEPTH):
                    k, p = DEPTH * i + h, h % 2
                    act.wait_ge(turned, k + 3)
                    act.wait_ge(found, k + 1)
                    nc.scalar.copy(hot_t[p][:, :, :], ps_t[p][:, :, 0:P]).then_inc(hot_t_ready, 1)

        @block.tensor
        def _(pe):
            def turn(p, k):
                pe.wait_ge(hot_b_ready, k + 1)
                pe.wait_ge(hot_t_ready, k + 1)
                for c in range(HALF):
                    last = nc.tensor.transpose(ps_t[p][:, c, 0:P], hot_b[p][:, c, :], g.ident_b[:, :])
                last.then_inc(turned, 1)

            pe.sem_inc(turned, 2)
            pe.sem_inc(found, 2)
            turn(0, 0)
            with pe.Fori(0, TURNS) as i:
                for h in range(DEPTH):
                    k, p = DEPTH * i + h, h % 2
                    b = two_blocks(nc, pe, g.blk_dst, k + 1, 5, NB - 1)
                    turn(1 - p, k + 1)
                    pe.wait_ge(hot_t_ready, k + 3)
                    pe.wait_ge(row_ready, k + 1)
                    for c in range(HALF):
                        for j in range(3):
                            last = nc.tensor.matmul(ps_x[p][:, c, 0:C], hot_t[p][:, c, :],
                                                    split[:, j, bass.ds(b[c // PAIR], 1), :].squeeze(1),
                                                    start=(j == 0), stop=(j == 2))
                    last.then_inc(found, 1)

        @block.vector
        def _(dve):
            def hots(p, at, k):
                dve.wait_ge(turned, k + 1)
                one_hot(nc, g, hot_b[p][:, :, :], at, M_DLO).then_inc(hot_b_ready, 1)

            dve.sem_inc(row_ready, 2)
            hots(0, 0, 0)
            with dve.Fori(0, TURNS) as i:
                for h in range(DEPTH):
                    k, p = DEPTH * i + h, h % 2
                    at = i * TURN + h * HALF
                    hots(1 - p, at + HALF, k + 1)
                    dve.wait_ge(found, k + 3)
                    dve.wait_ge(row_free, k + 1)
                    nc.vector.tensor_tensor(row[h][:, :, 0:C], ps_x[p][:, :, 0:C],
                                            wide(g.meta[:, bass.ds(at, HALF), M_WEIGHT], C), ALU.mult)
                    nc.vector.tensor_copy(row[h][:, :, C], g.meta[:, bass.ds(at, HALF), M_SLO])
                    gather_idx(nc, g, to, h, at, M_SROW).then_inc(row_ready, 1)


def split_rows(nc, g, name, of, split):
    with Stage(nc, name) as s:
        rest = s.sb("rest", [P, *of.shape[1:]])
        step = s.sem("step")
        block = s.block()

        @block.vector
        def _(dve):
            link = chain(dve, step)
            link(nc.vector.tensor_copy(rest[:], of[:]))
            split_bf16(nc, link, [split[:, j] for j in range(3)], rest[:], rest[:])


def open_sums(nc, pe, g, ps_sum):
    for j in range(4):
        last = nc.tensor.matmul(ps_sum[:, j * BANK:(j + 1) * BANK], g.zeros[:, 0:P], g.zeros[:, :],
                                start=True, stop=True, skip_group_check=True)
    return last


def add_sums(nc, pe, ps_sum, col, hot, val, width):
    for c in range(HALF):
        last = nc.tensor.matmul(ps_sum[:, bass.ds(col[c // PAIR], width)], hot[:, c, :], val[:, c, :],
                                start=False, stop=True, skip_group_check=True)
    return last


def take_sums(nc, name, ps_sum, out, width):
    with Stage(nc, name) as s:
        block = s.block()

        @block.vector
        def _(dve):
            for j in range(-(-NB // 7)):
                n = min(7, NB - 7 * j)
                nc.vector.tensor_copy(out[:, 7 * j:7 * j + n, 0:width],
                                      ps_sum[:, j * BANK:j * BANK + n * UC].rearrange("p (b w) -> p b w", w=UC)
                                      [:, :, 0:width])


def stream_sum_pass(nc, g, name, slots, width, columns, node, weight, out):
    with Stage(nc, name) as s:
        LOAD = 2 * HALF
        RING = 4
        rows = [s.sb(f"rows{h}", [P, LOAD, width]) for h in range(RING)]
        hot = [s.sb(f"hot{h}", [P, HALF, P]) for h in range(4)]
        ps_sum = s.ps("sum", [P, 4 * BANK])
        rows_ready = [s.sem(f"rows_ready{h}") for h in range(RING)]
        hot_ready = s.sem("hot_ready")
        summed = s.sem("summed")
        src = slots.rearrange("(p n) w -> p n w", p=P)
        loops = NC // (RING * LOAD)
        steps = [(h, q) for h in range(RING) for q in range(2)]
        assert NC % (RING * LOAD) == 0

        with Stage(nc, name + "_block") as t:
            block = t.block()

            @block.sync
            def _(sp):
                with sp.Fori(0, loops) as i:
                    for h in range(RING):
                        sp.wait_ge(summed, 2 * RING * i + 2 * h + 2)
                        sp.dma_start(rows[h][:, :, :], src[:, bass.ds((RING * i + h) * LOAD, LOAD), :]
                                     ).then_inc(rows_ready[h], 16)

            @block.vector
            def _(dve):
                with dve.Fori(0, loops) as i:
                    for n, (h, q) in enumerate(steps):
                        k = 2 * RING * i + n
                        at = i * (RING * LOAD) + n * HALF
                        dve.wait_ge(rows_ready[h], 16 * i + 16)
                        dve.wait_ge(summed, k + 2 * RING - 3)
                        for c in range(HALF):
                            where = node(rows[h], q * HALF + c, at + c)
                            if weight is None:
                                last = nc.vector.tensor_scalar(hot[n % 4][:, c, :], g.iota[:, :], where, None,
                                                               ALU.is_equal)
                            else:
                                last = nc.vector.tensor_scalar(hot[n % 4][:, c, :], g.iota[:, :], where,
                                                               weight(at + c), ALU.is_equal, ALU.mult)
                        last.then_inc(hot_ready, 1)

            @block.tensor
            def _(pe):
                packed = g.col_src if weight is None else g.col_dst
                pe.sem_inc(summed, 2 * RING - 1)
                open_sums(nc, pe, g, ps_sum).then_inc(summed, 1)
                with pe.Fori(0, loops) as i:
                    for n, (h, q) in enumerate(steps):
                        k = 2 * RING * i + n
                        col = two_blocks(nc, pe, packed, k + 1, 12, psum_column(NB - 1))
                        pe.wait_ge(hot_ready, k + 1)
                        pe.wait_ge(rows_ready[h], 16 * i + 16)
                        add_sums(nc, pe, ps_sum, col, hot[n % 4], rows[h][:, q * HALF:(q + 1) * HALF, 0:columns],
                                 columns).then_inc(summed, 1)

        take_sums(nc, name + "_take", ps_sum, out, columns)


def message_pass(nc, g, out):
    with Stage(nc, "message") as s:
        idx = [s.sb(f"idx{h}", [P, HALF], I32) for h in range(DEPTH)]
        row = [s.sb(f"row{h}", [P, HALF, C]) for h in range(DEPTH)]
        own = [s.sb(f"own{h}", [P, HALF, C]) for h in range(DEPTH)]
        both = [s.sb(f"both{h}", [P, HALF, C]) for h in range(2)]
        val = [s.sb(f"val{h}", [P, HALF, C]) for h in range(2)]
        hot = [s.sb(f"hot{h}", [P, HALF, P]) for h in range(2)]
        ps_sum = s.ps("sum", [P, 4 * BANK])
        opened = s.sem("opened")
        idx_ready = s.sem("idx_ready")
        gathered = [s.sem(f"gathered{h}") for h in range(DEPTH)]
        own_ready = [s.sem(f"own_ready{h}") for h in range(DEPTH)]
        both_ready = s.sem("both_ready")
        val_ready = s.sem("val_ready")
        hot_ready = s.sem("hot_ready")
        summed = s.sem("summed")

        with Stage(nc, "message_block") as t:
            block = t.block()

            @block.sync
            def _(sp):
                src = g.slots.rearrange("(p n) w -> p n w", p=P)
                with sp.Fori(0, TURNS) as i:
                    for h in range(DEPTH):
                        sp.wait_ge(both_ready, DEPTH * i + h + 1)
                        sp.dma_start(own[h][:, :, :], src[:, bass.ds(i * TURN + h * HALF, HALF), 0:C]
                                     ).then_inc(own_ready[h], 16)

            @block.gpsimd
            def _(pool):
                with pool.Fori(0, TURNS) as i:
                    for h in range(DEPTH):
                        pool.wait_ge(idx_ready, DEPTH * i + h + 1)
                        pool.sem_inc(opened, 1)
                        for c in range(HALF):
                            pool.indirect_dma_start(row[h][:, c, :], None, g.msg_table,
                                                    bass.IndirectOffsetOnAxis(ap=idx[h][:, c:c + 1], axis=0)
                                                    ).then_inc(gathered[h], 16)

            @block.vector
            def _(dve):
                dve.sem_inc(both_ready, DEPTH)
                for h in range(DEPTH):
                    gather_idx(nc, g, idx, h, h * HALF, M_SRC).then_inc(idx_ready, 1)
                with dve.Fori(0, TURNS) as i:
                    for h in range(DEPTH):
                        k = DEPTH * i + h
                        at = i * TURN + h * HALF
                        dve.wait_ge(summed, k + 1)
                        one_hot(nc, g, hot[h % 2][:, :, :], at, M_DLO).then_inc(hot_ready, 1)
                        dve.wait_ge(gathered[h], 16 * HALF * i + 16 * HALF)
                        dve.wait_ge(own_ready[h], 16 * i + 16)
                        dve.wait_ge(val_ready, k + 1)
                        nc.vector.tensor_tensor(both[h % 2][:, :, :], row[h][:, :, :], own[h][:, :, :], ALU.add
                                                ).then_inc(both_ready, 1)
                        gather_idx(nc, g, idx, h, at + TURN, M_SRC).then_inc(idx_ready, 1)

            @block.scalar
            def _(act):
                act.sem_inc(val_ready, 2)
                with act.Fori(0, TURNS) as i:
                    for h in range(DEPTH):
                        k = DEPTH * i + h
                        act.wait_ge(both_ready, k + 1 + DEPTH)
                        act.wait_ge(summed, k + 1)
                        nc.scalar.activation(val[h % 2][:, :, :], both[h % 2][:, :, :], ACT.Relu).then_inc(val_ready, 1)

            @block.tensor
            def _(pe):
                pe.sem_inc(summed, 1)
                open_sums(nc, pe, g, ps_sum).then_inc(summed, 1)
                with pe.Fori(0, TURNS) as i:
                    for h in range(DEPTH):
                        k = DEPTH * i + h
                        col = two_blocks(nc, pe, g.col_dst, k + 1, 12, psum_column(NB - 1))
                        pe.wait_ge(hot_ready, k + 1)
                        pe.wait_ge(val_ready, k + 3)
                        add_sums(nc, pe, ps_sum, col, hot[h % 2], val[h % 2], C).then_inc(summed, 1)

        take_sums(nc, "message_take", ps_sum, out, C)


def gat_max_pass(nc, g, l):
    with Stage(nc, f"gatmax{l}") as s:
        idx = [s.sb(f"idx{h}", [P, HALF], I32) for h in range(DEPTH)]
        row = [s.sb(f"row{h}", [P, HALF, GW]) for h in range(DEPTH)]
        score = [s.sb(f"score{h}", [P, HALF, P]) for h in range(2)]
        far = [s.sb(f"far{h}", [P, HALF, P]) for h in range(2)]
        dlo = [s.sb(f"dlo{h}", [P, HALF]) for h in range(DEPTH)]
        found = s.sb("found", [P, HALF])
        junk = s.sb("junk", [P, HALF, P])
        red = s.sb("red", [P, PAIR])
        ps = [s.ps(f"t{h}", [P, HALF, P]) for h in range(2)]
        opened = s.sem("opened")
        idx_ready = s.sem("idx_ready")
        gathered = [s.sem(f"gathered{h}") for h in range(DEPTH)]
        stored = [s.sem(f"stored{h}") for h in range(DEPTH)]
        row_free = s.sem("row_free")
        far_ready = s.sem("far_ready")
        drafted = s.sem("drafted")
        score_ready = s.sem("score_ready")
        turned = s.sem("turned")
        reduced = s.sem("reduced")
        lifted_first = s.sem("lifted_first")
        lifted = s.sem("lifted")
        looked_up = s.sem("looked_up")
        found_used = s.sem("found_used")
        block = s.block()
        to = g.gat_rows.rearrange("(p n) w -> p n w", p=P)


        @block.sync
        def _(sp):
            with sp.Fori(0, TURNS) as i:
                for h in range(DEPTH):
                    sp.wait_ge(gathered[h], 16 * HALF * i + 16 * HALF)
                    sp.dma_start(to[:, bass.ds(i * TURN + h * HALF, HALF), :], row[h][:, :, :]).then_inc(stored[h], 16)
            for h in range(DEPTH):
                sp.wait_ge(stored[h], 16 * TURNS)

        @block.scalar
        def _(act):
            def measure(h, p, k):
                act.wait_ge(idx_ready, k + 1)
                act.wait_ge(score_ready, k + 1)
                for c in range(HALF):
                    last = nc.scalar.activation(far[p][:, c, :], g.iota[:, :], ACT.Abs, bias=dlo[h][:, c:c + 1],
                                                scale=-1.0)
                last.then_inc(far_ready, 1)

            act.sem_inc(row_free, DEPTH)
            measure(0, 0, 0)
            with act.Fori(0, TURNS) as i:
                for h in range(DEPTH):
                    k = DEPTH * i + h
                    measure((h + 1) % DEPTH, (h + 1) % 2, k + 1)
                    act.wait_ge(stored[h], 16 * i + 16)
                    act.sem_inc(row_free, 1)

        @block.gpsimd
        def _(pool):
            with pool.Fori(0, TURNS) as i:
                for h in range(DEPTH):
                    pool.wait_ge(row_free, DEPTH * i + h + 1)
                    pool.wait_ge(idx_ready, DEPTH * i + h + 1)
                    pool.sem_inc(opened, 1)
                    for c in range(HALF):
                        pool.indirect_dma_start(row[h][:, c, :], None, g.gat_table,
                                                bass.IndirectOffsetOnAxis(ap=idx[h][:, c:c + 1], axis=0)
                                                ).then_inc(gathered[h], 16)

        @block.tensor
        def _(pe):
            def turn(p):
                for c in range(HALF):
                    last = nc.tensor.transpose(ps[p][:, c, :], score[p][:, c, :], g.ident[:, :])
                last.then_inc(turned, 1)

            pe.sem_inc(turned, 1)
            pe.wait_ge(score_ready, 1)
            turn(1)
            with pe.Fori(0, TURNS) as i:
                for h in range(DEPTH):
                    k = DEPTH * i + h
                    pe.wait_ge(score_ready, k + 2)
                    turn(h % 2)

        @block.vector
        def _(dve):
            def reduce(p, k):
                dve.wait_ge(turned, k + 2)
                dve.wait_ge(lifted, k + 1)
                nc.vector.tensor_reduce(red[:, :], ps[p][:, :, :].rearrange("p (j c) e -> p j (c e)", j=PAIR),
                                        AX, ALU.max).then_inc(reduced, 1)

            def lift(j, b):
                to = g.top[:, bass.ds(b, 1)]
                return nc.vector.tensor_tensor(to, to, red[:, j:j + 1], ALU.max)

            def stage(h, at):
                nc.vector.tensor_copy(dlo[h][:, :], g.meta[:, bass.ds(at, HALF), M_DLO])
                gather_idx(nc, g, idx, h, at, M_SRC).then_inc(idx_ready, 1)

            dve.sem_inc(lifted, 1)
            nc.vector.memset(score[1][:, :, :], -BIG).then_inc(score_ready, 1)
            for h in range(DEPTH):
                stage(h, h * HALF)
            with dve.Fori(0, TURNS) as i:
                before = two_blocks(nc, dve, g.blk_dst, DEPTH * i, 5, NB - 1)
                b = two_blocks(nc, dve, g.blk_dst, DEPTH * i + 1, 5, NB - 1)
                for h in range(DEPTH):
                    k, p = DEPTH * i + h, h % 2
                    at = i * TURN + h * HALF
                    dve.wait_ge(idx_ready, k + 1)
                    look_up(nc, g, b, dlo[h], g.dst_rows, found, junk).then_inc(looked_up, 1)
                    reduce(1 - p, k)
                    dve.wait_ge(gathered[h], 16 * HALF * i + 16 * HALF)
                    dve.wait_ge(turned, k + 1)
                    for c in range(HALF):
                        last = nc.vector.tensor_scalar(score[p][:, c, :], g.iota[:, :], dlo[h][:, c:c + 1],
                                                       row[h][:, c, C + 1:GW], ALU.is_equal, ALU.mult)
                    last.then_inc(drafted, 1)
                    after = two_blocks(nc, dve, g.blk_dst, k + 2, 5, NB - 1) if h + 1 < DEPTH else None
                    dve.wait_ge(reduced, k + 1)
                    lift(0, before[0]).then_inc(lifted_first, 1)
                    dve.wait_ge(looked_up, k + 1)
                    nc.vector.tensor_tensor(g.edge_score[:, bass.ds(at, HALF)], row[h][:, :, C + 1], found[:, :],
                                            ALU.add).then_inc(found_used, 1)
                    dve.wait_ge(drafted, k + 1)
                    dve.wait_ge(far_ready, k + 1)
                    nc.vector.scalar_tensor_tensor(score[p][:, :, :], far[p][:, :, :], -BIG, score[p][:, :, :],
                                                   ALU.mult, ALU.add).then_inc(score_ready, 1)
                    dve.wait_ge(lifted_first, k + 1)
                    lift(1, before[1]).then_inc(lifted, 1)
                    dve.wait_ge(found_used, k + 1)
                    stage(h, at + TURN)
                    before, b = b, after
            steps = DEPTH * TURNS
            b = two_blocks(nc, dve, g.blk_dst, steps, 5, NB - 1)
            reduce(1, steps)
            dve.wait_ge(reduced, steps + 1)
            lift(0, b[0]).then_inc(lifted_first, 1)
            dve.wait_ge(lifted_first, steps + 1)
            lift(1, b[1]).then_inc(lifted, 1)


def look_up(nc, g, b, dlo, nodes, to, junk):
    for c in range(HALF):
        last = nc.vector.scalar_tensor_tensor(junk[:, c, :], g.iota[:, :], dlo[:, c:c + 1],
                                              nodes[:, bass.ds(b[c // PAIR], 1), :].squeeze(1),
                                              ALU.is_equal, ALU.mult, accum_out=to[:, c:c + 1])
    return last


def spread_nodes(nc, g, name, of, to):
    with Stage(nc, name) as s:
        by_block = s.sb("by_block", [NB, P])
        ps = s.ps("turn", [NB, P])
        turned = s.sem("turned")
        taken = s.sem("taken")
        moved = s.sem("moved")
        block = s.block()

        @block.tensor
        def _(pe):
            nc.tensor.transpose(ps[:, :], of, g.ident[:, :]).then_inc(turned, 1)

        @block.vector
        def _(dve):
            dve.wait_ge(turned, 1)
            nc.vector.tensor_copy(by_block[:, :], ps[:, :]).then_inc(taken, 1)

        @block.sync
        def _(sp):
            sp.wait_ge(taken, 1)
            sp.dma_start(g.node_row, by_block[:, :]).then_inc(moved, 16)
            sp.wait_ge(moved, 16)
            sp.dma_start(to[:, :, :], g.node_row.unsqueeze(0).to_broadcast([P, NB, P])).then_inc(moved, 16)
            sp.wait_ge(moved, 32)


def gat_sum_pass(nc, g, l, out):
    with Stage(nc, f"gatleaky{l}") as s:
        step = s.sem("step")
        block = s.block()

        @block.vector
        def _(dve):
            nc.vector.scalar_tensor_tensor(g.edge_leaky[:, 0:NC], g.edge_score[:, 0:NC], 0.2, g.edge_score[:, 0:NC],
                                           ALU.mult, ALU.max)
            nc.vector.memset(g.edge_leaky[:, NC:CP], 0.0)

    with Stage(nc, f"gatsum{l}") as s:
        RING = 8
        LOAD = 2 * HALF
        LOADS = RING // 2
        AHEAD = 3
        ONES = 2
        small = lambda n: [s.sb(f"{n}{h}", [P, HALF]) for h in range(RING)]
        dlo, top, below, capped, w, minus_w = [small(n) for n in ("dlo", "top", "below", "capped", "w", "minus_w")]
        junk = s.sb("junk", [P, HALF, P])
        far = [s.sb(f"far{h}", [P, ONES, P]) for h in range(2)]
        hot = [s.sb(f"hot{h}", [P, HALF, P]) for h in range(4)]
        rows = [s.sb(f"rows{h}", [P, LOAD, GW]) for h in range(LOADS)]
        ps_sum = s.ps("sum", [P, 4 * BANK])
        rows_ready = [s.sem(f"rows_ready{h}") for h in range(LOADS)]
        dlo_ready = s.sem("dlo_ready")
        looked_up = s.sem("looked_up")
        lowered = s.sem("lowered")
        capped_ready = s.sem("capped_ready")
        w_ready = s.sem("w_ready")
        minus_ready = s.sem("minus_ready")
        far_ready = s.sem("far_ready")
        hot_act = s.sem("hot_act")
        hot_dve = s.sem("hot_dve")
        summed = s.sem("summed")
        loops = NC // (RING * HALF)
        assert NC % (RING * HALF) == 0
        src = g.gat_rows.rearrange("(p n) w -> p n w", p=P)

        with Stage(nc, f"gatsum{l}_block") as t:
            block = t.block()

            @block.sync
            def _(sp):
                with sp.Fori(0, loops) as i:
                    for h in range(LOADS):
                        sp.wait_ge(summed, RING * i + 2 * h + 2)
                        sp.dma_start(rows[h][:, :, :], src[:, bass.ds((LOADS * i + h) * LOAD, LOAD), :]
                                     ).then_inc(rows_ready[h], 16)

            @block.vector
            def _(dve):
                def stage(n, at):
                    nc.vector.tensor_copy(dlo[n][:, :], g.meta[:, bass.ds(at, HALF), M_DLO]).then_inc(dlo_ready, 1)

                def find(n, k, b):
                    dve.wait_ge(dlo_ready, k + 1)
                    look_up(nc, g, b, dlo[n], g.dst_rows, top[n], junk).then_inc(looked_up, 1)

                def lower(n, k, at):
                    dve.wait_ge(looked_up, k + 1)
                    nc.vector.tensor_tensor(below[n][:, :], g.edge_leaky[:, bass.ds(at, HALF)], top[n][:, :],
                                            ALU.subtract).then_inc(lowered, 1)

                def cap(n, k):
                    dve.wait_ge(lowered, k + 1)
                    nc.vector.tensor_scalar(capped[n][:, :], below[n][:, :], 0.0, None, ALU.min
                                            ).then_inc(capped_ready, 1)

                def weighted_hot(n, c):
                    return nc.vector.tensor_scalar(hot[n % 4][:, c, :], g.iota[:, :], dlo[n][:, c:c + 1],
                                                   w[n][:, c:c + 1], ALU.is_equal, ALU.mult)

                for n in range(AHEAD + 1):
                    stage(n, n * HALF)
                for n in range(AHEAD):
                    find(n, n, two_blocks(nc, dve, g.blk_dst, n + 1, 5, NB - 1))
                    lower(n, n, n * HALF)
                    cap(n, n)
                with dve.Fori(0, loops) as i:
                    for n in range(RING):
                        k = RING * i + n
                        at = i * (RING * HALF) + n * HALF
                        next_n = (n + AHEAD) % RING
                        if n == 0:
                            b = two_blocks(nc, dve, g.blk_dst, k + AHEAD + 1, 5, NB - 1)
                        dve.wait_ge(hot_act, k + 1)
                        stage((n + AHEAD + 1) % RING, at + (AHEAD + 1) * HALF)
                        find(next_n, k + AHEAD, b)
                        if n + 1 < RING:
                            b = two_blocks(nc, dve, g.blk_dst, k + AHEAD + 2, 5, NB - 1)
                        dve.wait_ge(w_ready, k + 1)
                        dve.wait_ge(summed, k + RING - 3)
                        for c in range(ONES, HALF - 1):
                            weighted_hot(n, c)
                        lower(next_n, k + AHEAD, at + AHEAD * HALF)
                        weighted_hot(n, HALF - 1).then_inc(hot_dve, 1)
                        cap(next_n, k + AHEAD)

            @block.scalar
            def _(act):
                def weigh(n, k):
                    act.wait_ge(capped_ready, k + 1)
                    nc.scalar.activation(w[n][:, :], capped[n][:, :], ACT.Exp).then_inc(w_ready, 1)

                act.sem_inc(hot_act, AHEAD + 1)
                weigh(0, 0)
                with act.Fori(0, loops) as i:
                    for n in range(RING):
                        k = RING * i + n
                        act.wait_ge(dlo_ready, k + 1)
                        act.wait_ge(hot_act, k + AHEAD)
                        for c in range(ONES):
                            last = nc.scalar.activation(far[n % 2][:, c, :], g.iota[:, :], ACT.Abs,
                                                        bias=dlo[n][:, c:c + 1], scale=-1.0)
                        last.then_inc(far_ready, 1)
                        act.wait_ge(w_ready, k + 1)
                        nc.scalar.mul(minus_w[n][:, :], w[n][:, :], -1.0).then_inc(minus_ready, 1)
                        weigh((n + 1) % RING, k + 1)
                        act.wait_ge(far_ready, k + 1)
                        act.wait_ge(minus_ready, k + 1)
                        act.wait_ge(summed, k + RING - 3)
                        for c in range(ONES):
                            last = nc.scalar.activation(hot[n % 4][:, c, :], far[n % 2][:, c, :], ACT.Relu,
                                                        bias=w[n][:, c:c + 1], scale=minus_w[n][:, c:c + 1])
                        last.then_inc(hot_act, 1)

            @block.tensor
            def _(pe):
                pe.sem_inc(summed, RING - 1)
                open_sums(nc, pe, g, ps_sum).then_inc(summed, 1)
                with pe.Fori(0, loops) as i:
                    for n in range(RING):
                        k, q = RING * i + n, n % 2
                        col = two_blocks(nc, pe, g.col_dst, k + 1, 12, psum_column(NB - 1))
                        pe.wait_ge(hot_dve, k + 1)
                        pe.wait_ge(hot_act, k + AHEAD + 2)
                        pe.wait_ge(rows_ready[n // 2], 16 * i + 16)
                        add_sums(nc, pe, ps_sum, col, hot[n % 4], rows[n // 2][:, q * HALF:(q + 1) * HALF, 0:C + 1],
                                 C + 1).then_inc(summed, 1)

        take_sums(nc, f"gatsum{l}_take", ps_sum, out, C + 1)


def weighted_layer(nc, g):
    weigh_pass(nc, g)
    with Stage(nc, "wsum") as s:
        agg = s.sb("agg", [P, NB, C])
        stream_sum_pass(nc, g, "srcsum", g.sslots, SROWW, C, lambda rows, c, at: rows[:, c, C:SROWW], None, agg)
        node_product(nc, g, "wproj", agg, C, g.w_agg, [(0, C, g.h)])
        norm = s.sb("norm", [P, NB])
        step = s.sem("step")
        square = s.sem("square")
        root = s.sem("root")
        block = s.block()

        @block.scalar
        def _(act):
            act.wait_ge(square, 1)
            nc.scalar.activation(norm[:, :], norm[:, :], ACT.Sqrt).then_inc(root, 1)

        @block.vector
        def _(dve):
            link = chain(dve, step)
            link(nc.vector.tensor_tensor(g.h[:, :, :], g.h[:, :, :], g.b_agg.unsqueeze(1).to_broadcast([P, NB, C]),
                                         ALU.add))
            link(nc.vector.tensor_tensor(agg[:, :, :], g.h[:, :, :], g.h[:, :, :], ALU.mult))
            nc.vector.tensor_reduce(norm[:, :], agg[:, :, :], AX, ALU.add).then_inc(square, 1)
            dve.wait_ge(root, 1)
            link(nc.vector.tensor_scalar(norm[:, :], norm[:, :], 1e-12, None, ALU.max))
            link(nc.vector.reciprocal(norm[:, :], norm[:, :]))
            link(nc.vector.tensor_tensor(g.h[:, :, :], g.h[:, :, :], wide(norm[:, :], C), ALU.mult))


def store_table(nc, name, table, rows):
    with Stage(nc, name) as s:
        stored = s.sem("stored")
        block = s.block()

        @block.sync
        def _(sp):
            sp.dma_start(table.rearrange("(b p) w -> p b w", p=P), rows[:, :, :]).then_inc(stored, 16)
            sp.wait_ge(stored, 16)


def message_layer(nc, g):
    with Stage(nc, "msg") as s:
        pair = s.sb("pair", [P, NB, 2 * C])
        node_product(nc, g, "msgp", g.h, C, g.w_msg_node, [(0, C, pair[:, :, 0:C])])
        store_table(nc, "msgt", g.msg_table, pair[:, :, 0:C])
        message_pass(nc, g, pair[:, :, C:2 * C])
        with Stage(nc, "msgpair") as t:
            block = t.block()

            @block.vector
            def _(dve):
                nc.vector.tensor_copy(pair[:, :, 0:C], g.h[:, :, :])
        node_product(nc, g, "msgu", pair, 2 * C, g.w_upd, [(0, C, g.h)])
        step = s.sem("step")
        block = s.block()

        @block.vector
        def _(dve):
            link = chain(dve, step)
            link(nc.vector.tensor_tensor(g.h[:, :, :], g.h[:, :, :], g.b_upd.unsqueeze(1).to_broadcast([P, NB, C]),
                                         ALU.add))
            link(nc.vector.tensor_scalar(g.h[:, :, :], g.h[:, :, :], 0.0, None, ALU.max))


def gat_layer(nc, g, l):
    with Stage(nc, f"gat{l}") as s:
        table = s.sb("table", [P, NB, GW])
        tmp = s.sb("tmp", [P, NB, C])
        both = s.sb("both", [P, 2, NB])
        self_e = s.sb("self_e", [P, NB])
        g.top = s.sb("top", [P, NB])
        g.dst_rows = s.sb("dst_rows", [P, NB, P])
        g.edge_score = s.sb("edge_score", [P, CP])
        g.edge_leaky = s.sb("edge_leaky", [P, CP])
        agg = s.sb("agg", [P, NB, C + 1])
        node_product(nc, g, f"gatp{l}", g.h, C, g.w_gat[l], [(0, C, table[:, :, 0:C])])
        with Stage(nc, f"gatscore{l}") as t:
            step = t.sem("step")
            block = t.block()

            @block.vector
            def _(dve):
                link = chain(dve, step)
                nc.vector.memset(table[:, :, C:C + 1], 1.0)
                for a, to in ((g.a_src[l], table[:, :, C + 1]), (g.a_dst[l], both[:, 0, :])):
                    link(nc.vector.tensor_tensor(tmp[:, :, :], table[:, :, 0:C], a.unsqueeze(1).to_broadcast([P, NB, C]),
                                                 ALU.mult))
                    link(nc.vector.tensor_reduce(to, tmp[:, :, :], AX, ALU.add))
                link(nc.vector.tensor_copy(g.top[:, :], table[:, :, C + 1]))
        store_table(nc, f"gatt{l}", g.gat_table, table)
        spread_nodes(nc, g, f"gatdst{l}", both[:, 0, :], g.dst_rows)
        gat_max_pass(nc, g, l)
        with Stage(nc, f"gattop{l}") as t:
            step = t.sem("step")
            block = t.block()

            @block.vector
            def _(dve):
                link = chain(dve, step)

                def leaky(to, a, b):
                    link(nc.vector.tensor_tensor(tmp[:, :, 0], a, b, ALU.add))
                    link(nc.vector.scalar_tensor_tensor(to, tmp[:, :, 0], 0.2, tmp[:, :, 0], ALU.mult, ALU.max))
                leaky(both[:, 1, :], g.top[:, :], both[:, 0, :])
                leaky(self_e[:, :], table[:, :, C + 1], both[:, 0, :])
        spread_nodes(nc, g, f"gattopr{l}", both[:, 1, :], g.dst_rows)
        with Stage(nc, f"gatorder{l}") as t:
            exp_in = t.sem("exp_in")
            block = t.block()

            @block.vector
            def _(dve):
                nc.vector.tensor_tensor(self_e[:, :], self_e[:, :], both[:, 1, :], ALU.subtract).then_inc(exp_in, 1)

            @block.scalar
            def _(act):
                act.wait_ge(exp_in, 1)
                nc.scalar.activation(self_e[:, :], self_e[:, :], ACT.Exp)
        gat_sum_pass(nc, g, l, agg)
        step = s.sem("step")
        block = s.block()

        @block.vector
        def _(dve):
            link = chain(dve, step)
            link(nc.vector.tensor_tensor(tmp[:, :, :], table[:, :, 0:C], wide(self_e[:, :], C), ALU.mult))
            link(nc.vector.tensor_tensor(agg[:, :, 0:C], agg[:, :, 0:C], tmp[:, :, :], ALU.add))
            link(nc.vector.tensor_tensor(self_e[:, :], self_e[:, :], agg[:, :, C], ALU.add))
            link(nc.vector.tensor_scalar(self_e[:, :], self_e[:, :], 1e-16, None, ALU.add))
            link(nc.vector.reciprocal(self_e[:, :], self_e[:, :]))
            link(nc.vector.tensor_tensor(g.h[:, :, :], agg[:, :, 0:C], wide(self_e[:, :], C), ALU.mult))
            link(nc.vector.tensor_tensor(g.h[:, :, :], g.h[:, :, :], g.b_gat[l].unsqueeze(1).to_broadcast([P, NB, C]),
                                         ALU.add))
            if l == 0:
                link(nc.vector.tensor_scalar(g.h[:, :, :], g.h[:, :, :], 0.0, None, ALU.max))



class Held:
    pass


NVEC = 2 * 3 + 8 + 1
(V_SEMW, V_LNG, V_LNB, V_AGGB, V_MSGB, V_UPDB, V_GATB, V_ASRC, V_ADST) = (0, 2, 4, 6, 7, 8, 9, 11, 13)


def build(nc, d, out, stop=None):
    g = Held()
    ctx = ExitStack()
    with ctx:
        def sb(name, shape, dt=F32):
            return ctx.enter_context(nc.sbuf_tensor(name, shape, dt))

        g.x = sb("x", [P, NB, C])
        g.h = sb("h", [P, NB, C])
        g.own = sb("own", [P, NB, C])
        g.meta = sb("meta", [P, CP, META])
        g.blk_dst = sb("blk_dst", [1, 1 + NPK], I32)
        g.col_dst = sb("col_dst", [1, 1 + NPK], I32)
        g.blk_src = sb("blk_src", [1, 1 + NPK], I32)
        g.col_src = sb("col_src", [1, 1 + NPK], I32)
        g.ident = sb("ident", [P, P])
        g.iota = sb("iota", [P, P])
        g.before = sb("before", [P, P])
        g.no_node = sb("no_node", [P, 1])
        g.ident_b = sb("ident_b", [P, P], BF16)
        g.iota_b = sb("iota_b", [P, P], BF16)
        g.zeros = sb("zeros", [P, BANK])
        g.ones = sb("ones", [P, P])
        g.pair_slot = sb("pair_slot", [NB, CP // PAIR])
        g.w_rel_t = sb("w_rel_t", [C, 2, R * (TW + C) + C])
        g.w_cat_t = sb("w_cat_t", [P, 4, P])
        g.vec = sb("vec", [P, NVEC, C])
        g.sem_b = sb("sem_b", [P, 2])
        g.w_agg = sb("w_agg", [C, C])
        g.w_msg_edge = sb("w_msg_edge", [C, C])
        g.w_msg_node = sb("w_msg_node", [C, C])
        g.w_upd = sb("w_upd", [2 * C, C])
        g.w_gat_t = sb("w_gat_t", [C, 2, C])
        g.w_rel = [g.w_rel_t[:, l, :] for l in range(2)]
        g.w_cat = [[g.w_cat_t[:, 2 * l + j, :] for j in range(2)] for l in range(2)]
        g.w_gat = [g.w_gat_t[:, l, :] for l in range(2)]
        vec = lambda i: g.vec[:, i, :]
        g.sem_w = [vec(V_SEMW + l) for l in range(2)]
        g.ln_g = [vec(V_LNG + l) for l in range(2)]
        g.ln_b = [vec(V_LNB + l) for l in range(2)]
        g.b_agg, g.b_msg, g.b_upd = vec(V_AGGB), vec(V_MSGB), vec(V_UPDB)
        g.b_gat = [vec(V_GATB + l) for l in range(2)]
        g.a_src = [vec(V_ASRC + l) for l in range(2)]
        g.a_dst = [vec(V_ADST + l) for l in range(2)]
        dram = lambda name, shape: nc.dram_tensor(name, shape, F32).ap()
        g.slots = dram("slots", [ROWS, ROWW])
        g.sslots = dram("sslots", [ROWS, SROWW])
        g.rel_table = dram("rel_table", [R * NPAD, TW])
        g.msg_table = dram("msg_table", [NPAD, C])
        g.gat_table = dram("gat_table", [NPAD, GW])
        g.gat_rows = dram("gat_rows", [ROWS, GW])
        g.node_row = dram("node_row", [NB, P])
        g.attr = d["attr"]

        with ExitStack() as routing:
            def tmp(name, shape, dt=F32):
                return routing.enter_context(nc.sbuf_tensor(name, shape, dt))
            g.src_i = tmp("src_i", [P, EC], I32)
            g.dst_i = tmp("dst_i", [P, EC], I32)
            g.typ_i = tmp("typ_i", [P, EC], I32)
            g.weight0 = tmp("weight0", [P, EC])
            g.absent = tmp("absent", [P, EC])
            g.meta0 = tmp("meta0", [P, EC, META])
            g.row0 = tmp("row0", [P, EC], I32)
            g.fill = tmp("fill", [P, TURN, ROWW])
            g.sfill = tmp("sfill", [P, TURN, SROWW])
            load_constants(nc, g, [
                (g.src_i[:, :], d["src"]), (g.dst_i[:, :], d["dst"]), (g.typ_i[:, :], d["typ"]),
                (g.absent[:, :], d["absent"]), (g.weight0[:, :], d["weight"]), (g.iota[:, :], d["iota"]),
                (g.before[:, :], d["before"]), (g.ident[:, :], d["ident"]), (g.pair_slot[:, :], d["pair_slot"]),
                (g.x[:, :, :], d["x"].rearrange("(b p) c -> p b c", p=P)),
                (g.h[:, :, :], d["x"].rearrange("(b p) c -> p b c", p=P)),
                (g.no_node[:, :], d["no_node"]), (g.w_rel_t[:, :, :], d["w_rel"]), (g.w_cat_t[:, :, :], d["w_cat"]),
                (g.vec[:, :, :], d["vectors"]), (g.sem_b[:, :], d["sem_b"]), (g.w_agg[:, :], d["w_agg"]),
                (g.w_msg_edge[:, :], d["w_msg_edge"]), (g.w_msg_node[:, :], d["w_msg_node"]),
                (g.w_upd[:, :], d["w_upd"]), (g.w_gat_t[:, :, :], d["w_gat"])])
            fill_tables(nc, g)
            route(nc, g)
            scatter_edges(nc, g)
        if stop == "scatter":
            return finish(nc, g, out, g.x)
        with ExitStack() as relations:
            def tmp(name, shape, dt=F32):
                return relations.enter_context(nc.sbuf_tensor(name, shape, dt))
            g.mask = tmp("mask", [P, CP, R])
            load_meta(nc, g)
            for l in range(2):
                with nc.sbuf_tensor(f"acc{l}", [P, NB, R * C + R * H], F32) as acc:
                    g.acc = acc
                    with nc.sbuf_tensor(f"q_split{l}", [P, 3, NB, R * C], BF16) as q_split:
                        g.q_split = q_split
                        relation_products(nc, g, l)
                        relation_pass(nc, g, l)
                    relation_nodes(nc, g, l)
                if stop == f"rel{l}":
                    return finish(nc, g, out, g.h)
            residual_norm(nc, g, "res0")
        if stop == "res0":
            return finish(nc, g, out, g.x)
        weighted_layer(nc, g)
        residual_norm(nc, g, "res1")
        if stop == "res1":
            return finish(nc, g, out, g.x)
        message_layer(nc, g)
        residual_norm(nc, g, "res2")
        if stop == "res2":
            return finish(nc, g, out, g.x)
        for l in range(2):
            gat_layer(nc, g, l)
        residual_norm(nc, g, "res3")
        finish(nc, g, out, g.x)


def finish(nc, g, out, what):
    with Stage(nc, "store") as s:
        stored = s.sem("stored")
        block = s.block()

        @block.sync
        def _(sp):
            full = (NB - 1) * P
            sp.dma_start(out[0:full, :].rearrange("(b p) c -> p b c", p=P), what[:, 0:NB - 1, :]).then_inc(stored, 16)
            sp.dma_start(out[full:N, :], what[0:LAST, NB - 1, :]).then_inc(stored, 16)
            sp.wait_ge(stored, 32)


STOP = None


def kernel(**inputs):
    import numpy as np
    from concourse import bacc
    from concourse.bass_utils import run_bass_kernel_spmd

    a = {k: np.asarray(v) for k, v in inputs.items()}
    f = np.float32

    def lanes(v):
        o = np.zeros(P * EC, v.dtype)
        o[:E] = v
        return o.reshape(P, EC)

    attr = np.zeros((P * EC, C), f)
    attr[:E] = a["edge_attr_64"]
    x = np.zeros((NPAD, C), f)
    x[:N] = a["x"]
    w_rel = np.zeros((C, 2, R * (TW + C) + C), f)
    w_cat = np.zeros((P, 4, P), f)
    for l in range(2):
        cols = lambda w, r: a[w][l, r].transpose(1, 0, 2).reshape(C, C)
        for r in range(R):
            w_rel[:, l, r * TW:r * TW + C] = cols("L0_gnn_W_K", r)
            w_rel[:, l, r * TW + C:(r + 1) * TW] = cols("L0_gnn_W_V", r)
            w_rel[:, l, R * TW + r * C:R * TW + (r + 1) * C] = cols("L0_gnn_W_Q", r)
            j, k = divmod(r, 2)
            w_cat[k * C:(k + 1) * C, 2 * l + j, k * C:(k + 1) * C] = a["L0_gnn_W_concat"][l, r]
        w_rel[:, l, R * (TW + C):] = a["L0_gnn_W_self"][l]
    vectors = [a["L0_gnn_sem_w"][0], a["L0_gnn_sem_w"][1], a["L0_gnn_ln_g"][0], a["L0_gnn_ln_g"][1],
               a["L0_gnn_ln_b"][0], a["L0_gnn_ln_b"][1], a["L1_gnn_bias"], a["L2_gnn_M_b"], a["L2_gnn_U_b"],
               a["L3_gnn_b1"], a["L3_gnn_b2"], a["L3_gnn_a_src1"], a["L3_gnn_a_src2"], a["L3_gnn_a_dst1"],
               a["L3_gnn_a_dst2"]]
    order = np.arange(P)
    arrays = {
        "x": x, "src": lanes(a["src"]), "dst": lanes(a["dst"]), "typ": lanes(a["edge_type_4"]),
        "weight": lanes(a["edge_weight"]),
        "attr": np.ascontiguousarray(attr.reshape(P, EC, C).transpose(2, 1, 0)).reshape(C, EC * P),
        "absent": (np.arange(P * EC) >= E).astype(f).reshape(P, EC),
        "no_node": np.where(order >= LAST, -BIG, 0.0).astype(f)[:, None],
        "ident": np.eye(P, dtype=f), "iota": np.broadcast_to(order.astype(f), (P, P)).copy(),
        "before": (order[:, None] < order[None, :]).astype(f),
        "pair_slot": np.broadcast_to(np.arange(CP // PAIR, dtype=f) * (PAIR * P), (NB, CP // PAIR)).copy(),
        "w_rel": w_rel, "w_cat": w_cat,
        "vectors": np.ascontiguousarray(np.broadcast_to(np.stack(vectors), (P, NVEC, C))),
        "sem_b": np.ascontiguousarray(np.broadcast_to(a["L0_gnn_sem_b"], (P, 2))),
        "w_agg": a["L1_gnn_weight"],
        "w_msg_node": np.ascontiguousarray(a["L2_gnn_M_W"][:, :C].T),
        "w_msg_edge": np.ascontiguousarray(a["L2_gnn_M_W"][:, C:].T),
        "w_upd": np.ascontiguousarray(a["L2_gnn_U_W"].T),
        "w_gat": np.ascontiguousarray(np.stack([a["L3_gnn_W1"], a["L3_gnn_W2"]], axis=1)),
    }
    nc = bacc.Bacc("TRN2", target_bir_lowering=False, num_devices=1)
    d = {k: nc.dram_tensor(f"in_{k}", v.shape, mybir.dt.from_np(v.dtype), kind="ExternalInput").ap()
         for k, v in arrays.items()}
    out = nc.dram_tensor("out_x", (N, C), F32, kind="ExternalOutput").ap()
    build(nc, d, out, STOP)
    r = run_bass_kernel_spmd(nc, [{f"in_{k}": v for k, v in arrays.items()}], core_ids=[0])
    return r.results[0]["out_x"]
```

```python
from contextlib import ExitStack

import concourse.bass as bass
from concourse import mybir

P = 128
N = 3125
NB = -(-N // P)
NPAD = NB * P
LAST = N - (NB - 1) * P
E = 103125
C = 64
R = 4
H = 8
D = C // H
EC = 808
HALF = 4
DEPTH = 4
TURN = DEPTH * HALF
ETURN = 2 * HALF
PAIR = 2
PAIRS = (E - NB) // (PAIR * P) + NB
NC = -(-PAIRS * PAIR // TURN) * TURN
TURNS = NC // TURN
CP = NC + TURN
NPK = CP // HALF
ROWS = P * CP
META = 8
ROWW = C + META
(M_REL, M_SRC, M_DLO, M_TYPE, M_WEIGHT, M_SROW, M_SLO, M_SPARE) = range(META)
NOWHERE = 1 << 20
NOBODY = 200.0
SROWW = C + 1
TW = 2 * C
GW = C + 2
BANK = 512
UC = BANK // 7
BIG = 1.0e30
assert P * EC >= E and EC % ETURN == 0 and NPAD >= N

F32 = mybir.dt.float32
BF16 = mybir.dt.bfloat16
I32 = mybir.dt.int32
ALU = mybir.AluOpType
ACT = mybir.ActivationFunctionType
AX = mybir.AxisListType.X
IN_RANGE = "worked out on the chip from 25 blocks, so it is below that"


def psum_column(b):
    return b // 7 * BANK + b % 7 * UC


class Stage:

    def __init__(self, nc, name):
        self.nc, self.name, self.ctx, self.sems = nc, name, ExitStack(), []

    def __enter__(self):
        self.ctx.__enter__()
        return self

    def __exit__(self, *a):
        said = self.ctx.__exit__(*a)
        if self.sems and a[0] is None:
            self.nc.clear_and_free_semaphores(self.sems)
            self.nc.all_engine_barrier()
        return said

    def sb(self, name, shape, dt=F32):
        return self.ctx.enter_context(self.nc.sbuf_tensor(f"{self.name}_{name}", shape, dt))

    def ps(self, name, shape, dt=F32):
        return self.ctx.enter_context(self.nc.psum_tensor(f"{self.name}_ps_{name}", shape, dt))

    def sem(self, name):
        self.sems.append(self.nc.alloc_semaphore(f"{self.name}_sem_{name}"))
        return self.sems[-1]

    def block(self):
        return self.ctx.enter_context(self.nc.Block())


def chain(engine, sem):
    count = [0]

    def link(instruction):
        count[0] += 1
        instruction.then_inc(sem, 1)
        engine.wait_ge(sem, count[0])
    return link


def wide(ap, n):
    return ap.unsqueeze(len(ap.shape)).to_broadcast([*ap.shape, n])


def load_constants(nc, g, src):
    with Stage(nc, "load") as s:
        loaded = s.sem("loaded")
        block = s.block()

        @block.sync
        def _(sp):
            n = 0
            for to, of in src:
                sp.dma_start(to, of).then_inc(loaded, 16)
                n += 16
            sp.wait_ge(loaded, n)

        @block.vector
        def _(dve):
            nc.vector.memset(g.ones[:, :], 1.0)
            nc.vector.memset(g.zeros[:, :], 0.0)
            nc.vector.memset(g.fill[:, :, :], 0.0)


def fill_tables(nc, g):
    with Stage(nc, "fill") as s:
        block = s.block()

        @block.vector
        def _(dve):
            nc.vector.memset(g.fill[:, :, C + M_DLO:C + M_DLO + 1], NOBODY)
            nc.vector.memset(g.fill[:, :, C + M_SLO:C + M_SLO + 1], NOBODY)
            nc.vector.memset(g.fill[:, :, C + M_SROW:C + M_SROW + 1].bitcast(I32), NOWHERE)
            nc.vector.memset(g.sfill[:, :, 0:C], 0.0)
            nc.vector.memset(g.sfill[:, :, C:C + 1], NOBODY)
            nc.vector.tensor_copy(g.ident_b[:, :], g.ident[:, :])


def route(nc, g):
    RING = 5
    PLACE = (0, 1, 0, 1, 2)
    KEYS = range(2)
    with Stage(nc, "route") as s:
        two = lambda name, shape, dt=F32: [s.sb(f"{name}{k}", shape, dt) for k in KEYS]
        hi_i = s.sb("hi_i", [P, EC], I32)
        lo_i = s.sb("lo_i", [P, EC], I32)
        hi = two("hi", [P, EC])
        ones = s.sb("ones", [P, EC])
        far = [s.sb(f"far{r}", [P, EC]) for r in range(3)]
        eq = [s.sb(f"eq{r}", [P, EC]) for r in range(RING)]
        cum = [s.sb(f"cum{r}", [P, EC]) for r in range(RING)]
        hit = [s.sb(f"hit{r}", [P, EC]) for r in range(RING)]
        cnt = two("cnt", [P, 32])
        base = two("base", [P, 32])
        padded_i = two("padded_i", [NB, 1], I32)
        padded = two("padded", [NB, 1])
        start = two("start", [NB, 1])
        diag = two("diag", [NB, NB])
        begun = two("begun", [NB, CP // PAIR])
        blk = s.sb("blk", [1, CP // PAIR])
        bank_no = s.sb("bank_no", [1, CP // PAIR])
        col = s.sb("col", [1, CP // PAIR])
        ps_tot = s.ps("tot", [NB, 2])
        ps_base = s.ps("base", [P, NB])
        ps_start = s.ps("start", [NB, 2])
        ps_blk = s.ps("blk", [1, CP // PAIR])
        ps_rank = [s.ps(f"rank{k}", [P, 2 * BANK]) for k in KEYS]
        filled = s.sem("filled")
        step = s.sem("step")
        keyed = s.sem("keyed")
        tallied = s.sem("tallied")
        counted = s.sem("counted")
        totals = s.sem("totals")
        rounded = s.sem("rounded")
        started = s.sem("started")
        diagonal = s.sem("diagonal")
        based = s.sem("based")
        based_taken = s.sem("based_taken")
        begun_ready = s.sem("begun_ready")
        blocks = s.sem("blocks")
        blocks_taken = s.sem("blocks_taken")
        measured = s.sem("measured")
        eq_ready = s.sem("eq_ready")
        scanned = s.sem("scanned")
        hit_ready = s.sem("hit_ready")
        ranked = s.sem("ranked")
        block = s.block()
        pieces = [(0, BANK), (BANK, EC)]

        @block.sync
        def _(sp):
            n = CP // TURN
            sp.dma_start(g.slots.rearrange("(p n u) w -> p n (u w)", p=P, n=n),
                         g.fill[:, :, :].rearrange("p u w -> p (u w)").unsqueeze(1)
                         .to_broadcast([P, n, TURN * ROWW])).then_inc(filled, 16)
            sp.dma_start(g.sslots.rearrange("(p n u) w -> p n (u w)", p=P, n=n),
                         g.sfill[:, :, :].rearrange("p u w -> p (u w)").unsqueeze(1)
                         .to_broadcast([P, n, TURN * SROWW])).then_inc(filled, 16)
            sp.wait_ge(filled, 32)

        @block.scalar
        def _(act):
            act.sem_inc(measured, 2)
            act.sem_inc(eq_ready, 2)
            for k in KEYS:
                act.wait_ge(keyed, k + 1)
                with act.Fori(0, NB // RING) as i:
                    for r in range(RING):
                        b, j = i * RING + r, i * RING + (k * NB + r)
                        act.wait_ge(eq_ready, j + 1)
                        nc.scalar.activation(far[PLACE[r]][:, :], hi[k][:, :], ACT.Abs, bias=g.iota[:, bass.ds(b, 1)],
                                             scale=-1.0).then_inc(measured, 1)
                        act.wait_ge(measured, j + 3)
                        act.wait_ge(hit_ready, j + 1)
                        nc.scalar.activation(eq[r][:, :], far[PLACE[r]][:, :], ACT.Relu, bias=g.ones[:, 0:1],
                                             scale=-1.0).then_inc(eq_ready, 1)

        @block.tensor
        def _(pe):
            pe.sem_inc(ranked, RING)
            for k in KEYS:
                for c0, c1 in pieces:
                    nc.tensor.matmul(ps_rank[k][:, c0:c1], g.zeros[:, 0:P], g.zeros[:, 0:c1 - c0],
                                     start=True, stop=True, skip_group_check=True)
            for k in KEYS:
                pe.wait_ge(counted, k + 1)
                nc.tensor.matmul(ps_tot[:, k:k + 1], cnt[k][:, 0:NB], g.ones[:, 0:1],
                                 start=True, stop=True).then_inc(totals, 1)
            for k in KEYS:
                pe.wait_ge(rounded, k + 1)
                nc.tensor.matmul(ps_start[:, k:k + 1], g.before[0:NB, 0:NB], padded[k][:, :],
                                 start=True, stop=True).then_inc(started, 1)
            for k in KEYS:
                pe.wait_ge(diagonal, k + 1)
                if k > 0:
                    pe.wait_ge(based_taken, k)
                nc.tensor.matmul(ps_base[:, :], g.before[:, :], cnt[k][:, 0:NB], start=True, stop=False)
                nc.tensor.matmul(ps_base[:, :], g.ones[0:NB, :], diag[k][:, :],
                                 start=False, stop=True).then_inc(based, 1)
            for k in KEYS:
                if k > 0:
                    pe.wait_ge(blocks_taken, k)
                pe.wait_ge(begun_ready, k + 1)
                nc.tensor.matmul(ps_blk[:, :], g.ones[0:NB, 0:1], begun[k][:, :],
                                 start=True, stop=True).then_inc(blocks, 1)
                with pe.Fori(0, NB // RING) as i:
                    for r in range(RING):
                        pe.wait_ge(hit_ready, i * RING + (k * NB + r + 1 + RING))
                        for c0, c1 in pieces:
                            last = nc.tensor.matmul(ps_rank[k][:, c0:c1], g.ident[:, :], hit[r][:, c0:c1],
                                                    start=False, stop=True, skip_group_check=True)
                        last.then_inc(ranked, 1)

        @block.vector
        def _(dve):
            link = chain(dve, step)
            dve.sem_inc(tallied, RING)
            dve.sem_inc(hit_ready, RING)
            plan = [(g.dst_i, g.blk_dst, g.col_dst, M_DLO, None), (g.src_i, g.blk_src, None, M_SLO, M_SROW)]
            link(nc.vector.memset(ones[:, :], 1.0))
            for k, (key, blk_out, col_out, m_lo, m_row) in enumerate(plan):
                link(nc.vector.tensor_scalar(hi_i[:, :], key[:, :], 7, None, ALU.logical_shift_right))
                link(nc.vector.tensor_copy(hi[k][:, :], hi_i[:, :]))
                link(nc.vector.scalar_tensor_tensor(hi[k][:, :], g.absent[:, :], 100.0, hi[k][:, :], ALU.mult, ALU.add))
                dve.sem_inc(keyed, 1)
                link(nc.vector.tensor_scalar(lo_i[:, :], key[:, :], P - 1, None, ALU.bitwise_and))
                link(nc.vector.tensor_copy(g.meta0[:, :, m_lo], lo_i[:, :]))
            for k in KEYS:
                with dve.Fori(0, NB // RING) as i:
                    for r in range(RING):
                        b, j = i * RING + r, i * RING + (k * NB + r)
                        dve.wait_ge(tallied, j + 1)
                        nc.vector.scalar_tensor_tensor(cum[r][:, :], hi[k][:, :], g.iota[:, bass.ds(b, 1)], ones[:, :],
                                                       ALU.is_equal, ALU.mult, accum_out=cnt[k][:, bass.ds(b, 1)]
                                                       ).then_inc(tallied, 1)
                dve.wait_ge(tallied, (k + 1) * NB + RING)
                dve.sem_inc(counted, 1)
            dve.wait_ge(totals, 2)
            for k in KEYS:
                link(nc.vector.tensor_scalar(padded_i[k][:, :], ps_tot[:, k:k + 1], float(PAIR * P - 1), None, ALU.add))
                link(nc.vector.tensor_scalar(padded_i[k][:, :], padded_i[k][:, :], 8, 8,
                                             ALU.logical_shift_right, ALU.logical_shift_left))
                nc.vector.tensor_copy(padded[k][:, :], padded_i[k][:, :]).then_inc(rounded, 1)
            dve.wait_ge(started, 2)
            for k in KEYS:
                link(nc.vector.tensor_copy(start[k][:, :], ps_start[:, k:k + 1]))
                nc.vector.tensor_scalar(diag[k][:, :], g.ident[0:NB, 0:NB], start[k][:, 0:1], None,
                                        ALU.mult).then_inc(diagonal, 1)
                nc.vector.tensor_scalar(begun[k][:, :], g.pair_slot[:, :], start[k][:, 0:1], None,
                                        ALU.is_ge).then_inc(begun_ready, 1)
            for k in KEYS:
                dve.wait_ge(based, k + 1)
                nc.vector.tensor_scalar(base[k][:, 0:NB], ps_base[:, :], -1.0, None, ALU.add).then_inc(based_taken, 1)
            dve.wait_ge(based_taken, 2)
            for k, (key, blk_out, col_out, m_lo, m_row) in enumerate(plan):
                with dve.Fori(0, NB // RING) as i:
                    def scan(r):
                        j = i * RING + (k * NB + r)
                        dve.wait_ge(eq_ready, j + 3)
                        dve.wait_ge(hit_ready, j + 1)
                        nc.vector.tensor_tensor_scan(cum[r][:, :], ones[:, :], eq[r][:, :], 0.0,
                                                     ALU.mult, ALU.add).then_inc(scanned, 1)

                    def place(r):
                        b, j = i * RING + r, i * RING + (k * NB + r)
                        dve.wait_ge(scanned, j + 1)
                        dve.wait_ge(ranked, j + 1)
                        nc.vector.scalar_tensor_tensor(hit[r][:, :], cum[r][:, :], base[k][:, bass.ds(b, 1)],
                                                       eq[r][:, :], ALU.add, ALU.mult).then_inc(hit_ready, 1)

                    scan(0)
                    for r in range(1, RING):
                        scan(r)
                        place(r - 1)
                    place(RING - 1)
                dve.wait_ge(blocks, k + 1)
                nc.vector.tensor_scalar(blk[:, :], ps_blk[:, :], -1.0, None, ALU.add).then_inc(blocks_taken, 1)
                dve.wait_ge(blocks_taken, k + 1)
                packed = [(blk, blk_out, 5)]
                if col_out is not None:
                    packed.append((col, col_out, 12))
                    link(nc.vector.tensor_scalar(bank_no[:, :], blk[:, :], 7.0, None, ALU.is_ge))
                    for edge in (14.0, 21.0):
                        link(nc.vector.scalar_tensor_tensor(bank_no[:, :], blk[:, :], edge, bank_no[:, :], ALU.is_ge, ALU.add))
                    link(nc.vector.tensor_scalar(bank_no[:, :], bank_no[:, :], float(BANK - 7 * UC), None, ALU.mult))
                    link(nc.vector.scalar_tensor_tensor(col[:, :], blk[:, :], float(UC), bank_no[:, :], ALU.mult, ALU.add))
                for of, to, shift in packed:
                    both = of[:, :].rearrange("a (h j) -> a h j", j=PAIR)
                    link(nc.vector.memset(to[:, 0:1], 0))
                    link(nc.vector.scalar_tensor_tensor(to[:, 1:1 + NPK], both[:, :, 1], float(1 << shift),
                                                        both[:, :, 0], ALU.mult, ALU.add))
                dve.wait_ge(ranked, (k + 1) * NB + RING)
                link(nc.vector.tensor_copy(hi_i[:, :], ps_rank[k][:, 0:EC]))
                link(nc.vector.tensor_scalar(lo_i[:, :], hi_i[:, :], P - 1, None, ALU.bitwise_and))
                link(nc.vector.tensor_scalar(hi_i[:, :], hi_i[:, :], 7, None, ALU.logical_shift_right))
                chunk = hi[k]
                link(nc.vector.tensor_copy(chunk[:, :], hi_i[:, :]))
                link(nc.vector.scalar_tensor_tensor(chunk[:, :], lo_i[:, :], float(CP), chunk[:, :], ALU.mult, ALU.add))
                to = g.row0[:, :] if m_row is None else g.meta0[:, :, m_row].bitcast(I32)
                link(nc.vector.scalar_tensor_tensor(to, g.absent[:, :], float(NOWHERE), chunk[:, :], ALU.mult, ALU.add))
            typ, src = cum[0], cum[1]
            link(nc.vector.tensor_copy(typ[:, :], g.typ_i[:, :]))
            link(nc.vector.tensor_copy(g.meta0[:, :, M_TYPE], typ[:, :]))
            link(nc.vector.tensor_copy(src[:, :], g.src_i[:, :]))
            link(nc.vector.scalar_tensor_tensor(g.meta0[:, :, M_REL].bitcast(I32), typ[:, :], float(NPAD), src[:, :],
                                                ALU.mult, ALU.add))
            link(nc.vector.tensor_copy(g.meta0[:, :, M_SRC].bitcast(I32), src[:, :]))
            link(nc.vector.tensor_copy(g.meta0[:, :, M_WEIGHT], g.weight0[:, :]))
            link(nc.vector.memset(g.meta0[:, :, M_SPARE:M_SPARE + 1], 0.0))


def scatter_edges(nc, g):
    with Stage(nc, "scatter") as s:
        chan = [s.sb(f"chan{h}", [C, HALF * P]) for h in range(2)]
        row = [s.sb(f"row{h}", [P, HALF, ROWW]) for h in range(2)]
        to = [s.sb(f"to{h}", [P, HALF], I32) for h in range(2)]
        ps = [s.ps(f"msg{h}", [P, HALF, C]) for h in range(2)]
        chan_ready = [s.sem(f"chan_ready{h}") for h in range(2)]
        msg_ready = s.sem("msg_ready")
        row_ready = s.sem("row_ready")
        scattered = [s.sem(f"scattered{h}") for h in range(2)]
        row_free = s.sem("row_free")
        opened = s.sem("opened")
        block = s.block()

        @block.sync
        def _(sp):
            sp.sem_inc(row_free, 2)
            with sp.Fori(0, EC // ETURN) as i:
                for h in range(2):
                    sp.wait_ge(msg_ready, 2 * i + h + 1)
                    sp.dma_start(chan[h][:, :], g.attr[:, bass.ds(i * (ETURN * P) + h * HALF * P, HALF * P)]
                                 ).then_inc(chan_ready[h], 16)

        @block.scalar
        def _(act):
            with act.Fori(0, EC // ETURN) as i:
                for h in range(2):
                    act.wait_ge(scattered[h], 16 * HALF * i + 16 * HALF)
                    act.sem_inc(row_free, 1)

        @block.tensor
        def _(pe):
            pe.sem_inc(msg_ready, 2)
            with pe.Fori(0, EC // ETURN) as i:
                for h in range(2):
                    pe.wait_ge(chan_ready[h], 16 * i + 16)
                    pe.wait_ge(row_ready, 2 * i + h + 1)
                    for c in range(HALF):
                        last = nc.tensor.matmul(ps[h][:, c, :], chan[h][:, c * P:(c + 1) * P], g.w_msg_edge[:, :],
                                                start=True, stop=True)
                    last.then_inc(msg_ready, 1)

        @block.vector
        def _(dve):
            dve.sem_inc(row_ready, 2)
            with dve.Fori(0, EC // ETURN) as i:
                for h in range(2):
                    k = 2 * i + h
                    at = i * ETURN + h * HALF
                    dve.wait_ge(msg_ready, k + 3)
                    dve.wait_ge(row_free, k + 1)
                    nc.vector.tensor_tensor(row[h][:, :, 0:C], ps[h][:, :, :],
                                            g.b_msg[:, :].unsqueeze(1).to_broadcast([P, HALF, C]), ALU.add)
                    nc.vector.tensor_copy(row[h][:, :, C:ROWW], g.meta0[:, bass.ds(at, HALF), :])
                    nc.vector.tensor_copy(to[h][:, :], g.row0[:, bass.ds(at, HALF)]).then_inc(row_ready, 1)

        @block.gpsimd
        def _(pool):
            with pool.Fori(0, EC // ETURN) as i:
                for h in range(2):
                    pool.wait_ge(row_ready, 2 * i + h + 3)
                    pool.sem_inc(opened, 1)
                    for c in range(HALF):
                        pool.indirect_dma_start(g.slots, bass.IndirectOffsetOnAxis(ap=to[h][:, c:c + 1], axis=0),
                                                row[h][:, c, :], None, bounds_check=ROWS - 1, oob_is_err=False
                                                ).then_inc(scattered[h], 16)
            for h in range(2):
                pool.wait_ge(scattered[h], 16 * HALF * (EC // ETURN))


def load_meta(nc, g):
    def program(sp, loaded):
        rows = g.slots.rearrange("(p n) w -> p n w", p=P)
        sp.dma_start(g.meta[:, :, :], rows[:, :, C:ROWW]).then_inc(loaded, 16)
        sp.wait_ge(loaded, 16)
    return program


def node_product(nc, g, name, src, width, weight, outs, beside=None):
    GROUP = 5
    GROUPS = NB // GROUP
    units = [(b, o) for b in range(GROUP) for o in outs]
    U = len(units)
    with Stage(nc, name) as s:
        rows = s.sb("rows", [P, GROUP, width])
        cols = s.sb("cols", [width, GROUP, P])
        ps_t = s.ps("t", [width, GROUP, P])
        ps = [s.ps(f"p{j}", [P, BANK]) for j in range(4)]
        rows_ready = s.sem("rows_ready")
        opened = s.sem("opened")
        turned = s.sem("turned")
        cols_ready = s.sem("cols_ready")
        product = s.sem("product")
        taken = s.sem("taken")
        loaded = s.sem("loaded")
        block = s.block()

        if beside is not None:
            @block.sync
            def _(sp):
                beside(sp, loaded)

        @block.vector
        def _(dve):
            with dve.Fori(0, GROUPS) as i:
                dve.wait_ge(turned, i + 1)
                nc.vector.tensor_copy(rows[:, :, :], src[:, bass.ds(i * GROUP, GROUP), :]).then_inc(rows_ready, 1)

        @block.tensor
        def _(pe):
            pe.sem_inc(turned, 1)

            def turn(i):
                pe.wait_ge(rows_ready, i + 1)
                pe.wait_ge(cols_ready, i + 1)
                pe.sem_inc(opened, 1)
                for b in range(GROUP):
                    last = nc.tensor.transpose(ps_t[:, b, :], rows[:, b, :], g.ident[:, :])
                last.then_inc(turned, 1)

            def multiply(i):
                pe.wait_ge(cols_ready, i + 2)
                for u, (b, (c0, c1, to)) in enumerate(units):
                    before = u - 4 if u >= 4 else max(v for v in range(U) if v % 4 == u % 4) - U if U > u else 0
                    pe.wait_ge(taken, i * U + (before + 1 + U))
                    nc.tensor.matmul(ps[u % 4][:, 0:c1 - c0], cols[:, b, :], weight[:, c0:c1],
                                     start=True, stop=True).then_inc(product, 1)

            turn(0)
            with pe.Fori(0, GROUPS - 1) as i:
                turn(i + 1)
                multiply(i)
            multiply(GROUPS - 1)

        @block.scalar
        def _(act):
            def columns(i):
                act.wait_ge(turned, i + 2)
                nc.scalar.copy(cols[:, :, :], ps_t[:, :, :]).then_inc(cols_ready, 1)

            def take(i):
                for u, (b, (c0, c1, to)) in enumerate(units):
                    act.wait_ge(product, i * U + (u + 1))
                    nc.scalar.copy(to[:, bass.ds(i * GROUP + b, 1), :], ps[u % 4][:, 0:c1 - c0].unsqueeze(1)
                                   ).then_inc(taken, 1)

            act.sem_inc(cols_ready, 1)
            act.sem_inc(taken, U)
            columns(0)
            with act.Fori(0, GROUPS - 1) as i:
                take(i)
                columns(i + 1)
            take(GROUPS - 1)


def split_bf16(nc, link, parts, whole, rest):
    link(nc.vector.tensor_copy(parts[0], whole))
    link(nc.vector.tensor_tensor(rest, whole, parts[0], ALU.subtract))
    link(nc.vector.tensor_copy(parts[1], rest))
    link(nc.vector.tensor_tensor(parts[2], rest, parts[1], ALU.subtract))


def two_blocks(nc, engine, packed, k, shift, top):
    word = engine.value_load(packed[0:1, bass.ds(k, 1)])
    return [nc.s_assert_within((word >> (shift * j)) & ((1 << shift) - 1), 0, top,
                               skip_runtime_bounds_check_because=IN_RANGE) for j in range(2)]


def relation_products(nc, g, l):
    with Stage(nc, f"rel{l}") as s:
        kv = s.sb("kv", [P, NB, R * TW])
        q = g.acc[:, :, 0:R * C]
        node_product(nc, g, f"relp{l}", g.h, C, g.w_rel[l],
                     [(0, R * TW, kv), (R * TW, R * (TW + C), q), (R * (TW + C), R * (TW + C) + C, g.own)],
                     beside=load_meta(nc, g) if l == 0 else None)
        written = s.sem("written")
        step = s.sem("step")
        block = s.block()

        @block.sync
        def _(sp):
            rows = g.rel_table.rearrange("(r b p) w -> r p b w", r=R, p=P)
            for r in range(R):
                sp.dma_start(rows[r], kv[:, :, r * TW:(r + 1) * TW]).then_inc(written, 16)
            sp.wait_ge(written, 16 * R)

        @block.vector
        def _(dve):
            link = chain(dve, step)
            if l == 0:
                for r in range(R):
                    nc.vector.tensor_scalar(g.mask[:, :, r], g.meta[:, :, M_TYPE], float(r), None, ALU.is_equal)
            high, middle, low = [g.q_split[:, j, :, :] for j in range(3)]
            scale = float(D) ** -0.5
            link(nc.vector.tensor_scalar(high, q[:, :, :], scale, None, ALU.mult))
            link(nc.vector.scalar_tensor_tensor(q[:, :, :], q[:, :, :], scale, high, ALU.mult, ALU.subtract))
            link(nc.vector.tensor_copy(middle, q[:, :, :]))
            link(nc.vector.tensor_tensor(low, q[:, :, :], middle, ALU.subtract))


def relation_pass(nc, g, l):
    W = R * C + R * H
    BY_DVE = 0
    AHEAD = 3
    UNROLL = 2 * DEPTH
    loops = NC // (UNROLL * HALF)
    assert NC % (UNROLL * HALF) == 0
    with Stage(nc, f"relpass{l}") as s:
        idx = [s.sb(f"idx{h}", [P, HALF], I32) for h in range(DEPTH)]
        row = [s.sb(f"row{h}", [P, HALF, TW]) for h in range(DEPTH)]
        hot_t = [s.sb(f"hot_t{h}", [P, HALF, P], BF16) for h in range(2)]
        hot = [s.sb(f"hot{n}", [P, HALF, P]) for n in range(UNROLL)]
        prod = s.sb("prod", [P, HALF, R * C])
        en = s.sb("en", [P, HALF, R * H])
        en_m = s.sb("en_m", [P, HALF, R * H])
        val = [s.sb(f"val{h}", [P, HALF, W]) for h in range(2)]
        ps_t = [s.ps(f"t{h}", [P, HALF, P]) for h in range(2)]
        ps_q = [s.ps(f"q{h}", [P, HALF, R * C]) for h in range(2)]
        ps_s = [s.ps(f"s{j}", [P, BANK]) for j in range(2)]
        idx_ready = s.sem("idx_ready")
        opened = s.sem("opened")
        gathered = [s.sem(f"gathered{h}") for h in range(DEPTH)]
        hot_ready = s.sem("hot_ready")
        turned = s.sem("turned")
        hot_t_ready = s.sem("hot_t_ready")
        query_ready = s.sem("query_ready")
        query_used = s.sem("query_used")
        reduced = s.sem("reduced")
        masked = s.sem("masked")
        energy_ready = s.sem("energy_ready")
        value_ready = s.sem("value_ready")
        summed = s.sem("summed")
        added_first = s.sem("added_first")
        added = s.sem("added")
        block = s.block()


        @block.gpsimd
        def _(pool):
            with pool.Fori(0, loops) as i:
                for n in range(UNROLL):
                    k, h = UNROLL * i + n, n % DEPTH
                    pool.wait_ge(idx_ready, k + 1)
                    pool.wait_ge(value_ready, k + 1)
                    pool.sem_inc(opened, 1)
                    for c in range(HALF):
                        pool.indirect_dma_start(row[h][:, c, :], None, g.rel_table,
                                                bass.IndirectOffsetOnAxis(ap=idx[h][:, c:c + 1], axis=0)
                                                ).then_inc(gathered[h], 16)

        @block.scalar
        def _(act):
            def take(p, k):
                act.wait_ge(turned, k + 3)
                nc.scalar.copy(hot_t[p][:, :, :], ps_t[p][:, :, :]).then_inc(hot_t_ready, 1)

            act.sem_inc(hot_t_ready, 2)
            act.sem_inc(value_ready, DEPTH)
            take(0, 0)
            take(1, 1)
            with act.Fori(0, loops) as i:
                for n in range(UNROLL):
                    k, h, p = UNROLL * i + n, n % DEPTH, n % 2
                    act.wait_ge(gathered[h], 16 * HALF * 2 * i + 16 * HALF * (n // DEPTH + 1))
                    act.wait_ge(summed, k + 1)
                    for c in range(HALF):
                        for r in range(0 if c < HALF - BY_DVE else 1, R):
                            last = nc.scalar.mul(val[p][:, c, r * C:(r + 1) * C], row[h][:, c, C:TW],
                                                 g.mask[:, bass.ds(i * (UNROLL * HALF) + n * HALF + c, 1), r])
                    last.then_inc(value_ready, 1)
                    act.wait_ge(query_ready, k + 3)
                    take(p, k + 2)

        @block.tensor
        def _(pe):
            def turn(n, k):
                pe.wait_ge(hot_ready, k + 1)
                pe.wait_ge(hot_t_ready, k + 1)
                for c in range(HALF):
                    last = nc.tensor.transpose(ps_t[n % 2][:, c, :], hot[n][:, c, :], g.ident[:, :])
                last.then_inc(turned, 1)

            def query(p, k, b):
                pe.wait_ge(hot_t_ready, k + 3)
                pe.wait_ge(query_used, k + 1)
                for c in range(HALF):
                    for j in range(3):
                        last = nc.tensor.matmul(ps_q[p][:, c, :], hot_t[p][:, c, :],
                                                g.q_split[:, j, bass.ds(b[c // PAIR], 1), :].squeeze(1),
                                                start=(j == 0), stop=(j == 2))
                last.then_inc(query_ready, 1)

            pe.sem_inc(turned, 2)
            pe.sem_inc(query_ready, 2)
            pe.sem_inc(summed, 1)
            for j in range(2):
                last = nc.tensor.matmul(ps_s[j][:, :], g.zeros[:, 0:P], g.zeros[:, :], start=True, stop=True)
            last.then_inc(summed, 1)
            turn(0, 0)
            turn(1, 1)
            query(0, 0, two_blocks(nc, pe, g.blk_dst, 1, 5, NB - 1))
            with pe.Fori(0, loops) as i:
                for n in range(UNROLL):
                    k, p = UNROLL * i + n, n % 2
                    b = two_blocks(nc, pe, g.blk_dst, k + 2, 5, NB - 1)
                    turn((n + 2) % UNROLL, k + 2)
                    query(1 - p, k + 1, b)
                    pe.wait_ge(energy_ready, k + 1)
                    pe.wait_ge(value_ready, k + 1 + DEPTH)
                    pe.wait_ge(added, k + 2)
                    for c in range(HALF):
                        last = nc.tensor.matmul(ps_s[c // PAIR][:, 0:W], hot[n][:, c, :], val[p][:, c, :],
                                                start=(c % PAIR == 0), stop=(c % PAIR == PAIR - 1))
                    last.then_inc(summed, 1)

        @block.vector
        def _(dve):
            def hots(n, at, chunks):
                for c in chunks:
                    last = nc.vector.tensor_scalar(hot[n][:, c, :], g.iota[:, :],
                                                   g.meta[:, bass.ds(at + c, 1), M_DLO], None, ALU.is_equal)
                return last

            def stage(h, at):
                gather_idx(nc, g, idx, h, at, M_REL).then_inc(idx_ready, 1)

            def add(j, b):
                to = g.acc[:, bass.ds(b, 1), :].squeeze(1)
                return nc.vector.tensor_tensor(to, ps_s[j][:, 0:W], to, ALU.add)

            dve.sem_inc(query_used, 2)
            for h in range(DEPTH):
                stage(h, h * HALF)
            for n in range(AHEAD):
                hots(n, n * HALF, range(HALF)).then_inc(hot_ready, 1)
            nc.vector.memset(g.acc[:, :, :], 0.0).then_inc(added, 1)
            with dve.Fori(0, loops) as i:
                for n in range(UNROLL):
                    k, h, p = UNROLL * i + n, n % DEPTH, n % 2
                    at = i * (UNROLL * HALF) + n * HALF
                    ahead, at_ahead = (n + AHEAD) % UNROLL, at + AHEAD * HALF
                    dve.wait_ge(query_ready, k + 3)
                    dve.wait_ge(gathered[h], 16 * HALF * 2 * i + 16 * HALF * (n // DEPTH + 1))
                    nc.vector.tensor_tensor(
                        prod[:, :, :].rearrange("p c (r w) -> p c r w", r=R),
                        ps_q[p][:, :, :].rearrange("p c (r w) -> p c r w", r=R),
                        row[h][:, :, 0:C].unsqueeze(2).to_broadcast([P, HALF, R, C]), ALU.mult
                    ).then_inc(query_used, 1)
                    for c in range(HALF - BY_DVE, HALF):
                        nc.vector.tensor_scalar(val[p][:, c, 0:C], row[h][:, c, C:TW],
                                                g.mask[:, bass.ds(at + c, 1), 0], None, ALU.mult)
                    stage(h, at + TURN)
                    b = two_blocks(nc, dve, g.blk_dst, k, 5, NB - 1)
                    dve.wait_ge(query_used, k + 3)
                    nc.vector.tensor_reduce(en[:, :, :], prod[:, :, :].rearrange("p c (g d) -> p c g d", d=D),
                                            AX, ALU.add).then_inc(reduced, 1)
                    hots(ahead, at_ahead, range(HALF - 2))
                    dve.wait_ge(reduced, k + 1)
                    nc.vector.tensor_tensor(en_m[:, :, :].rearrange("p c (r h) -> p (c r) h", r=R),
                                            en[:, :, :].rearrange("p c (r h) -> p (c r) h", r=R),
                                            wide(g.mask[:, bass.ds(at, HALF), :].rearrange("p c r -> p (c r)"), H),
                                            ALU.mult).then_inc(masked, 1)
                    hots(ahead, at_ahead, [HALF - 2])
                    dve.wait_ge(masked, k + 1)
                    nc.vector.scalar_tensor_tensor(val[p][:, :, R * C:W], en_m[:, :, :], 0.01, en_m[:, :, :],
                                                   ALU.mult, ALU.max).then_inc(energy_ready, 1)
                    dve.wait_ge(summed, k + 2)
                    dve.wait_ge(added, k + 1)
                    add(0, b[0]).then_inc(added_first, 1)
                    hots(ahead, at_ahead, [HALF - 1]).then_inc(hot_ready, 1)
                    dve.wait_ge(added_first, k + 1)
                    add(1, b[1]).then_inc(added, 1)
            last_step = UNROLL * loops
            b = two_blocks(nc, dve, g.blk_dst, last_step, 5, NB - 1)
            dve.wait_ge(summed, last_step + 2)
            dve.wait_ge(added, last_step + 1)
            add(0, b[0]).then_inc(added_first, 1)
            dve.wait_ge(added_first, last_step + 1)
            add(1, b[1]).then_inc(added, 1)


def layer_norm(nc, g, name, y, affine=None, plus=None, copy=None):
    with Stage(nc, name) as s:
        mean = s.sb("mean", [P, NB])
        sq = s.sb("sq", [P, NB, C])
        step = s.sem("step")
        var_ready = s.sem("var_ready")
        sd_ready = s.sem("sd_ready")
        block = s.block()

        @block.scalar
        def _(act):
            act.wait_ge(var_ready, 1)
            nc.scalar.activation(mean[:, :], mean[:, :], ACT.Sqrt).then_inc(sd_ready, 1)

        @block.vector
        def _(dve):
            link = chain(dve, step)
            if plus is not None:
                link(nc.vector.tensor_tensor(y[:, :, :], y[:, :, :], plus[:, :, :], ALU.add))
            link(nc.vector.tensor_reduce(mean[:, :], y[:, :, :], AX, ALU.add))
            link(nc.vector.tensor_scalar(mean[:, :], mean[:, :], 1.0 / C, None, ALU.mult))
            link(nc.vector.tensor_tensor(y[:, :, :], y[:, :, :], wide(mean[:, :], C), ALU.subtract))
            link(nc.vector.tensor_tensor(sq[:, :, :], y[:, :, :], y[:, :, :], ALU.mult))
            link(nc.vector.tensor_reduce(mean[:, :], sq[:, :, :], AX, ALU.add))
            nc.vector.tensor_scalar(mean[:, :], mean[:, :], 1.0 / C, 1e-5, ALU.mult, ALU.add).then_inc(var_ready, 1)
            dve.wait_ge(sd_ready, 1)
            link(nc.vector.reciprocal(mean[:, :], mean[:, :]))
            link(nc.vector.tensor_tensor(y[:, :, :], y[:, :, :], wide(mean[:, :], C), ALU.mult))
            if affine is not None:
                for v, op in zip(affine, (ALU.mult, ALU.add)):
                    link(nc.vector.tensor_tensor(y[:, :, :], y[:, :, :],
                                                 v.unsqueeze(1).to_broadcast([P, NB, C]), op))
            if copy is not None:
                nc.vector.tensor_copy(copy[:, :, :], y[:, :, :])


def relation_nodes(nc, g, l):
    RH = R * H
    with Stage(nc, f"relnode{l}") as s:
        en = s.sb("en", [P, NB, RH])
        part = s.sb("part", [P, RH])
        top = s.sb("top", [RH, 1])
        diag = s.sb("diag", [RH, RH])
        msg = s.sb("msg", [P, NB, R * C])
        mix = s.sb("mix", [P, NB * R, C])
        score = s.sb("score", [P, NB, R])
        best = s.sb("best", [P, NB])
        val = g.acc[:, :, 0:R * C]

        with Stage(nc, f"alpha{l}") as a:
            ps_a = a.ps("a", [P, BANK])
            ps_b = a.ps("b", [P, BANK])
            ps_c = a.ps("c", [P, BANK])
            step = a.sem("step")
            part_ready = a.sem("part_ready")
            turned = a.sem("turned")
            diag_ready = a.sem("diag_ready")
            shift_ready = a.sem("shift_ready")
            shifted = a.sem("shifted")
            exps = a.sem("exps")
            sums_ready = a.sem("sums_ready")
            total = a.sem("total")
            block = a.block()

            @block.tensor
            def _(pe):
                pe.wait_ge(part_ready, 1)
                nc.tensor.transpose(ps_a[0:RH, 0:P], part[:, :], g.ident[:, :]).then_inc(turned, 1)
                pe.wait_ge(diag_ready, 1)
                nc.tensor.matmul(ps_b[:, 0:RH], g.ones[0:RH, :], diag[:, :], start=True, stop=True).then_inc(shift_ready, 1)
                pe.wait_ge(sums_ready, 1)
                nc.tensor.matmul(ps_c[:, 0:RH], g.ones[:, :], part[:, :], start=True, stop=True).then_inc(total, 1)

            @block.scalar
            def _(act):
                act.wait_ge(shifted, 1)
                nc.scalar.activation(en[:, :, :], en[:, :, :], ACT.Exp).then_inc(exps, 1)

            @block.vector
            def _(dve):
                link = chain(dve, step)
                link(nc.vector.tensor_copy(en[:, :, :], g.acc[:, :, R * C:]))
                link(nc.vector.tensor_scalar(en[:, NB - 1, :], en[:, NB - 1, :], g.no_node[:, 0:1], None, ALU.add))
                nc.vector.tensor_reduce(part[:, :], en[:, :, :].rearrange("p b g -> p g b"), AX, ALU.max
                                        ).then_inc(part_ready, 1)
                dve.wait_ge(turned, 1)
                link(nc.vector.tensor_reduce(top[:, :], ps_a[0:RH, 0:P], AX, ALU.max))
                nc.vector.tensor_scalar(diag[:, :], g.ident[0:RH, 0:RH], top[:, 0:1], None, ALU.mult
                                        ).then_inc(diag_ready, 1)
                dve.wait_ge(shift_ready, 1)
                nc.vector.tensor_tensor(en[:, :, :], en[:, :, :], ps_b[:, 0:RH].unsqueeze(1).to_broadcast([P, NB, RH]),
                                        ALU.subtract).then_inc(shifted, 1)
                dve.wait_ge(exps, 1)
                nc.vector.tensor_reduce(part[:, :], en[:, :, :].rearrange("p b g -> p g b"), AX, ALU.add
                                        ).then_inc(sums_ready, 1)
                dve.wait_ge(total, 1)
                link(nc.vector.reciprocal(part[:, :], ps_c[:, 0:RH]))
                link(nc.vector.tensor_tensor(en[:, :, :], en[:, :, :], part[:, :].unsqueeze(1).to_broadcast([P, NB, RH]),
                                             ALU.mult))
                v = val.rearrange("p b (g d) -> p b g d", d=D)
                link(nc.vector.tensor_tensor(v, v, wide(en[:, :, :], D), ALU.mult))

        for j in range(2):
            node_product(nc, g, f"cat{l}{j}", g.acc[:, :, j * P:(j + 1) * P], P, g.w_cat[l][j],
                         [(0, P, msg[:, :, j * P:(j + 1) * P])])

        with Stage(nc, f"mix{l}") as a:
            step = a.sem("step")
            shifted = a.sem("shifted")
            exps = a.sem("exps")
            sum_ready = a.sem("sum_ready")
            gelu = a.sem("gelu")
            block = a.block()
            m = msg[:, :, :].rearrange("p b (r c) -> p (b r) c", c=C)

            @block.scalar
            def _(act):
                act.wait_ge(shifted, 1)
                nc.scalar.activation(score[:, :, :], score[:, :, :], ACT.Exp).then_inc(exps, 1)
                act.wait_ge(sum_ready, 1)
                nc.scalar.activation(g.own[:, :, :], g.own[:, :, :], ACT.Gelu).then_inc(gelu, 1)

            @block.vector
            def _(dve):
                link = chain(dve, step)
                flat = score[:, :, :].rearrange("p b r -> p (b r)")
                link(nc.vector.tensor_tensor(mix[:, :, :], m, g.sem_w[l].unsqueeze(1).to_broadcast([P, NB * R, C]),
                                             ALU.mult))
                link(nc.vector.tensor_reduce(flat, mix[:, :, :], AX, ALU.add))
                link(nc.vector.tensor_scalar(flat, flat, g.sem_b[:, l:l + 1], None, ALU.add))
                link(nc.vector.tensor_reduce(best[:, :], score[:, :, :], AX, ALU.max))
                nc.vector.tensor_tensor(score[:, :, :], score[:, :, :], wide(best[:, :], R), ALU.subtract
                                        ).then_inc(shifted, 1)
                dve.wait_ge(exps, 1)
                link(nc.vector.tensor_reduce(best[:, :], score[:, :, :], AX, ALU.add))
                link(nc.vector.reciprocal(best[:, :], best[:, :]))
                link(nc.vector.tensor_tensor(score[:, :, :], score[:, :, :], wide(best[:, :], R), ALU.mult))
                link(nc.vector.tensor_tensor(mix[:, :, :], m, wide(flat, C), ALU.mult))
                link(nc.vector.tensor_reduce(msg[:, :, 0:C], mix[:, :, :].rearrange("p (b r) c -> p b c r", r=R),
                                             AX, ALU.add))
                nc.vector.tensor_tensor(g.own[:, :, :], g.own[:, :, :], msg[:, :, 0:C], ALU.add).then_inc(sum_ready, 1)
                dve.wait_ge(gelu, 1)
                link(nc.vector.tensor_tensor(g.h[:, :, :], g.h[:, :, :], g.own[:, :, :], ALU.add))
    layer_norm(nc, g, f"relln{l}", g.h, (g.ln_g[l], g.ln_b[l]))


def residual_norm(nc, g, name):
    layer_norm(nc, g, name, g.x, plus=g.h, copy=g.h)


def gather_idx(nc, g, idx, h, at, word):
    return nc.vector.tensor_copy(idx[h][:, :], g.meta[:, bass.ds(at, HALF), word].bitcast(I32))


def one_hot(nc, g, to, at, word):
    return nc.vector.tensor_tensor(to, g.iota[:, :].unsqueeze(1).to_broadcast([P, HALF, P]),
                                   wide(g.meta[:, bass.ds(at, HALF), word], P), ALU.is_equal)


def weigh_pass(nc, g):
    with Stage(nc, "weigh") as s:
        split = s.sb("split", [P, 3, NB, C], BF16)
        to = [s.sb(f"to{h}", [P, HALF], I32) for h in range(DEPTH)]
        row = [s.sb(f"row{h}", [P, HALF, SROWW]) for h in range(DEPTH)]
        hot_b = [s.sb(f"hot_b{h}", [P, HALF, P], BF16) for h in range(2)]
        hot_t = [s.sb(f"hot_t{h}", [P, HALF, P], BF16) for h in range(2)]
        ps_t = [s.ps(f"t{h}", [P, HALF, 2 * P], BF16) for h in range(2)]
        ps_x = [s.ps(f"x{h}", [P, HALF, 2 * C]) for h in range(2)]
        opened = s.sem("opened")
        hot_b_ready = s.sem("hot_b_ready")
        turned = s.sem("turned")
        hot_t_ready = s.sem("hot_t_ready")
        found = s.sem("found")
        row_ready = s.sem("row_ready")
        row_free = s.sem("row_free")
        scattered = [s.sem(f"scattered{h}") for h in range(DEPTH)]
        split_rows(nc, g, "weigh_split", g.h, split)
        block = s.block()

        @block.sync
        def _(sp):
            sp.sem_inc(row_free, DEPTH)
            with sp.Fori(0, TURNS) as i:
                for h in range(DEPTH):
                    sp.wait_ge(scattered[h], 16 * HALF * i + 16 * HALF)
                    sp.sem_inc(row_free, 1)

        @block.gpsimd
        def _(pool):
            with pool.Fori(0, TURNS) as i:
                for h in range(DEPTH):
                    pool.wait_ge(row_ready, DEPTH * i + h + 3)
                    pool.sem_inc(opened, 1)
                    for c in range(HALF):
                        pool.indirect_dma_start(g.sslots, bass.IndirectOffsetOnAxis(ap=to[h][:, c:c + 1], axis=0),
                                                row[h][:, c, :], None, bounds_check=ROWS - 1, oob_is_err=False
                                                ).then_inc(scattered[h], 16)
            for h in range(DEPTH):
                pool.wait_ge(scattered[h], 16 * HALF * TURNS)

        @block.scalar
        def _(act):
            act.sem_inc(hot_t_ready, 2)
            with act.Fori(0, TURNS) as i:
                for h in range(DEPTH):
                    k, p = DEPTH * i + h, h % 2
                    act.wait_ge(turned, k + 3)
                    act.wait_ge(found, k + 1)
                    nc.scalar.copy(hot_t[p][:, :, :], ps_t[p][:, :, 0:P]).then_inc(hot_t_ready, 1)

        @block.tensor
        def _(pe):
            def turn(p, k):
                pe.wait_ge(hot_b_ready, k + 1)
                pe.wait_ge(hot_t_ready, k + 1)
                for c in range(HALF):
                    last = nc.tensor.transpose(ps_t[p][:, c, 0:P], hot_b[p][:, c, :], g.ident_b[:, :])
                last.then_inc(turned, 1)

            pe.sem_inc(turned, 2)
            pe.sem_inc(found, 2)
            turn(0, 0)
            with pe.Fori(0, TURNS) as i:
                for h in range(DEPTH):
                    k, p = DEPTH * i + h, h % 2
                    b = two_blocks(nc, pe, g.blk_dst, k + 1, 5, NB - 1)
                    turn(1 - p, k + 1)
                    pe.wait_ge(hot_t_ready, k + 3)
                    pe.wait_ge(row_ready, k + 1)
                    for c in range(HALF):
                        for j in range(3):
                            last = nc.tensor.matmul(ps_x[p][:, c, 0:C], hot_t[p][:, c, :],
                                                    split[:, j, bass.ds(b[c // PAIR], 1), :].squeeze(1),
                                                    start=(j == 0), stop=(j == 2))
                    last.then_inc(found, 1)

        @block.vector
        def _(dve):
            def hots(p, at, k):
                dve.wait_ge(turned, k + 1)
                one_hot(nc, g, hot_b[p][:, :, :], at, M_DLO).then_inc(hot_b_ready, 1)

            dve.sem_inc(row_ready, 2)
            hots(0, 0, 0)
            with dve.Fori(0, TURNS) as i:
                for h in range(DEPTH):
                    k, p = DEPTH * i + h, h % 2
                    at = i * TURN + h * HALF
                    hots(1 - p, at + HALF, k + 1)
                    dve.wait_ge(found, k + 3)
                    dve.wait_ge(row_free, k + 1)
                    nc.vector.tensor_tensor(row[h][:, :, 0:C], ps_x[p][:, :, 0:C],
                                            wide(g.meta[:, bass.ds(at, HALF), M_WEIGHT], C), ALU.mult)
                    nc.vector.tensor_copy(row[h][:, :, C], g.meta[:, bass.ds(at, HALF), M_SLO])
                    gather_idx(nc, g, to, h, at, M_SROW).then_inc(row_ready, 1)


def split_rows(nc, g, name, of, split):
    with Stage(nc, name) as s:
        rest = s.sb("rest", [P, *of.shape[1:]])
        step = s.sem("step")
        block = s.block()

        @block.vector
        def _(dve):
            link = chain(dve, step)
            link(nc.vector.tensor_copy(rest[:], of[:]))
            split_bf16(nc, link, [split[:, j] for j in range(3)], rest[:], rest[:])


def open_sums(nc, pe, g, ps_sum):
    for j in range(4):
        last = nc.tensor.matmul(ps_sum[:, j * BANK:(j + 1) * BANK], g.zeros[:, 0:P], g.zeros[:, :],
                                start=True, stop=True, skip_group_check=True)
    return last


def add_sums(nc, pe, ps_sum, col, hot, val, width):
    for c in range(HALF):
        last = nc.tensor.matmul(ps_sum[:, bass.ds(col[c // PAIR], width)], hot[:, c, :], val[:, c, :],
                                start=False, stop=True, skip_group_check=True)
    return last


def take_sums(nc, name, ps_sum, out, width):
    with Stage(nc, name) as s:
        block = s.block()

        @block.vector
        def _(dve):
            for j in range(-(-NB // 7)):
                n = min(7, NB - 7 * j)
                nc.vector.tensor_copy(out[:, 7 * j:7 * j + n, 0:width],
                                      ps_sum[:, j * BANK:j * BANK + n * UC].rearrange("p (b w) -> p b w", w=UC)
                                      [:, :, 0:width])


def source_sum_pass(nc, g, sums):
    with Stage(nc, "srcsum") as s:
        LOAD = 2 * HALF
        RING = 4
        HOTS = 4
        banks = -(-NPAD // BANK)
        rows = [s.sb(f"rows{h}", [P, LOAD, SROWW]) for h in range(RING)]
        hot = [s.sb(f"hot{h}", [P, HALF, P]) for h in range(HOTS)]
        ps_sum = s.ps("sum", [C, banks * BANK])
        rows_ready = [s.sem(f"rows_ready{h}") for h in range(RING)]
        hot_ready = s.sem("hot_ready")
        summed = s.sem("summed")
        src = g.sslots.rearrange("(p n) w -> p n w", p=P)
        loops = NC // (RING * LOAD)
        steps = [(h, q) for h in range(RING) for q in range(2)]
        assert NC % (RING * LOAD) == 0

        with Stage(nc, "srcsum_block") as t:
            block = t.block()

            @block.sync
            def _(sp):
                with sp.Fori(0, loops) as i:
                    for h in range(RING):
                        sp.wait_ge(summed, 2 * RING * i + 2 * h + 2)
                        sp.dma_start(rows[h][:, :, :], src[:, bass.ds((RING * i + h) * LOAD, LOAD), :]
                                     ).then_inc(rows_ready[h], 16)

            @block.vector
            def _(dve):
                with dve.Fori(0, loops) as i:
                    for n, (h, q) in enumerate(steps):
                        k = 2 * RING * i + n
                        dve.wait_ge(rows_ready[h], 16 * i + 16)
                        dve.wait_ge(summed, k + 2 * RING + 1 - HOTS)
                        for c in range(HALF):
                            last = nc.vector.tensor_scalar(hot[n % HOTS][:, c, :], g.iota[:, :],
                                                           rows[h][:, q * HALF + c, C:SROWW], None, ALU.is_equal)
                        last.then_inc(hot_ready, 1)

            @block.tensor
            def _(pe):
                pe.sem_inc(summed, 2 * RING - 1)
                for j in range(banks):
                    last = nc.tensor.matmul(ps_sum[:, j * BANK:(j + 1) * BANK], g.zeros[:, 0:C], g.zeros[:, :],
                                            start=True, stop=True, skip_group_check=True)
                last.then_inc(summed, 1)
                with pe.Fori(0, loops) as i:
                    for n, (h, q) in enumerate(steps):
                        k = 2 * RING * i + n
                        b = two_blocks(nc, pe, g.blk_src, k + 1, 5, NB - 1)
                        pe.wait_ge(hot_ready, k + 1)
                        pe.wait_ge(rows_ready[h], 16 * i + 16)
                        for c in range(HALF):
                            last = nc.tensor.matmul(ps_sum[:, bass.ds(b[c // PAIR] * P, P)],
                                                    rows[h][:, q * HALF + c, 0:C], hot[n % HOTS][:, c, :],
                                                    start=False, stop=True, skip_group_check=True)
                        last.then_inc(summed, 1)

        with Stage(nc, "srcsum_take") as t:
            block = t.block()
            half = banks // 2 * BANK

            @block.vector
            def _(dve):
                nc.vector.tensor_copy(sums[:, 0:half], ps_sum[:, 0:half])

            @block.scalar
            def _(act):
                nc.scalar.copy(sums[:, half:NPAD], ps_sum[:, half:NPAD])


def message_pass(nc, g, out):
    with Stage(nc, "message") as s:
        idx = [s.sb(f"idx{h}", [P, HALF], I32) for h in range(DEPTH)]
        row = [s.sb(f"row{h}", [P, HALF, C]) for h in range(DEPTH)]
        own = [s.sb(f"own{h}", [P, HALF, C]) for h in range(DEPTH)]
        both = [s.sb(f"both{h}", [P, HALF, C]) for h in range(2)]
        val = [s.sb(f"val{h}", [P, HALF, C]) for h in range(2)]
        hot = [s.sb(f"hot{h}", [P, HALF, P]) for h in range(2)]
        ps_sum = s.ps("sum", [P, 4 * BANK])
        opened = s.sem("opened")
        idx_ready = s.sem("idx_ready")
        gathered = [s.sem(f"gathered{h}") for h in range(DEPTH)]
        own_ready = [s.sem(f"own_ready{h}") for h in range(DEPTH)]
        both_ready = s.sem("both_ready")
        val_ready = s.sem("val_ready")
        hot_ready = s.sem("hot_ready")
        summed = s.sem("summed")

        with Stage(nc, "message_block") as t:
            block = t.block()

            @block.sync
            def _(sp):
                src = g.slots.rearrange("(p n) w -> p n w", p=P)
                with sp.Fori(0, TURNS) as i:
                    for h in range(DEPTH):
                        sp.wait_ge(both_ready, DEPTH * i + h + 1)
                        sp.dma_start(own[h][:, :, :], src[:, bass.ds(i * TURN + h * HALF, HALF), 0:C]
                                     ).then_inc(own_ready[h], 16)

            @block.gpsimd
            def _(pool):
                with pool.Fori(0, TURNS) as i:
                    for h in range(DEPTH):
                        pool.wait_ge(idx_ready, DEPTH * i + h + 1)
                        pool.sem_inc(opened, 1)
                        for c in range(HALF):
                            pool.indirect_dma_start(row[h][:, c, :], None, g.msg_table,
                                                    bass.IndirectOffsetOnAxis(ap=idx[h][:, c:c + 1], axis=0)
                                                    ).then_inc(gathered[h], 16)

            @block.vector
            def _(dve):
                dve.sem_inc(both_ready, DEPTH)
                for h in range(DEPTH):
                    gather_idx(nc, g, idx, h, h * HALF, M_SRC).then_inc(idx_ready, 1)
                with dve.Fori(0, TURNS) as i:
                    for h in range(DEPTH):
                        k = DEPTH * i + h
                        at = i * TURN + h * HALF
                        dve.wait_ge(summed, k + 1)
                        one_hot(nc, g, hot[h % 2][:, :, :], at, M_DLO).then_inc(hot_ready, 1)
                        dve.wait_ge(gathered[h], 16 * HALF * i + 16 * HALF)
                        dve.wait_ge(own_ready[h], 16 * i + 16)
                        dve.wait_ge(val_ready, k + 1)
                        nc.vector.tensor_tensor(both[h % 2][:, :, :], row[h][:, :, :], own[h][:, :, :], ALU.add
                                                ).then_inc(both_ready, 1)
                        gather_idx(nc, g, idx, h, at + TURN, M_SRC).then_inc(idx_ready, 1)

            @block.scalar
            def _(act):
                act.sem_inc(val_ready, 2)
                with act.Fori(0, TURNS) as i:
                    for h in range(DEPTH):
                        k = DEPTH * i + h
                        act.wait_ge(both_ready, k + 1 + DEPTH)
                        act.wait_ge(summed, k + 1)
                        nc.scalar.activation(val[h % 2][:, :, :], both[h % 2][:, :, :], ACT.Relu).then_inc(val_ready, 1)

            @block.tensor
            def _(pe):
                pe.sem_inc(summed, 1)
                open_sums(nc, pe, g, ps_sum).then_inc(summed, 1)
                with pe.Fori(0, TURNS) as i:
                    for h in range(DEPTH):
                        k = DEPTH * i + h
                        col = two_blocks(nc, pe, g.col_dst, k + 1, 12, psum_column(NB - 1))
                        pe.wait_ge(hot_ready, k + 1)
                        pe.wait_ge(val_ready, k + 3)
                        add_sums(nc, pe, ps_sum, col, hot[h % 2], val[h % 2], C).then_inc(summed, 1)

        take_sums(nc, "message_take", ps_sum, out, C)


def gat_max_pass(nc, g, l):
    with Stage(nc, f"gatmax{l}") as s:
        idx = [s.sb(f"idx{h}", [P, HALF], I32) for h in range(DEPTH)]
        row = [s.sb(f"row{h}", [P, HALF, GW]) for h in range(DEPTH)]
        score = [s.sb(f"score{h}", [P, HALF, P]) for h in range(2)]
        far = [s.sb(f"far{h}", [P, HALF, P]) for h in range(2)]
        dlo = [s.sb(f"dlo{h}", [P, HALF]) for h in range(DEPTH)]
        found = s.sb("found", [P, HALF])
        junk = s.sb("junk", [P, HALF, P])
        red = s.sb("red", [P, PAIR])
        ps = [s.ps(f"t{h}", [P, HALF, P]) for h in range(2)]
        opened = s.sem("opened")
        idx_ready = s.sem("idx_ready")
        gathered = [s.sem(f"gathered{h}") for h in range(DEPTH)]
        stored = [s.sem(f"stored{h}") for h in range(DEPTH)]
        row_free = s.sem("row_free")
        far_ready = s.sem("far_ready")
        drafted = s.sem("drafted")
        score_ready = s.sem("score_ready")
        turned = s.sem("turned")
        reduced = s.sem("reduced")
        lifted_first = s.sem("lifted_first")
        lifted = s.sem("lifted")
        looked_up = s.sem("looked_up")
        found_used = s.sem("found_used")
        block = s.block()
        to = g.gat_rows.rearrange("(p n) w -> p n w", p=P)


        @block.sync
        def _(sp):
            with sp.Fori(0, TURNS) as i:
                for h in range(DEPTH):
                    sp.wait_ge(gathered[h], 16 * HALF * i + 16 * HALF)
                    sp.dma_start(to[:, bass.ds(i * TURN + h * HALF, HALF), :], row[h][:, :, :]).then_inc(stored[h], 16)
            for h in range(DEPTH):
                sp.wait_ge(stored[h], 16 * TURNS)

        @block.scalar
        def _(act):
            def measure(h, p, k):
                act.wait_ge(idx_ready, k + 1)
                act.wait_ge(score_ready, k + 1)
                for c in range(HALF):
                    last = nc.scalar.activation(far[p][:, c, :], g.iota[:, :], ACT.Abs, bias=dlo[h][:, c:c + 1],
                                                scale=-1.0)
                last.then_inc(far_ready, 1)

            act.sem_inc(row_free, DEPTH)
            measure(0, 0, 0)
            with act.Fori(0, TURNS) as i:
                for h in range(DEPTH):
                    k = DEPTH * i + h
                    measure((h + 1) % DEPTH, (h + 1) % 2, k + 1)
                    act.wait_ge(stored[h], 16 * i + 16)
                    act.sem_inc(row_free, 1)

        @block.gpsimd
        def _(pool):
            with pool.Fori(0, TURNS) as i:
                for h in range(DEPTH):
                    pool.wait_ge(row_free, DEPTH * i + h + 1)
                    pool.wait_ge(idx_ready, DEPTH * i + h + 1)
                    pool.sem_inc(opened, 1)
                    for c in range(HALF):
                        pool.indirect_dma_start(row[h][:, c, :], None, g.gat_table,
                                                bass.IndirectOffsetOnAxis(ap=idx[h][:, c:c + 1], axis=0)
                                                ).then_inc(gathered[h], 16)

        @block.tensor
        def _(pe):
            def turn(p):
                for c in range(HALF):
                    last = nc.tensor.transpose(ps[p][:, c, :], score[p][:, c, :], g.ident[:, :])
                last.then_inc(turned, 1)

            pe.sem_inc(turned, 1)
            pe.wait_ge(score_ready, 1)
            turn(1)
            with pe.Fori(0, TURNS) as i:
                for h in range(DEPTH):
                    k = DEPTH * i + h
                    pe.wait_ge(score_ready, k + 2)
                    turn(h % 2)

        @block.vector
        def _(dve):
            def reduce(p, k):
                dve.wait_ge(turned, k + 2)
                dve.wait_ge(lifted, k + 1)
                nc.vector.tensor_reduce(red[:, :], ps[p][:, :, :].rearrange("p (j c) e -> p j (c e)", j=PAIR),
                                        AX, ALU.max).then_inc(reduced, 1)

            def lift(j, b):
                to = g.top[:, bass.ds(b, 1)]
                return nc.vector.tensor_tensor(to, to, red[:, j:j + 1], ALU.max)

            def stage(h, at):
                nc.vector.tensor_copy(dlo[h][:, :], g.meta[:, bass.ds(at, HALF), M_DLO])
                gather_idx(nc, g, idx, h, at, M_SRC).then_inc(idx_ready, 1)

            dve.sem_inc(lifted, 1)
            nc.vector.memset(score[1][:, :, :], -BIG).then_inc(score_ready, 1)
            for h in range(DEPTH):
                stage(h, h * HALF)
            with dve.Fori(0, TURNS) as i:
                before = two_blocks(nc, dve, g.blk_dst, DEPTH * i, 5, NB - 1)
                b = two_blocks(nc, dve, g.blk_dst, DEPTH * i + 1, 5, NB - 1)
                for h in range(DEPTH):
                    k, p = DEPTH * i + h, h % 2
                    at = i * TURN + h * HALF
                    dve.wait_ge(idx_ready, k + 1)
                    look_up(nc, g, b, dlo[h], g.dst_rows, found, junk).then_inc(looked_up, 1)
                    reduce(1 - p, k)
                    dve.wait_ge(gathered[h], 16 * HALF * i + 16 * HALF)
                    dve.wait_ge(turned, k + 1)
                    for c in range(HALF):
                        last = nc.vector.tensor_scalar(score[p][:, c, :], g.iota[:, :], dlo[h][:, c:c + 1],
                                                       row[h][:, c, C + 1:GW], ALU.is_equal, ALU.mult)
                    last.then_inc(drafted, 1)
                    after = two_blocks(nc, dve, g.blk_dst, k + 2, 5, NB - 1) if h + 1 < DEPTH else None
                    dve.wait_ge(reduced, k + 1)
                    lift(0, before[0]).then_inc(lifted_first, 1)
                    dve.wait_ge(looked_up, k + 1)
                    nc.vector.tensor_tensor(g.edge_score[:, bass.ds(at, HALF)], row[h][:, :, C + 1], found[:, :],
                                            ALU.add).then_inc(found_used, 1)
                    dve.wait_ge(drafted, k + 1)
                    dve.wait_ge(far_ready, k + 1)
                    nc.vector.scalar_tensor_tensor(score[p][:, :, :], far[p][:, :, :], -BIG, score[p][:, :, :],
                                                   ALU.mult, ALU.add).then_inc(score_ready, 1)
                    dve.wait_ge(lifted_first, k + 1)
                    lift(1, before[1]).then_inc(lifted, 1)
                    dve.wait_ge(found_used, k + 1)
                    stage(h, at + TURN)
                    before, b = b, after
            steps = DEPTH * TURNS
            b = two_blocks(nc, dve, g.blk_dst, steps, 5, NB - 1)
            reduce(1, steps)
            dve.wait_ge(reduced, steps + 1)
            lift(0, b[0]).then_inc(lifted_first, 1)
            dve.wait_ge(lifted_first, steps + 1)
            lift(1, b[1]).then_inc(lifted, 1)


def look_up(nc, g, b, dlo, nodes, to, junk):
    for c in range(HALF):
        last = nc.vector.scalar_tensor_tensor(junk[:, c, :], g.iota[:, :], dlo[:, c:c + 1],
                                              nodes[:, bass.ds(b[c // PAIR], 1), :].squeeze(1),
                                              ALU.is_equal, ALU.mult, accum_out=to[:, c:c + 1])
    return last


def spread_nodes(nc, g, name, of, to):
    with Stage(nc, name) as s:
        by_block = s.sb("by_block", [NB, P])
        ps = s.ps("turn", [NB, P])
        turned = s.sem("turned")
        taken = s.sem("taken")
        moved = s.sem("moved")
        block = s.block()

        @block.tensor
        def _(pe):
            nc.tensor.transpose(ps[:, :], of, g.ident[:, :]).then_inc(turned, 1)

        @block.vector
        def _(dve):
            dve.wait_ge(turned, 1)
            nc.vector.tensor_copy(by_block[:, :], ps[:, :]).then_inc(taken, 1)

        @block.sync
        def _(sp):
            sp.wait_ge(taken, 1)
            sp.dma_start(g.node_row, by_block[:, :]).then_inc(moved, 16)
            sp.wait_ge(moved, 16)
            sp.dma_start(to[:, :, :], g.node_row.unsqueeze(0).to_broadcast([P, NB, P])).then_inc(moved, 16)
            sp.wait_ge(moved, 32)


def gat_sum_pass(nc, g, l, out):
    with Stage(nc, f"gatleaky{l}") as s:
        block = s.block()

        @block.vector
        def _(dve):
            nc.vector.scalar_tensor_tensor(g.edge_leaky[:, 0:NC], g.edge_score[:, 0:NC], 0.2, g.edge_score[:, 0:NC],
                                           ALU.mult, ALU.max)
            nc.vector.memset(g.edge_leaky[:, NC:CP], 0.0)

    with Stage(nc, f"gatsum{l}") as s:
        RING = 8
        LOAD = 2 * HALF
        LOADS = RING // 2
        AHEAD = 3
        ONES = 2
        small = lambda n: [s.sb(f"{n}{h}", [P, HALF]) for h in range(RING)]
        dlo, top, below, capped, w, minus_w = [small(n) for n in ("dlo", "top", "below", "capped", "w", "minus_w")]
        junk = s.sb("junk", [P, HALF, P])
        far = [s.sb(f"far{h}", [P, ONES, P]) for h in range(2)]
        hot = [s.sb(f"hot{h}", [P, HALF, P]) for h in range(4)]
        rows = [s.sb(f"rows{h}", [P, LOAD, GW]) for h in range(LOADS)]
        ps_sum = s.ps("sum", [P, 4 * BANK])
        rows_ready = [s.sem(f"rows_ready{h}") for h in range(LOADS)]
        dlo_ready = s.sem("dlo_ready")
        looked_up = s.sem("looked_up")
        lowered = s.sem("lowered")
        capped_ready = s.sem("capped_ready")
        w_ready = s.sem("w_ready")
        minus_ready = s.sem("minus_ready")
        far_ready = s.sem("far_ready")
        hot_act = s.sem("hot_act")
        hot_dve = s.sem("hot_dve")
        summed = s.sem("summed")
        loops = NC // (RING * HALF)
        assert NC % (RING * HALF) == 0
        src = g.gat_rows.rearrange("(p n) w -> p n w", p=P)

        with Stage(nc, f"gatsum{l}_block") as t:
            block = t.block()

            @block.sync
            def _(sp):
                with sp.Fori(0, loops) as i:
                    for h in range(LOADS):
                        sp.wait_ge(summed, RING * i + 2 * h + 2)
                        sp.dma_start(rows[h][:, :, :], src[:, bass.ds((LOADS * i + h) * LOAD, LOAD), :]
                                     ).then_inc(rows_ready[h], 16)

            @block.vector
            def _(dve):
                def stage(n, at):
                    nc.vector.tensor_copy(dlo[n][:, :], g.meta[:, bass.ds(at, HALF), M_DLO]).then_inc(dlo_ready, 1)

                def find(n, k, b):
                    dve.wait_ge(dlo_ready, k + 1)
                    look_up(nc, g, b, dlo[n], g.dst_rows, top[n], junk).then_inc(looked_up, 1)

                def lower(n, k, at):
                    dve.wait_ge(looked_up, k + 1)
                    nc.vector.tensor_tensor(below[n][:, :], g.edge_leaky[:, bass.ds(at, HALF)], top[n][:, :],
                                            ALU.subtract).then_inc(lowered, 1)

                def cap(n, k):
                    dve.wait_ge(lowered, k + 1)
                    nc.vector.tensor_scalar(capped[n][:, :], below[n][:, :], 0.0, None, ALU.min
                                            ).then_inc(capped_ready, 1)

                def weighted_hot(n, c):
                    return nc.vector.tensor_scalar(hot[n % 4][:, c, :], g.iota[:, :], dlo[n][:, c:c + 1],
                                                   w[n][:, c:c + 1], ALU.is_equal, ALU.mult)

                for n in range(AHEAD + 1):
                    stage(n, n * HALF)
                for n in range(AHEAD):
                    find(n, n, two_blocks(nc, dve, g.blk_dst, n + 1, 5, NB - 1))
                    lower(n, n, n * HALF)
                    cap(n, n)
                with dve.Fori(0, loops) as i:
                    for n in range(RING):
                        k = RING * i + n
                        at = i * (RING * HALF) + n * HALF
                        next_n = (n + AHEAD) % RING
                        if n == 0:
                            b = two_blocks(nc, dve, g.blk_dst, k + AHEAD + 1, 5, NB - 1)
                        dve.wait_ge(hot_act, k + 1)
                        stage((n + AHEAD + 1) % RING, at + (AHEAD + 1) * HALF)
                        find(next_n, k + AHEAD, b)
                        if n + 1 < RING:
                            b = two_blocks(nc, dve, g.blk_dst, k + AHEAD + 2, 5, NB - 1)
                        dve.wait_ge(w_ready, k + 1)
                        dve.wait_ge(summed, k + RING - 3)
                        for c in range(ONES, HALF - 1):
                            weighted_hot(n, c)
                        lower(next_n, k + AHEAD, at + AHEAD * HALF)
                        weighted_hot(n, HALF - 1).then_inc(hot_dve, 1)
                        cap(next_n, k + AHEAD)

            @block.scalar
            def _(act):
                def weigh(n, k):
                    act.wait_ge(capped_ready, k + 1)
                    nc.scalar.activation(w[n][:, :], capped[n][:, :], ACT.Exp).then_inc(w_ready, 1)

                act.sem_inc(hot_act, AHEAD + 1)
                weigh(0, 0)
                with act.Fori(0, loops) as i:
                    for n in range(RING):
                        k = RING * i + n
                        act.wait_ge(dlo_ready, k + 1)
                        act.wait_ge(hot_act, k + AHEAD)
                        for c in range(ONES):
                            last = nc.scalar.activation(far[n % 2][:, c, :], g.iota[:, :], ACT.Abs,
                                                        bias=dlo[n][:, c:c + 1], scale=-1.0)
                        last.then_inc(far_ready, 1)
                        act.wait_ge(w_ready, k + 1)
                        nc.scalar.mul(minus_w[n][:, :], w[n][:, :], -1.0).then_inc(minus_ready, 1)
                        weigh((n + 1) % RING, k + 1)
                        act.wait_ge(far_ready, k + 1)
                        act.wait_ge(minus_ready, k + 1)
                        act.wait_ge(summed, k + RING - 3)
                        for c in range(ONES):
                            last = nc.scalar.activation(hot[n % 4][:, c, :], far[n % 2][:, c, :], ACT.Relu,
                                                        bias=w[n][:, c:c + 1], scale=minus_w[n][:, c:c + 1])
                        last.then_inc(hot_act, 1)

            @block.tensor
            def _(pe):
                pe.sem_inc(summed, RING - 1)
                open_sums(nc, pe, g, ps_sum).then_inc(summed, 1)
                with pe.Fori(0, loops) as i:
                    for n in range(RING):
                        k, q = RING * i + n, n % 2
                        col = two_blocks(nc, pe, g.col_dst, k + 1, 12, psum_column(NB - 1))
                        pe.wait_ge(hot_dve, k + 1)
                        pe.wait_ge(hot_act, k + AHEAD + 2)
                        pe.wait_ge(rows_ready[n // 2], 16 * i + 16)
                        add_sums(nc, pe, ps_sum, col, hot[n % 4], rows[n // 2][:, q * HALF:(q + 1) * HALF, 0:C + 1],
                                 C + 1).then_inc(summed, 1)

        take_sums(nc, f"gatsum{l}_take", ps_sum, out, C + 1)


def weighted_layer(nc, g):
    weigh_pass(nc, g)
    with Stage(nc, "wsum") as s:
        agg = s.sb("agg", [P, NB, C])
        sums = s.sb("sums", [C, NPAD])
        source_sum_pass(nc, g, sums)
        with Stage(nc, "wproj") as t:
            per_bank = BANK // C
            parts = [range(b, min(b + per_bank, NB)) for b in range(0, NB, per_bank)]
            ps = [t.ps(f"p{j}", [P, per_bank, C]) for j in range(len(parts))]
            projected = t.sem("projected")
            block = t.block()

            @block.tensor
            def _(pe):
                for j, part in enumerate(parts):
                    for b in part:
                        last = nc.tensor.matmul(ps[j][:, b % per_bank, :], sums[:, b * P:(b + 1) * P], g.w_agg[:, :],
                                                start=True, stop=True)
                    last.then_inc(projected, 1)

            @block.vector
            def _(dve):
                for j, part in enumerate(parts):
                    dve.wait_ge(projected, j + 1)
                    nc.vector.tensor_tensor(g.h[:, part[0]:part[-1] + 1, :], ps[j][:, 0:len(part), :],
                                            g.b_agg.unsqueeze(1).to_broadcast([P, len(part), C]), ALU.add)
        norm = s.sb("norm", [P, NB])
        step = s.sem("step")
        square = s.sem("square")
        root = s.sem("root")
        block = s.block()

        @block.scalar
        def _(act):
            act.wait_ge(square, 1)
            nc.scalar.activation(norm[:, :], norm[:, :], ACT.Sqrt).then_inc(root, 1)

        @block.vector
        def _(dve):
            link = chain(dve, step)
            link(nc.vector.tensor_tensor(agg[:, :, :], g.h[:, :, :], g.h[:, :, :], ALU.mult))
            nc.vector.tensor_reduce(norm[:, :], agg[:, :, :], AX, ALU.add).then_inc(square, 1)
            dve.wait_ge(root, 1)
            link(nc.vector.tensor_scalar(norm[:, :], norm[:, :], 1e-12, None, ALU.max))
            link(nc.vector.reciprocal(norm[:, :], norm[:, :]))
            link(nc.vector.tensor_tensor(g.h[:, :, :], g.h[:, :, :], wide(norm[:, :], C), ALU.mult))


def store_table(nc, name, table, rows):
    with Stage(nc, name) as s:
        stored = s.sem("stored")
        block = s.block()

        @block.sync
        def _(sp):
            sp.dma_start(table.rearrange("(b p) w -> p b w", p=P), rows[:, :, :]).then_inc(stored, 16)
            sp.wait_ge(stored, 16)


def message_layer(nc, g):
    with Stage(nc, "msg") as s:
        pair = s.sb("pair", [P, NB, 2 * C])
        node_product(nc, g, "msgp", g.h, C, g.w_msg_node, [(0, C, pair[:, :, 0:C])])
        store_table(nc, "msgt", g.msg_table, pair[:, :, 0:C])
        message_pass(nc, g, pair[:, :, C:2 * C])
        with Stage(nc, "msgpair") as t:
            block = t.block()

            @block.vector
            def _(dve):
                nc.vector.tensor_copy(pair[:, :, 0:C], g.h[:, :, :])
        node_product(nc, g, "msgu", pair, 2 * C, g.w_upd, [(0, C, g.h)])
        step = s.sem("step")
        block = s.block()

        @block.vector
        def _(dve):
            link = chain(dve, step)
            link(nc.vector.tensor_tensor(g.h[:, :, :], g.h[:, :, :], g.b_upd.unsqueeze(1).to_broadcast([P, NB, C]),
                                         ALU.add))
            link(nc.vector.tensor_scalar(g.h[:, :, :], g.h[:, :, :], 0.0, None, ALU.max))


def gat_layer(nc, g, l):
    with Stage(nc, f"gat{l}") as s:
        table = s.sb("table", [P, NB, GW])
        tmp = s.sb("tmp", [P, NB, C])
        both = s.sb("both", [P, 2, NB])
        self_e = s.sb("self_e", [P, NB])
        g.top = s.sb("top", [P, NB])
        g.dst_rows = s.sb("dst_rows", [P, NB, P])
        g.edge_score = s.sb("edge_score", [P, CP])
        g.edge_leaky = s.sb("edge_leaky", [P, CP])
        agg = s.sb("agg", [P, NB, C + 1])
        node_product(nc, g, f"gatp{l}", g.h, C, g.w_gat[l], [(0, C, table[:, :, 0:C])])
        with Stage(nc, f"gatscore{l}") as t:
            step = t.sem("step")
            block = t.block()

            @block.vector
            def _(dve):
                link = chain(dve, step)
                nc.vector.memset(table[:, :, C:C + 1], 1.0)
                for a, to in ((g.a_src[l], table[:, :, C + 1]), (g.a_dst[l], both[:, 0, :])):
                    link(nc.vector.tensor_tensor(tmp[:, :, :], table[:, :, 0:C], a.unsqueeze(1).to_broadcast([P, NB, C]),
                                                 ALU.mult))
                    link(nc.vector.tensor_reduce(to, tmp[:, :, :], AX, ALU.add))
                link(nc.vector.tensor_copy(g.top[:, :], table[:, :, C + 1]))
        store_table(nc, f"gatt{l}", g.gat_table, table)
        spread_nodes(nc, g, f"gatdst{l}", both[:, 0, :], g.dst_rows)
        gat_max_pass(nc, g, l)
        with Stage(nc, f"gattop{l}") as t:
            step = t.sem("step")
            block = t.block()

            @block.vector
            def _(dve):
                link = chain(dve, step)

                def leaky(to, a, b):
                    link(nc.vector.tensor_tensor(tmp[:, :, 0], a, b, ALU.add))
                    link(nc.vector.scalar_tensor_tensor(to, tmp[:, :, 0], 0.2, tmp[:, :, 0], ALU.mult, ALU.max))
                leaky(both[:, 1, :], g.top[:, :], both[:, 0, :])
                leaky(self_e[:, :], table[:, :, C + 1], both[:, 0, :])
        spread_nodes(nc, g, f"gattopr{l}", both[:, 1, :], g.dst_rows)
        with Stage(nc, f"gatorder{l}") as t:
            exp_in = t.sem("exp_in")
            block = t.block()

            @block.vector
            def _(dve):
                nc.vector.tensor_tensor(self_e[:, :], self_e[:, :], both[:, 1, :], ALU.subtract).then_inc(exp_in, 1)

            @block.scalar
            def _(act):
                act.wait_ge(exp_in, 1)
                nc.scalar.activation(self_e[:, :], self_e[:, :], ACT.Exp)
        gat_sum_pass(nc, g, l, agg)
        step = s.sem("step")
        block = s.block()

        @block.vector
        def _(dve):
            link = chain(dve, step)
            link(nc.vector.tensor_tensor(tmp[:, :, :], table[:, :, 0:C], wide(self_e[:, :], C), ALU.mult))
            link(nc.vector.tensor_tensor(agg[:, :, 0:C], agg[:, :, 0:C], tmp[:, :, :], ALU.add))
            link(nc.vector.tensor_tensor(self_e[:, :], self_e[:, :], agg[:, :, C], ALU.add))
            link(nc.vector.tensor_scalar(self_e[:, :], self_e[:, :], 1e-16, None, ALU.add))
            link(nc.vector.reciprocal(self_e[:, :], self_e[:, :]))
            link(nc.vector.tensor_tensor(g.h[:, :, :], agg[:, :, 0:C], wide(self_e[:, :], C), ALU.mult))
            link(nc.vector.tensor_tensor(g.h[:, :, :], g.h[:, :, :], g.b_gat[l].unsqueeze(1).to_broadcast([P, NB, C]),
                                         ALU.add))
            if l == 0:
                link(nc.vector.tensor_scalar(g.h[:, :, :], g.h[:, :, :], 0.0, None, ALU.max))



class Held:
    pass


NVEC = 2 * 3 + 8 + 1
(V_SEMW, V_LNG, V_LNB, V_AGGB, V_MSGB, V_UPDB, V_GATB, V_ASRC, V_ADST) = (0, 2, 4, 6, 7, 8, 9, 11, 13)


def build(nc, d, out, stop=None):
    g = Held()
    ctx = ExitStack()
    with ctx:
        def sb(name, shape, dt=F32):
            return ctx.enter_context(nc.sbuf_tensor(name, shape, dt))

        g.x = sb("x", [P, NB, C])
        g.h = sb("h", [P, NB, C])
        g.own = sb("own", [P, NB, C])
        g.meta = sb("meta", [P, CP, META])
        g.blk_dst = sb("blk_dst", [1, 1 + NPK], I32)
        g.col_dst = sb("col_dst", [1, 1 + NPK], I32)
        g.blk_src = sb("blk_src", [1, 1 + NPK], I32)
        g.ident = sb("ident", [P, P])
        g.iota = sb("iota", [P, P])
        g.before = sb("before", [P, P])
        g.no_node = sb("no_node", [P, 1])
        g.ident_b = sb("ident_b", [P, P], BF16)
        g.zeros = sb("zeros", [P, BANK])
        g.ones = sb("ones", [P, P])
        g.pair_slot = sb("pair_slot", [NB, CP // PAIR])
        g.w_rel_t = sb("w_rel_t", [C, 2, R * (TW + C) + C])
        g.w_cat_t = sb("w_cat_t", [P, 4, P])
        g.vec = sb("vec", [P, NVEC, C])
        g.sem_b = sb("sem_b", [P, 2])
        g.w_agg = sb("w_agg", [C, C])
        g.w_msg_edge = sb("w_msg_edge", [C, C])
        g.w_msg_node = sb("w_msg_node", [C, C])
        g.w_upd = sb("w_upd", [2 * C, C])
        g.w_gat_t = sb("w_gat_t", [C, 2, C])
        g.w_rel = [g.w_rel_t[:, l, :] for l in range(2)]
        g.w_cat = [[g.w_cat_t[:, 2 * l + j, :] for j in range(2)] for l in range(2)]
        g.w_gat = [g.w_gat_t[:, l, :] for l in range(2)]
        vec = lambda i: g.vec[:, i, :]
        g.sem_w = [vec(V_SEMW + l) for l in range(2)]
        g.ln_g = [vec(V_LNG + l) for l in range(2)]
        g.ln_b = [vec(V_LNB + l) for l in range(2)]
        g.b_agg, g.b_msg, g.b_upd = vec(V_AGGB), vec(V_MSGB), vec(V_UPDB)
        g.b_gat = [vec(V_GATB + l) for l in range(2)]
        g.a_src = [vec(V_ASRC + l) for l in range(2)]
        g.a_dst = [vec(V_ADST + l) for l in range(2)]
        dram = lambda name, shape: nc.dram_tensor(name, shape, F32).ap()
        g.slots = dram("slots", [ROWS, ROWW])
        g.sslots = dram("sslots", [ROWS, SROWW])
        g.rel_table = dram("rel_table", [R * NPAD, TW])
        g.msg_table = dram("msg_table", [NPAD, C])
        g.gat_table = dram("gat_table", [NPAD, GW])
        g.gat_rows = dram("gat_rows", [ROWS, GW])
        g.node_row = dram("node_row", [NB, P])
        g.attr = d["attr"]

        with ExitStack() as routing:
            def tmp(name, shape, dt=F32):
                return routing.enter_context(nc.sbuf_tensor(name, shape, dt))
            g.src_i = tmp("src_i", [P, EC], I32)
            g.dst_i = tmp("dst_i", [P, EC], I32)
            g.typ_i = tmp("typ_i", [P, EC], I32)
            g.weight0 = tmp("weight0", [P, EC])
            g.absent = tmp("absent", [P, EC])
            g.meta0 = tmp("meta0", [P, EC, META])
            g.row0 = tmp("row0", [P, EC], I32)
            g.fill = tmp("fill", [P, TURN, ROWW])
            g.sfill = tmp("sfill", [P, TURN, SROWW])
            load_constants(nc, g, [
                (g.src_i[:, :], d["src"]), (g.dst_i[:, :], d["dst"]), (g.typ_i[:, :], d["typ"]),
                (g.absent[:, :], d["absent"]), (g.weight0[:, :], d["weight"]), (g.iota[:, :], d["iota"]),
                (g.before[:, :], d["before"]), (g.ident[:, :], d["ident"]), (g.pair_slot[:, :], d["pair_slot"]),
                (g.x[:, :, :], d["x"].rearrange("(b p) c -> p b c", p=P)),
                (g.h[:, :, :], d["x"].rearrange("(b p) c -> p b c", p=P)),
                (g.no_node[:, :], d["no_node"]), (g.w_rel_t[:, :, :], d["w_rel"]), (g.w_cat_t[:, :, :], d["w_cat"]),
                (g.vec[:, :, :], d["vectors"]), (g.sem_b[:, :], d["sem_b"]), (g.w_agg[:, :], d["w_agg"]),
                (g.w_msg_edge[:, :], d["w_msg_edge"]), (g.w_msg_node[:, :], d["w_msg_node"]),
                (g.w_upd[:, :], d["w_upd"]), (g.w_gat_t[:, :, :], d["w_gat"])])
            fill_tables(nc, g)
            route(nc, g)
            scatter_edges(nc, g)
        if stop == "scatter":
            return finish(nc, g, out, g.x)
        with ExitStack() as relations:
            def tmp(name, shape, dt=F32):
                return relations.enter_context(nc.sbuf_tensor(name, shape, dt))
            g.mask = tmp("mask", [P, CP, R])
            for l in range(2):
                with nc.sbuf_tensor(f"acc{l}", [P, NB, R * C + R * H], F32) as acc:
                    g.acc = acc
                    with nc.sbuf_tensor(f"q_split{l}", [P, 3, NB, R * C], BF16) as q_split:
                        g.q_split = q_split
                        relation_products(nc, g, l)
                        relation_pass(nc, g, l)
                    relation_nodes(nc, g, l)
                if stop == f"rel{l}":
                    return finish(nc, g, out, g.h)
            residual_norm(nc, g, "res0")
        if stop == "res0":
            return finish(nc, g, out, g.x)
        weighted_layer(nc, g)
        residual_norm(nc, g, "res1")
        if stop == "res1":
            return finish(nc, g, out, g.x)
        message_layer(nc, g)
        residual_norm(nc, g, "res2")
        if stop == "res2":
            return finish(nc, g, out, g.x)
        for l in range(2):
            gat_layer(nc, g, l)
        residual_norm(nc, g, "res3")
        finish(nc, g, out, g.x)


def finish(nc, g, out, what):
    with Stage(nc, "store") as s:
        stored = s.sem("stored")
        block = s.block()

        @block.sync
        def _(sp):
            full = (NB - 1) * P
            sp.dma_start(out[0:full, :].rearrange("(b p) c -> p b c", p=P), what[:, 0:NB - 1, :]).then_inc(stored, 16)
            sp.dma_start(out[full:N, :], what[0:LAST, NB - 1, :]).then_inc(stored, 16)
            sp.wait_ge(stored, 32)


STOP = None


def kernel(**inputs):
    import numpy as np
    from concourse import bacc
    from concourse.bass_utils import run_bass_kernel_spmd

    a = {k: np.asarray(v) for k, v in inputs.items()}
    f = np.float32

    def lanes(v):
        o = np.zeros(P * EC, v.dtype)
        o[:E] = v
        return o.reshape(P, EC)

    attr = np.zeros((P * EC, C), f)
    attr[:E] = a["edge_attr_64"]
    x = np.zeros((NPAD, C), f)
    x[:N] = a["x"]
    w_rel = np.zeros((C, 2, R * (TW + C) + C), f)
    w_cat = np.zeros((P, 4, P), f)
    for l in range(2):
        cols = lambda w, r: a[w][l, r].transpose(1, 0, 2).reshape(C, C)
        for r in range(R):
            w_rel[:, l, r * TW:r * TW + C] = cols("L0_gnn_W_K", r)
            w_rel[:, l, r * TW + C:(r + 1) * TW] = cols("L0_gnn_W_V", r)
            w_rel[:, l, R * TW + r * C:R * TW + (r + 1) * C] = cols("L0_gnn_W_Q", r)
            j, k = divmod(r, 2)
            w_cat[k * C:(k + 1) * C, 2 * l + j, k * C:(k + 1) * C] = a["L0_gnn_W_concat"][l, r]
        w_rel[:, l, R * (TW + C):] = a["L0_gnn_W_self"][l]
    vectors = [a["L0_gnn_sem_w"][0], a["L0_gnn_sem_w"][1], a["L0_gnn_ln_g"][0], a["L0_gnn_ln_g"][1],
               a["L0_gnn_ln_b"][0], a["L0_gnn_ln_b"][1], a["L1_gnn_bias"], a["L2_gnn_M_b"], a["L2_gnn_U_b"],
               a["L3_gnn_b1"], a["L3_gnn_b2"], a["L3_gnn_a_src1"], a["L3_gnn_a_src2"], a["L3_gnn_a_dst1"],
               a["L3_gnn_a_dst2"]]
    order = np.arange(P)
    arrays = {
        "x": x, "src": lanes(a["src"]), "dst": lanes(a["dst"]), "typ": lanes(a["edge_type_4"]),
        "weight": lanes(a["edge_weight"]),
        "attr": np.ascontiguousarray(attr.reshape(P, EC, C).transpose(2, 1, 0)).reshape(C, EC * P),
        "absent": (np.arange(P * EC) >= E).astype(f).reshape(P, EC),
        "no_node": np.where(order >= LAST, -BIG, 0.0).astype(f)[:, None],
        "ident": np.eye(P, dtype=f), "iota": np.broadcast_to(order.astype(f), (P, P)).copy(),
        "before": (order[:, None] < order[None, :]).astype(f),
        "pair_slot": np.broadcast_to(np.arange(CP // PAIR, dtype=f) * (PAIR * P), (NB, CP // PAIR)).copy(),
        "w_rel": w_rel, "w_cat": w_cat,
        "vectors": np.ascontiguousarray(np.broadcast_to(np.stack(vectors), (P, NVEC, C))),
        "sem_b": np.ascontiguousarray(np.broadcast_to(a["L0_gnn_sem_b"], (P, 2))),
        "w_agg": a["L1_gnn_weight"],
        "w_msg_node": np.ascontiguousarray(a["L2_gnn_M_W"][:, :C].T),
        "w_msg_edge": np.ascontiguousarray(a["L2_gnn_M_W"][:, C:].T),
        "w_upd": np.ascontiguousarray(a["L2_gnn_U_W"].T),
        "w_gat": np.ascontiguousarray(np.stack([a["L3_gnn_W1"], a["L3_gnn_W2"]], axis=1)),
    }
    nc = bacc.Bacc("TRN2", target_bir_lowering=False, num_devices=1)
    d = {k: nc.dram_tensor(f"in_{k}", v.shape, mybir.dt.from_np(v.dtype), kind="ExternalInput").ap()
         for k, v in arrays.items()}
    out = nc.dram_tensor("out_x", (N, C), F32, kind="ExternalOutput").ap()
    build(nc, d, out, STOP)
    r = run_bass_kernel_spmd(nc, [{f"in_{k}": v for k, v in arrays.items()}], core_ids=[0])
    return r.results[0]["out_x"]
```
